# Optimizing a Trainium2 kernel written in Bass

```python
import numpy as np
import jax
import jax.numpy as jnp

def _softmax(x, axis=-1):
    return jax.nn.softmax(x, axis=axis)

def _gelu(x):
    return jax.nn.gelu(x, approximate=True)

def _silu(x):
    return jax.nn.silu(x)

def _sigmoid(x):
    return jax.nn.sigmoid(x)

def _layernorm(x, axis=-1, eps=1e-05):
    m = jnp.mean(x, axis=axis, keepdims=True)
    v = jnp.var(x, axis=axis, keepdims=True)
    return (x - m) / jnp.sqrt(v + eps)

def _scatter_add(tgt, idx, src, axis=0):
    return tgt.at[idx].add(src)

def _segment_sum(src, seg, n):
    return jax.ops.segment_sum(src, seg, n)
kernel_name = 'mk_adaln_d2_jaxref_r8_19e8a1'

def setup_inputs(seed: int=0):
    np.random.seed(seed)
    _w = jnp.asarray

    def _L0_attn_setup():
        import jax, jax.numpy as jnp
        import numpy as np
        NL, H, N, B, L = (4, 128, 32, 8, 128)

        def _layernorm_channels(z, w, b):
            mu = jnp.mean(z, axis=1, keepdims=True)
            var = jnp.mean((z - mu) ** 2, axis=1, keepdims=True)
            zn = (z - mu) * jax.lax.rsqrt(var + 1e-05)
            return zn * w[None, :, None] + b[None, :, None]

        def _s4d_layer(z, log_dt, A_re_log, A_im, C_re, C_im, D_skip, W, bvec):
            Bz, Hh, Lz = z.shape
            dt = jnp.exp(log_dt)
            A = -jnp.exp(A_re_log) + 1j * A_im
            dtA = A * dt[:, None]
            C = (C_re + 1j * C_im) * (jnp.expm1(dtA) / A)
            l = jnp.arange(Lz, dtype=jnp.float32)
            K = 2.0 * jnp.einsum('hn,hnl->hl', C, jnp.exp(dtA[:, :, None] * l)).real
            kf = jnp.fft.rfft(K, n=2 * Lz)
            uf = jnp.fft.rfft(z, n=2 * Lz)
            y = jnp.fft.irfft(uf * kf, n=2 * Lz)[..., :Lz]
            y = y + z * D_skip[:, None]
            y = jax.nn.gelu(y)
            out = jnp.einsum('oh,bhl->bol', W, y) + bvec[None, :, None]
            return out[:, :Hh] * jax.nn.sigmoid(out[:, Hh:])
        key = jax.random.key(seed)
        ks = jax.random.split(key, 10)
        x = jax.random.normal(ks[0], (B, L, H), dtype=jnp.float32)
        ln_w = jnp.ones((NL, H), jnp.float32)
        ln_b = jnp.zeros((NL, H), jnp.float32)
        log_dt = (jax.random.uniform(ks[1], (NL, H)) * (np.log(0.1) - np.log(0.001)) + np.log(0.001)).astype(jnp.float32)
        A_re_log = jnp.full((NL, H, N), np.log(0.5), jnp.float32)
        A_im = jnp.broadcast_to(np.pi * jnp.arange(N, dtype=jnp.float32), (NL, H, N))
        C_re = jax.random.normal(ks[2], (NL, H, N), jnp.float32) * 0.5 ** 0.5
        C_im = jax.random.normal(ks[3], (NL, H, N), jnp.float32) * 0.5 ** 0.5
        D_skip = jax.random.normal(ks[4], (NL, H), jnp.float32)
        W_out = jax.random.normal(ks[5], (NL, 2 * H, H), jnp.float32) * (1.0 / np.sqrt(H))
        b_out = jnp.zeros((NL, 2 * H), jnp.float32)
        return {'x': x, 'ln_w': ln_w, 'ln_b': ln_b, 'log_dt': log_dt, 'A_re_log': A_re_log, 'A_im': A_im, 'C_re': C_re, 'C_im': C_im, 'D_skip': D_skip, 'W_out': W_out, 'b_out': b_out}
    _L0_attn_in = _L0_attn_setup()

    def _L0_ffn_setup():
        import jax, jax.numpy as jnp
        import numpy as np
        K = 3
        TAU = 1.0
        EPS = 1e-08

        def _route_dense(z, k, tau):
            topi = jax.lax.top_k(z, k)[1]
            topv = jnp.take_along_axis(z, topi, axis=1)
            w = jax.nn.softmax(topv / (tau + EPS), axis=1)
            N, L = z.shape
            dw = jnp.zeros((N, L), z.dtype)
            dw = dw.at[jnp.arange(N)[:, None], topi].add(w)
            return dw

        def _apply_mixture(x, dw, W):
            y = jnp.zeros((x.shape[0], W.shape[1]), x.dtype)
            for e in range(W.shape[0]):
                y = y + x @ W[e].T * dw[:, e:e + 1]
            return y
        key = jax.random.key(seed)
        ks = jax.random.split(key, 8)
        B, T, D_in, H, D_out, L, d_addr = (4, 256, 128, 512, 128, 12, 64)

        def unitize(U):
            U = U - U.mean(axis=1, keepdims=True)
            return U / (jnp.linalg.norm(U, axis=1, keepdims=True) + EPS)
        x = jax.random.normal(ks[0], (B, T, D_in), jnp.float32)
        P_w = jax.random.normal(ks[1], (d_addr, D_in), jnp.float32) / np.sqrt(D_in)
        U1 = unitize(jax.random.normal(ks[2], (L, d_addr), jnp.float32))
        U2 = unitize(jax.random.normal(ks[3], (L, d_addr), jnp.float32))
        U3 = unitize(jax.random.normal(ks[4], (L, d_addr), jnp.float32))
        W1 = jax.random.normal(ks[5], (L, H, D_in), jnp.float32)
        W1 = W1 / jnp.linalg.norm(W1.reshape(L, -1), axis=1)[:, None, None]
        W2 = jax.random.normal(ks[6], (L, D_out, H), jnp.float32)
        W2 = W2 / jnp.linalg.norm(W2.reshape(L, -1), axis=1)[:, None, None]
        b2 = jax.random.normal(ks[7], (L, D_out), jnp.float32)
        b2 = b2 / jnp.linalg.norm(b2, axis=1, keepdims=True)
        return {'x': x, 'P_w': P_w, 'U1': U1, 'U2': U2, 'U3': U3, 'W1': W1, 'W2': W2, 'b2': b2}
    _L0_ffn_in = _L0_ffn_setup()
    _L0_c = _w((lambda *s: np.random.randn(*s).astype(np.float32) * 0.05)(1, 128))
    _L0_wmod = _w((lambda *s: np.random.randn(*s).astype(np.float32) * 0.05)(128, 6 * 128) * 128 ** (-0.5))

    def _L1_attn_setup():
        import jax, jax.numpy as jnp
        import numpy as np
        from jax import lax
        B, L, D, H = (4, 256, 128, 16)
        DK = D // H
        DV = D // H
        SCALE = DK ** (-0.5)

        def _gla_forward(hidden_states, Wq, Wf, Wi, Wo):
            b, l, d = hidden_states.shape
            q_logits = hidden_states @ Wq
            f_logits = hidden_states @ Wf
            v = hidden_states @ Wi
            q = jax.nn.softmax(q_logits, axis=-1)
            k = 1.0 - jax.nn.softmax(f_logits, axis=-1)
            g = jax.nn.log_softmax(f_logits, axis=-1)

            def split_heads(x, hd):
                return x.reshape(b, l, H, hd).transpose(1, 0, 2, 3)
            q_t = split_heads(q, DK)
            k_t = split_heads(k, DK)
            g_t = split_heads(g, DK)
            v_t = split_heads(v, DV)

            def step(S, inp):
                qt, kt, vt, gt = inp
                S = S * jnp.exp(gt)[..., None] + kt[..., None] * vt[..., None, :]
                ot = jnp.einsum('bhk,bhkv->bhv', qt * SCALE, S)
                return (S, ot)
            S0 = jnp.zeros((b, H, DK, DV), hidden_states.dtype)
            _, o = lax.scan(step, S0, (q_t, k_t, v_t, g_t))
            o = o.transpose(1, 0, 2, 3).reshape(b, l, d)
            return o @ Wo
        key = jax.random.key(seed)
        ks = jax.random.split(key, 5)
        std = 0.02
        return {'hidden_states': jax.random.normal(ks[0], (B, L, D), jnp.float32), 'Wq': jax.random.normal(ks[1], (D, D), jnp.float32) * std, 'Wf': jax.random.normal(ks[2], (D, D), jnp.float32) * std, 'Wi': jax.random.normal(ks[3], (D, D), jnp.float32) * std, 'Wo': jax.random.normal(ks[4], (D, D), jnp.float32) * std}
    _L1_attn_in = _L1_attn_setup()

    def _L1_ffn_setup():
        import jax, jax.numpy as jnp
        import numpy as np
        DIM = 128
        DEPTH = 2
        HEADS = 8
        DIM_HEAD = 64
        WINDOW = 64
        INNER = HEADS * DIM_HEAD
        HID = int(DIM * 4 * 2 / 3)
        B, N = (2, 1024)
        QK_SCALE = 8.0

        def shift_token(t):
            t1, t2 = jnp.split(t, 2, axis=-1)
            t2 = jnp.pad(t2, ((0, 0), (1, 0), (0, 0)))[:, :-1]
            return jnp.concatenate([t1, t2], axis=-1)

        def l2norm(t):
            return t / jnp.clip(jnp.linalg.norm(t, axis=-1, keepdims=True), 1e-12)

        def rotate_half(x):
            x1, x2 = jnp.split(x, 2, axis=-1)
            return jnp.concatenate([-x2, x1], axis=-1)

        def rotary_xpos(q, k):
            n = q.shape[-2]
            half_idx = jnp.arange(0, DIM_HEAD, 2, dtype=jnp.float32)
            inv_freq = 1.0 / 10000.0 ** (half_idx / DIM_HEAD)
            t = jnp.arange(n, dtype=jnp.float32)
            freqs = t[:, None] * inv_freq[None, :]
            freqs = jnp.concatenate([freqs, freqs], axis=-1)
            base = (half_idx + 0.4 * DIM_HEAD) / (1.4 * DIM_HEAD)
            power = (t - n // 2) / float(WINDOW // 2)
            scale = base[None, :] ** power[:, None]
            scale = jnp.concatenate([scale, scale], axis=-1)
            cos, sin = (jnp.cos(freqs), jnp.sin(freqs))
            q = q * cos * scale + rotate_half(q) * sin * scale
            k = k * cos / scale + rotate_half(k) * sin / scale
            return (q, k)

        def local_attention(q, k, v):
            b, h, n, d = q.shape
            w = n // WINDOW
            bq = q.reshape(b, h, w, WINDOW, d) * QK_SCALE
            bk = k.reshape(b, h, w, WINDOW, d)
            bv = v.reshape(b, h, w, WINDOW, d)

            def look_around(t):
                p = jnp.pad(t, ((0, 0), (0, 0), (1, 0), (0, 0), (0, 0)))
                return jnp.concatenate([p[:, :, :w], p[:, :, 1:]], axis=3)
            bk, bv = (look_around(bk), look_around(bv))
            bt = jnp.arange(n).reshape(w, WINDOW)
            btp = jnp.pad(bt, ((1, 0), (0, 0)), constant_values=-1)
            btk = jnp.concatenate([btp[:w], btp[1:]], axis=1)
            sim = jnp.einsum('bhwid,bhwjd->bhwij', bq, bk)
            i = bt[:, :, None]
            j = btk[:, None, :]
            mask = (i < j) | (i > j + WINDOW) | (j == -1)
            sim = jnp.where(mask, -jnp.finfo(sim.dtype).max, sim)
            attn = jax.nn.softmax(sim, axis=-1)
            out = jnp.einsum('bhwij,bhwjd->bhwid', attn, bv)
            return out.reshape(b, h, n, d)

        def _layer(x, wqkv, qs, ksc, wo, lg, lb, w1, b1, w2, b2):
            b, n, _ = x.shape
            h = shift_token(x)
            qkv = h @ wqkv
            q, k, v = jnp.split(qkv, 3, axis=-1)
            to_heads = lambda t: t.reshape(b, n, HEADS, DIM_HEAD).transpose(0, 2, 1, 3)
            q, k, v = (to_heads(q), to_heads(k), to_heads(v))
            q = l2norm(q) * qs
            k = l2norm(k) * ksc
            q, k = rotary_xpos(q, k)
            o = local_attention(q, k, v)
            o = o.transpose(0, 2, 1, 3).reshape(b, n, INNER)
            x = x + o @ wo
            h = shift_token(x)
            mu = h.mean(-1, keepdims=True)
            var = h.var(-1, keepdims=True)
            h = (h - mu) / jnp.sqrt(var + 1e-05) * lg + lb
            h = h @ w1 + b1
            a, g = jnp.split(h, 2, axis=-1)
            h = a * jax.nn.gelu(g, approximate=False)
            x = x + h @ w2 + b2
            return x
        key = jax.random.key(seed)
        ks = jax.random.split(key, 6)
        return {'x': jax.random.normal(ks[0], (B, N, DIM), jnp.float32), 'wqkv': jax.random.normal(ks[1], (DEPTH, DIM, 3 * INNER), jnp.float32) * 0.02, 'q_scale': jnp.ones((DEPTH, DIM_HEAD), jnp.float32), 'k_scale': jnp.ones((DEPTH, DIM_HEAD), jnp.float32), 'wo': jax.random.normal(ks[2], (DEPTH, INNER, DIM), jnp.float32) * 0.02, 'ln_g': jnp.ones((DEPTH, DIM), jnp.float32), 'ln_b': jnp.zeros((DEPTH, DIM), jnp.float32), 'w1': jax.random.normal(ks[3], (DEPTH, DIM, 2 * HID), jnp.float32) * 0.02, 'b1': jnp.zeros((DEPTH, 2 * HID), jnp.float32), 'w2': jax.random.normal(ks[4], (DEPTH, HID, DIM), jnp.float32) * 0.02, 'b2': jnp.zeros((DEPTH, DIM), jnp.float32)}
    _L1_ffn_in = _L1_ffn_setup()
    _L1_c = _w((lambda *s: np.random.randn(*s).astype(np.float32) * 0.05)(1, 128))
    _L1_wmod = _w((lambda *s: np.random.randn(*s).astype(np.float32) * 0.05)(128, 6 * 128) * 128 ** (-0.5))
    _d = {'L0_attn_x': _L0_attn_in['x'], 'L0_attn_ln_w': _L0_attn_in['ln_w'], 'L0_attn_ln_b': _L0_attn_in['ln_b'], 'L0_attn_log_dt': _L0_attn_in['log_dt'], 'L0_attn_A_re_log': _L0_attn_in['A_re_log'], 'L0_attn_A_im': _L0_attn_in['A_im'], 'L0_attn_C_re': _L0_attn_in['C_re'], 'L0_attn_C_im': _L0_attn_in['C_im'], 'L0_attn_D_skip': _L0_attn_in['D_skip'], 'L0_attn_W_out': _L0_attn_in['W_out'], 'L0_attn_b_out': _L0_attn_in['b_out'], 'L0_ffn_P_w': _L0_ffn_in['P_w'], 'L0_ffn_U1': _L0_ffn_in['U1'], 'L0_ffn_U2': _L0_ffn_in['U2'], 'L0_ffn_U3': _L0_ffn_in['U3'], 'L0_ffn_W1': _L0_ffn_in['W1'], 'L0_ffn_W2': _L0_ffn_in['W2'], 'L0_ffn_b2': _L0_ffn_in['b2'], 'L0_c': _L0_c, 'L0_wmod': _L0_wmod, 'L1_attn_Wq': _L1_attn_in['Wq'], 'L1_attn_Wf': _L1_attn_in['Wf'], 'L1_attn_Wi': _L1_attn_in['Wi'], 'L1_attn_Wo': _L1_attn_in['Wo'], 'L1_ffn_wqkv': _L1_ffn_in['wqkv'], 'L1_ffn_q_scale': _L1_ffn_in['q_scale'], 'L1_ffn_k_scale': _L1_ffn_in['k_scale'], 'L1_ffn_wo': _L1_ffn_in['wo'], 'L1_ffn_ln_g': _L1_ffn_in['ln_g'], 'L1_ffn_ln_b': _L1_ffn_in['ln_b'], 'L1_ffn_w1': _L1_ffn_in['w1'], 'L1_ffn_b1': _L1_ffn_in['b1'], 'L1_ffn_w2': _L1_ffn_in['w2'], 'L1_ffn_b2': _L1_ffn_in['b2'], 'L1_c': _L1_c, 'L1_wmod': _L1_wmod}
    _x0 = _d['L0_attn_x']
    _d['L0_attn_x'] = jax.random.normal(jax.random.fold_in(jax.random.key(seed), 1), (1, 2048, 128), dtype=_x0.dtype)
    del _x0
    return _d

def reference(L0_attn_x, L0_attn_ln_w, L0_attn_ln_b, L0_attn_log_dt, L0_attn_A_re_log, L0_attn_A_im, L0_attn_C_re, L0_attn_C_im, L0_attn_D_skip, L0_attn_W_out, L0_attn_b_out, L0_ffn_P_w, L0_ffn_U1, L0_ffn_U2, L0_ffn_U3, L0_ffn_W1, L0_ffn_W2, L0_ffn_b2, L0_c, L0_wmod, L1_attn_Wq, L1_attn_Wf, L1_attn_Wi, L1_attn_Wo, L1_ffn_wqkv, L1_ffn_q_scale, L1_ffn_k_scale, L1_ffn_wo, L1_ffn_ln_g, L1_ffn_ln_b, L1_ffn_w1, L1_ffn_b1, L1_ffn_w2, L1_ffn_b2, L1_c, L1_wmod):

    def _L0_attn_ref(x, ln_w, ln_b, log_dt, A_re_log, A_im, C_re, C_im, D_skip, W_out, b_out):
        import jax, jax.numpy as jnp
        import numpy as np
        NL, H, N, B, L = (4, 128, 32, 8, 128)

        def _layernorm_channels(z, w, b):
            mu = jnp.mean(z, axis=1, keepdims=True)
            var = jnp.mean((z - mu) ** 2, axis=1, keepdims=True)
            zn = (z - mu) * jax.lax.rsqrt(var + 1e-05)
            return zn * w[None, :, None] + b[None, :, None]

        def _s4d_layer(z, log_dt, A_re_log, A_im, C_re, C_im, D_skip, W, bvec):
            Bz, Hh, Lz = z.shape
            dt = jnp.exp(log_dt)
            A = -jnp.exp(A_re_log) + 1j * A_im
            dtA = A * dt[:, None]
            C = (C_re + 1j * C_im) * (jnp.expm1(dtA) / A)
            l = jnp.arange(Lz, dtype=jnp.float32)
            K = 2.0 * jnp.einsum('hn,hnl->hl', C, jnp.exp(dtA[:, :, None] * l)).real
            kf = jnp.fft.rfft(K, n=2 * Lz)
            uf = jnp.fft.rfft(z, n=2 * Lz)
            y = jnp.fft.irfft(uf * kf, n=2 * Lz)[..., :Lz]
            y = y + z * D_skip[:, None]
            y = jax.nn.gelu(y)
            out = jnp.einsum('oh,bhl->bol', W, y) + bvec[None, :, None]
            return out[:, :Hh] * jax.nn.sigmoid(out[:, Hh:])
        h = jnp.transpose(x, (0, 2, 1))
        for i in range(NL):
            z = _layernorm_channels(h, ln_w[i], ln_b[i])
            z = _s4d_layer(z, log_dt[i], A_re_log[i], A_im[i], C_re[i], C_im[i], D_skip[i], W_out[i], b_out[i])
            h = z + h
        return jnp.transpose(h, (0, 2, 1))

    def _L0_ffn_ref(x, P_w, U1, U2, U3, W1, W2, b2):
        import jax, jax.numpy as jnp
        import numpy as np
        K = 3
        TAU = 1.0
        EPS = 1e-08

        def _route_dense(z, k, tau):
            topi = jax.lax.top_k(z, k)[1]
            topv = jnp.take_along_axis(z, topi, axis=1)
            w = jax.nn.softmax(topv / (tau + EPS), axis=1)
            N, L = z.shape
            dw = jnp.zeros((N, L), z.dtype)
            dw = dw.at[jnp.arange(N)[:, None], topi].add(w)
            return dw

        def _apply_mixture(x, dw, W):
            y = jnp.zeros((x.shape[0], W.shape[1]), x.dtype)
            for e in range(W.shape[0]):
                y = y + x @ W[e].T * dw[:, e:e + 1]
            return y
        B, T, D = x.shape
        x_flat = x.reshape(B * T, D)
        x_addr = x_flat @ P_w.T
        dw1 = _route_dense(x_addr @ U1.T, K, TAU)
        dw2 = _route_dense(x_addr @ U2.T, K, TAU)
        dw3 = _route_dense(x_addr @ U3.T, K, TAU)
        h = _apply_mixture(x_flat, dw1, W1)
        h = jax.nn.gelu(h, approximate=False)
        y = _apply_mixture(h, dw2, W2)
        y = y + dw3 @ b2
        return y.reshape(B, T, -1)

    def _L1_attn_ref(hidden_states, Wq, Wf, Wi, Wo):
        import jax, jax.numpy as jnp
        import numpy as np
        from jax import lax
        B, L, D, H = (4, 256, 128, 16)
        DK = D // H
        DV = D // H
        SCALE = DK ** (-0.5)

        def _gla_forward(hidden_states, Wq, Wf, Wi, Wo):
            b, l, d = hidden_states.shape
            q_logits = hidden_states @ Wq
            f_logits = hidden_states @ Wf
            v = hidden_states @ Wi
            q = jax.nn.softmax(q_logits, axis=-1)
            k = 1.0 - jax.nn.softmax(f_logits, axis=-1)
            g = jax.nn.log_softmax(f_logits, axis=-1)

            def split_heads(x, hd):
                return x.reshape(b, l, H, hd).transpose(1, 0, 2, 3)
            q_t = split_heads(q, DK)
            k_t = split_heads(k, DK)
            g_t = split_heads(g, DK)
            v_t = split_heads(v, DV)

            def step(S, inp):
                qt, kt, vt, gt = inp
                S = S * jnp.exp(gt)[..., None] + kt[..., None] * vt[..., None, :]
                ot = jnp.einsum('bhk,bhkv->bhv', qt * SCALE, S)
                return (S, ot)
            S0 = jnp.zeros((b, H, DK, DV), hidden_states.dtype)
            _, o = lax.scan(step, S0, (q_t, k_t, v_t, g_t))
            o = o.transpose(1, 0, 2, 3).reshape(b, l, d)
            return o @ Wo
        return _gla_forward(hidden_states, Wq, Wf, Wi, Wo)

    def _L1_ffn_ref(x, wqkv, q_scale, k_scale, wo, ln_g, ln_b, w1, b1, w2, b2):
        import jax, jax.numpy as jnp
        import numpy as np
        DIM = 128
        DEPTH = 2
        HEADS = 8
        DIM_HEAD = 64
        WINDOW = 64
        INNER = HEADS * DIM_HEAD
        HID = int(DIM * 4 * 2 / 3)
        B, N = (2, 1024)
        QK_SCALE = 8.0

        def shift_token(t):
            t1, t2 = jnp.split(t, 2, axis=-1)
            t2 = jnp.pad(t2, ((0, 0), (1, 0), (0, 0)))[:, :-1]
            return jnp.concatenate([t1, t2], axis=-1)

        def l2norm(t):
            return t / jnp.clip(jnp.linalg.norm(t, axis=-1, keepdims=True), 1e-12)

        def rotate_half(x):
            x1, x2 = jnp.split(x, 2, axis=-1)
            return jnp.concatenate([-x2, x1], axis=-1)

        def rotary_xpos(q, k):
            n = q.shape[-2]
            half_idx = jnp.arange(0, DIM_HEAD, 2, dtype=jnp.float32)
            inv_freq = 1.0 / 10000.0 ** (half_idx / DIM_HEAD)
            t = jnp.arange(n, dtype=jnp.float32)
            freqs = t[:, None] * inv_freq[None, :]
            freqs = jnp.concatenate([freqs, freqs], axis=-1)
            base = (half_idx + 0.4 * DIM_HEAD) / (1.4 * DIM_HEAD)
            power = (t - n // 2) / float(WINDOW // 2)
            scale = base[None, :] ** power[:, None]
            scale = jnp.concatenate([scale, scale], axis=-1)
            cos, sin = (jnp.cos(freqs), jnp.sin(freqs))
            q = q * cos * scale + rotate_half(q) * sin * scale
            k = k * cos / scale + rotate_half(k) * sin / scale
            return (q, k)

        def local_attention(q, k, v):
            b, h, n, d = q.shape
            w = n // WINDOW
            bq = q.reshape(b, h, w, WINDOW, d) * QK_SCALE
            bk = k.reshape(b, h, w, WINDOW, d)
            bv = v.reshape(b, h, w, WINDOW, d)

            def look_around(t):
                p = jnp.pad(t, ((0, 0), (0, 0), (1, 0), (0, 0), (0, 0)))
                return jnp.concatenate([p[:, :, :w], p[:, :, 1:]], axis=3)
            bk, bv = (look_around(bk), look_around(bv))
            bt = jnp.arange(n).reshape(w, WINDOW)
            btp = jnp.pad(bt, ((1, 0), (0, 0)), constant_values=-1)
            btk = jnp.concatenate([btp[:w], btp[1:]], axis=1)
            sim = jnp.einsum('bhwid,bhwjd->bhwij', bq, bk)
            i = bt[:, :, None]
            j = btk[:, None, :]
            mask = (i < j) | (i > j + WINDOW) | (j == -1)
            sim = jnp.where(mask, -jnp.finfo(sim.dtype).max, sim)
            attn = jax.nn.softmax(sim, axis=-1)
            out = jnp.einsum('bhwij,bhwjd->bhwid', attn, bv)
            return out.reshape(b, h, n, d)

        def _layer(x, wqkv, qs, ksc, wo, lg, lb, w1, b1, w2, b2):
            b, n, _ = x.shape
            h = shift_token(x)
            qkv = h @ wqkv
            q, k, v = jnp.split(qkv, 3, axis=-1)
            to_heads = lambda t: t.reshape(b, n, HEADS, DIM_HEAD).transpose(0, 2, 1, 3)
            q, k, v = (to_heads(q), to_heads(k), to_heads(v))
            q = l2norm(q) * qs
            k = l2norm(k) * ksc
            q, k = rotary_xpos(q, k)
            o = local_attention(q, k, v)
            o = o.transpose(0, 2, 1, 3).reshape(b, n, INNER)
            x = x + o @ wo
            h = shift_token(x)
            mu = h.mean(-1, keepdims=True)
            var = h.var(-1, keepdims=True)
            h = (h - mu) / jnp.sqrt(var + 1e-05) * lg + lb
            h = h @ w1 + b1
            a, g = jnp.split(h, 2, axis=-1)
            h = a * jax.nn.gelu(g, approximate=False)
            x = x + h @ w2 + b2
            return x
        for l in range(DEPTH):
            x = _layer(x, wqkv[l], q_scale[l], k_scale[l], wo[l], ln_g[l], ln_b[l], w1[l], b1[l], w2[l], b2[l])
        return x
    x = L0_attn_x
    mod = (_silu(L0_c) @ L0_wmod).reshape(L0_c.shape[0], 6, 1, -1)
    sa, ca, ga, sb, cb, gb = (mod[:, 0], mod[:, 1], mod[:, 2], mod[:, 3], mod[:, 4], mod[:, 5])
    ga = (2 * (ga >= 0) - 1) * jnp.maximum(jnp.abs(ga), 0.25)
    gb = (2 * (gb >= 0) - 1) * jnp.maximum(jnp.abs(gb), 0.25)
    h = _layernorm(x, axis=-1) * (1 + ca) + sa
    x = x + ga * _L0_attn_ref(h, L0_attn_ln_w, L0_attn_ln_b, L0_attn_log_dt, L0_attn_A_re_log, L0_attn_A_im, L0_attn_C_re, L0_attn_C_im, L0_attn_D_skip, L0_attn_W_out, L0_attn_b_out)
    h = _layernorm(x, axis=-1) * (1 + cb) + sb
    x = x + gb * _L0_ffn_ref(h, L0_ffn_P_w, L0_ffn_U1, L0_ffn_U2, L0_ffn_U3, L0_ffn_W1, L0_ffn_W2, L0_ffn_b2)
    mod = (_silu(L1_c) @ L1_wmod).reshape(L1_c.shape[0], 6, 1, -1)
    sa, ca, ga, sb, cb, gb = (mod[:, 0], mod[:, 1], mod[:, 2], mod[:, 3], mod[:, 4], mod[:, 5])
    ga = (2 * (ga >= 0) - 1) * jnp.maximum(jnp.abs(ga), 0.25)
    gb = (2 * (gb >= 0) - 1) * jnp.maximum(jnp.abs(gb), 0.25)
    h = _layernorm(x, axis=-1) * (1 + ca) + sa
    x = x + ga * _L1_attn_ref(h, L1_attn_Wq, L1_attn_Wf, L1_attn_Wi, L1_attn_Wo)
    h = _layernorm(x, axis=-1) * (1 + cb) + sb
    x = x + gb * _L1_ffn_ref(h, L1_ffn_wqkv, L1_ffn_q_scale, L1_ffn_k_scale, L1_ffn_wo, L1_ffn_ln_g, L1_ffn_ln_b, L1_ffn_w1, L1_ffn_b1, L1_ffn_w2, L1_ffn_b2)
    return x

_drawn_inputs = setup_inputs


def setup_inputs(seed=0):
    import zlib

    import numpy as np

    out = dict(_drawn_inputs(seed))
    spreads = {'L0_attn_ln_w': (1.0, 0.2),
     'L0_attn_ln_b': (0.0, 0.1),
     'L0_attn_A_re_log': (-0.6931471824645996, 0.2),
     'L0_attn_b_out': (0.0, 0.1),
     'L1_ffn_q_scale': (1.0, 0.6),
     'L1_ffn_k_scale': (1.0, 0.6),
     'L1_ffn_ln_g': (1.0, 0.6),
     'L1_ffn_ln_b': (0.0, 0.8),
     'L1_ffn_b1': (0.0, 0.8),
     'L1_ffn_b2': (0.0, 0.8)}
    factors = {'L0_ffn_P_w': 4.88,
     'L0_ffn_U1': 8.0,
     'L0_ffn_U2': 8.0,
     'L0_ffn_U3': 4.929,
     'L0_ffn_W1': 8.0,
     'L0_ffn_W2': 8.0,
     'L0_ffn_b2': 4.517,
     'L1_attn_Wq': 8.0,
     'L1_attn_Wf': 64.0,
     'L1_attn_Wi': 8.0,
     'L1_attn_Wo': 8.0,
     'L1_ffn_wqkv': 6.625,
     'L1_ffn_wo': 6.312,
     'L1_ffn_w1': 8.0,
     'L1_ffn_w2': 8.0}
    for name, (base, spread) in spreads.items():
        noise = np.random.default_rng([zlib.crc32(name.encode()), seed]).standard_normal(out[name].shape)
        drawn = base * np.exp(spread * noise) if base else spread * noise
        out[name] = jnp.asarray(drawn.astype(out[name].dtype))
    for name, factor in factors.items():
        out[name] = (out[name] * factor).astype(out[name].dtype)
    return out
```

```python
import math
from contextlib import ExitStack

import numpy as np

import concourse.bass as bass
from concourse import mybir

STAGE = "full"

F32 = mybir.dt.float32
ALU = mybir.AluOpType
ACT = mybir.ActivationFunctionType
AX = mybir.AxisListType

P = 128
N_TOK = 2048
TILES = N_TOK // P
BLOCKS = N_TOK // 512
EPS_LN = 1e-5

S4_LAYERS = 4
MODES = 32
GROUPS = P // MODES
HG = P // GROUPS
CHUNK = 64
CHUNKS = N_TOK // CHUNK
LOW = 16
HIGH = CHUNK // LOW
NEAR = LOW + HIGH
ONE = LOW - 2
N_EXP = NEAR + CHUNKS
MAGIC = 1.5 * 2.0 ** 23
TWO_PI_1 = 6.28125
TWO_PI_2 = float(np.float32(np.round((2 * math.pi - TWO_PI_1) * 2 ** 21) / 2 ** 21))
TWO_PI_3 = 2 * math.pi - TWO_PI_1 - TWO_PI_2
PIECES = 4
PIECE = HG // PIECES

EXPERTS, TOP, HIDDEN, ADDR = 12, 3, 512, 64
ROUTERS = 3
HID_CHUNKS = HIDDEN // P

LIN_HEADS, LIN_DIM = 16, 8

DEPTH, HEADS, HEAD_DIM, WINDOW = 2, 8, 64, 64
FF = int(P * 4 * 2 / 3)
FF_CHUNKS = [(0, P), (P, P), (2 * P, FF - 2 * P)]
KEYS = WINDOW + P
QK_SCALE = 8.0
MASKED = -1e30


def rotary_tables():
    half = np.arange(0, HEAD_DIM, 2, dtype=np.float32)
    inv = (1.0 / 10000.0 ** (half / HEAD_DIM)).astype(np.float32)
    t = np.arange(N_TOK, dtype=np.float32)
    freqs = (t[:, None] * inv[None, :]).astype(np.float32).astype(np.float64)
    base = (half.astype(np.float64) + 0.4 * HEAD_DIM) / (1.4 * HEAD_DIM)
    power = (t.astype(np.float64) - N_TOK // 2) / float(WINDOW // 2)
    scale = base[None, :] ** power[:, None]
    cos, sin = np.cos(freqs), np.sin(freqs)
    two = lambda a, b: np.concatenate([a, b], axis=1).astype(np.float32)
    return np.stack([two(cos * scale, cos * scale), two(-sin * scale, sin * scale),
                     two(cos / scale, cos / scale), two(-sin / scale, sin / scale)])


def window_mask():
    i = np.arange(P)[:, None] + WINDOW
    j = np.arange(KEYS)[None, :]
    return np.where((i < j) | (i > j + WINDOW), MASKED, 0.0).astype(np.float32)


def exponents():
    e = [LOW - 1 - b for b in range(LOW)] + [LOW * (HIGH - 1 - a) for a in range(HIGH)] + [CHUNK * c for c in range(CHUNKS)]
    return np.array(e, np.float32)


class Chain:

    def __init__(self, engine, semaphore):
        self.engine, self.semaphore = engine, semaphore
        self.n = self.base = self.seen = 0

    def mark(self, instruction):
        instruction.then_inc(self.semaphore, 1)
        self.seen += 1
        self.n = self.base + self.seen

    def wait(self):
        self.engine.wait_ge(self.semaphore, self.n)

    def link(self, instruction):
        self.mark(instruction)
        self.wait()

    def body(self, step, per_step):
        self.start, self.per_step = self.n, per_step
        self.base, self.seen = step * per_step + self.start, 0
        self.n = self.base

    def leave(self, steps):
        assert self.seen == self.per_step, (self.seen, self.per_step)
        self.n = self.base = self.start + steps * self.per_step
        self.seen = 0


def program(nc, dram, out, stage):
    ctx = ExitStack()
    with ctx:
        sems = {}

        def sem(name):
            if name not in sems:
                sems[name] = ctx.enter_context(nc.semaphore(name))
            return sems[name]

        ARENA = 53000
        arena = ctx.enter_context(nc.sbuf_tensor("arena", [P, ARENA], F32))
        bank = [ctx.enter_context(nc.psum_tensor(f"bank{i}", [P, 512], F32)) for i in range(8)]

        def carve(at, *dims, parts=P):
            n = int(np.prod(dims))
            assert at + n <= ARENA, (at, dims)
            v = arena[0:parts, at:at + n]
            if len(dims) == 2:
                v = v.rearrange("p (a b) -> p a b", a=dims[0])
            if len(dims) == 3:
                v = v.rearrange("p (a b c) -> p a b c", a=dims[0], b=dims[1])
            return v

        top = [0]

        def keep(*dims, parts=P):
            at = top[0]
            top[0] += int(np.prod(dims))
            return carve(at, *dims, parts=parts)

        xT = keep(N_TOK)
        hT = keep(N_TOK)
        ident = keep(P)
        cond = keep(2)
        cond_sig = keep(2)
        cond_silu = keep(2)
        mod = keep(12)
        one_plus = keep(12)
        mod_sign = keep(12)
        mod_abs = keep(12)
        gate = keep(12)
        neg_half = keep(TILES)
        stats = keep(TILES, 6)
        mean_var = keep(TILES, 2)
        rstd = keep(TILES)
        var_eps = keep(TILES)
        eps_col = keep(TILES)
        turn_mark = keep(3)
        pool_mark = keep(1)
        phase_base = top[0]

        zu = keep(P, CHUNKS)
        tp = keep(P, CHUNK)
        wmod_sb = tp.rearrange("p a b -> p (a b)")[:, 0:2 * 768].rearrange("p (a b) -> p a b", a=2)
        back = keep(HG, 2, P, parts=CHUNK)
        pow_re = keep(HG, CHUNK)
        pow_im = keep(HG, CHUNK)
        k_re = keep(HG, CHUNK)
        k_im = keep(HG, CHUNK)
        b_re, b_im = (k_re.rearrange("p a b -> p (a b)")[:, i * HG * CHUNKS:(i + 1) * HG * CHUNKS].rearrange("p (h c) -> p h c", c=CHUNKS) for i in (0, 1))
        s_a, s_b = (k_im.rearrange("p a b -> p (a b)")[:, i * HG * CHUNKS:(i + 1) * HG * CHUNKS].rearrange("p (h c) -> p h c", c=CHUNKS) for i in (0, 1))
        z_tok = keep(TILES, P)
        yT = z_tok.rearrange("p a b -> p (a b)")
        states = keep(HG, 2, CHUNKS)
        y_act = states.rearrange("p a b c -> p (a b c)").rearrange("p (i h) -> p i h", h=HG)
        glu_sig = states.rearrange("p a b c -> p (a b c)")
        k_rows = keep(HG, CHUNK, parts=GROUPS)
        prm = keep(5, HG)
        skip = keep(HG, parts=GROUPS)
        ln_wb = keep(2, P)
        w_out = keep(2 * P)
        b_out = keep(2)
        sel = keep(2, GROUPS)
        expo = keep(N_EXP)
        exps = keep(2, HG)
        dta = keep(2, HG)
        theta = keep(HG, N_EXP)
        turns = keep(HG, N_EXP)
        sn = keep(HG, N_EXP)
        cosn = keep(HG, N_EXP)
        anc_re = keep(HG, NEAR)
        anc_im = keep(HG, NEAR)
        mag = keep(HG, NEAR)
        tanh = keep(HG)
        r_chunk = keep(HG)
        small = [keep(HG) for _ in range(12)]
        g_re = keep(HG, CHUNKS)
        g_im = keep(HG, CHUNKS)
        decay = keep(HG, CHUNKS)
        u_re, u_im = (glu_sig[:, i * HG * CHUNKS:(i + 1) * HG * CHUNKS].rearrange("p (h c) -> p h c", c=CHUNKS) for i in (0, 1))

        top[0] = phase_base
        w1_sb = keep(EXPERTS, HIDDEN)
        w2_sb = keep(EXPERTS, HID_CHUNKS, P)
        share1 = keep(EXPERTS, 512)
        share2 = keep(EXPERTS, 512)
        x_exp = keep(EXPERTS, 512)
        moe_norm = keep(TILES, P)
        addr = keep(N_TOK, parts=ADDR)
        logit = keep(TILES, ROUTERS * EXPERTS)
        weight = keep(TILES, ROUTERS * EXPERTS)
        above = keep(TILES, ROUTERS * EXPERTS)
        equal = keep(TILES, ROUTERS * EXPERTS)
        ranks = keep(TILES, ROUTERS * EXPERTS)
        fresh = keep(TILES, ROUTERS * EXPERTS)
        top8 = keep(TILES * ROUTERS, 8)
        room = keep(TILES * ROUTERS)
        total = keep(TILES * ROUTERS)
        weightT = keep(N_TOK, parts=ROUTERS * EXPERTS)
        pw_sb = keep(ADDR)
        u_sb = keep(ROUTERS * EXPERTS, parts=ADDR)
        b2_sb = keep(P, parts=EXPERTS)
        hid = keep(HID_CHUNKS, 512)
        y_acc = keep(512)
        y_part = [keep(512) for _ in range(2)]

        top[0] = phase_base
        gla_norm = keep(TILES, P)
        wqf_sb = keep(2 * P)
        wi_sb = keep(LIN_DIM, P)
        wo8_sb = keep(LIN_DIM, P)
        soft = keep(TILES, 2, P)
        neg_max = keep(TILES, 2)
        soft_sum = keep(TILES, 2)
        qT = keep(N_TOK)
        keepT = keep(N_TOK)
        kT = keep(N_TOK)
        kv = [keep(N_TOK) for _ in range(2)]
        state = [keep(N_TOK) for _ in range(2)]
        read = [keep(N_TOK) for _ in range(2)]

        top[0] = phase_base
        sT = keep(N_TOK)
        nT = sT
        wqkv_sb = keep(3 * HEADS * HEAD_DIM)
        wo_sb = keep(4, P)
        wf1_sb = keep(2 * FF)
        wf2_sb = keep(3, P)
        cols = keep(9)
        qk_rows = keep(4, HEAD_DIM)
        tables = keep(4, TILES, HEAD_DIM)
        scaled = keep(4, TILES, HEAD_DIM)
        mask_sb = keep(KEYS)
        at_rot = top[0]
        q_rot = keep(2, 512)
        k_rot = keep(2, 512)
        probsT = carve(at_rot, 2 * HEADS, P)
        at_rot = top[0]
        rot_tmp = keep(2, 512)
        squares = keep(2, 512)
        oT = carve(at_rot, 4, 512)
        norms = keep(TILES, 2, HEADS)
        inv_norm = keep(TILES, 2, HEADS)
        ff_norm = carve(top[0], TILES, P)
        qhT = keep(4, N_TOK)
        khT = keep(4, N_TOK)
        v_tok = keep(TILES, 512)
        scores = keep(HEADS, KEYS)
        probs = keep(HEADS, 2 * P)
        row_max = keep(HEADS)
        row_scale = keep(HEADS)
        row_bias = keep(HEADS)
        row_sum = keep(HEADS)
        row_inv = keep(HEADS)
        ff_g = squares
        ff_h = scores.rearrange("p a b -> p (a b)")[:, 0:3 * 512].rearrange("p (a b) -> p a b", a=3)
        share_d = nc.dram_tensor("share_d", [ROUTERS * EXPERTS, N_TOK], F32, kind="Internal").ap()
        k_pad = nc.dram_tensor("k_pad", [P, 2 * CHUNK], F32, kind="Internal").ap()

        block = ctx.enter_context(nc.Block())

        LN_A, LN_B, LN_C, LN_D = 0, 1 + S4_LAYERS, 2 + S4_LAYERS, 3 + S4_LAYERS
        LN_S4, LN_FF = 1, 4 + S4_LAYERS

        def going_back(n):
            return n if isinstance(n, int) and n == LN_A else n - S4_LAYERS

        def ln_pe_tokens(pe, src, written=None, base=0):
            for b in range(BLOCKS):
                if written is not None:
                    pe.wait_ge(sem(written), base + b + 1)
                for t in range(4):
                    c = 4 * b + t
                    last = nc.tensor.transpose(bank[b][:, t * P:(t + 1) * P], src[:, c * P:(c + 1) * P], ident)
                last.then_inc(sem("ln_tokens"), 1)

        def ln_pe_back(pe, n, normed):
            for b in range(BLOCKS):
                pe.wait_ge(sem("ln_normed"), going_back(n) * BLOCKS + b + 1)
                for t in range(4):
                    c = 4 * b + t
                    last = nc.tensor.transpose(bank[4 + b][:, t * P:(t + 1) * P], normed[:, c, :], ident)
                last.then_inc(sem("ln_back"), 1)

        def ln_dve_stats(dve, n):
            for b in range(BLOCKS):
                dve.wait_ge(sem("ln_tokens"), n * BLOCKS + b + 1)
                for t in range(4):
                    c = 4 * b + t
                    nc.vector.bn_stats(stats[:, c, :], bank[b][:, t * P:(t + 1) * P]).then_inc(sem("ln_stats"), 1)
            dve.wait_ge(sem("ln_stats"), n * TILES + TILES)
            nc.vector.memset(turn_mark[:, 0:1], 0.0)
            for c in range(TILES):
                nc.vector.bn_aggr(mean_var[:, c, :], stats[:, c, :]).then_inc(sem("ln_aggr"), 1)

        def ln_dve(dve, n, normed):
            ln_dve_stats(dve, n)
            dve.wait_ge(sem("ln_rstd"), n + 1)
            for b in range(BLOCKS):
                for t in range(4):
                    c = 4 * b + t
                    last = nc.vector.tensor_scalar(normed[:, c, :], bank[b][:, t * P:(t + 1) * P],
                                                   mean_var[:, c, 0:1], rstd[:, c:c + 1],
                                                   ALU.subtract, ALU.mult)
                    if t == 3:
                        last.then_inc(sem("ln_normed"), 1)

        def ln_pool(pool, n):
            pool.wait_ge(sem("ln_aggr"), n * TILES + TILES)
            nc.gpsimd.tensor_tensor(var_eps, mean_var[:, :, 1], eps_col, ALU.add).then_inc(sem("ln_eps"), 1)
            pool.wait_ge(sem("ln_eps"), n + 1)
            nc.gpsimd.tensor_tensor(rstd, var_eps, neg_half, ALU.pow).then_inc(sem("ln_rstd"), 1)

        def ln_act(act, n, out_name, dst, scale, bias):
            for b in range(BLOCKS):
                act.wait_ge(sem("ln_back"), going_back(n) * BLOCKS + b + 1)
                nc.scalar.activation(dst[:, 512 * b:512 * b + 512], bank[4 + b][:, :], ACT.Identity,
                                     bias=bias, scale=scale).then_inc(sem(out_name), 1)

        def s4_dve_angles(dve, G):
            V = nc.vector
            dve.wait_ge(sem("s4_exps"), G + 1)
            V.scalar_tensor_tensor(dta[:, 0, :], exps[:, 1, :], -1.0, exps[:, 0, :], ALU.mult, ALU.mult)
            V.tensor_tensor(dta[:, 1, :], prm[:, 2, :], exps[:, 0, :], ALU.mult).then_inc(sem("s4_dta"), 1)
            dve.wait_ge(sem("s4_dta"), G + 1)
            V.tensor_tensor(mag, dta[:, 0, :].unsqueeze(2).to_broadcast([P, HG, NEAR]),
                            expo[:, 0:NEAR].unsqueeze(1).to_broadcast([P, HG, NEAR]), ALU.mult).then_inc(sem("s4_marg"), 1)

        def s4_dve_reduce(dve, chain, G):
            V = nc.vector
            link = chain.link
            wide = [P, HG, N_EXP]
            link(V.tensor_tensor(theta, dta[:, 1, :].unsqueeze(2).to_broadcast(wide),
                                 expo.unsqueeze(1).to_broadcast(wide), ALU.mult))
            link(V.tensor_scalar(turns, theta, 1.0 / (2 * math.pi), MAGIC, ALU.mult, ALU.add))
            link(V.tensor_scalar(turns, turns, MAGIC, None, ALU.subtract))
            for part in (TWO_PI_1, TWO_PI_2, TWO_PI_3):
                link(V.scalar_tensor_tensor(theta, turns, -part, theta, ALU.mult, ALU.add))
            V.tensor_scalar(theta, theta, 3.1415925, -3.1415925, ALU.min, ALU.max).then_inc(sem("s4_theta"), 1)

        def s4_dve_powers(dve, chain, G):
            V = nc.vector
            link = chain.link
            a_im, c_re, c_im = (prm[:, i, :] for i in (2, 3, 4))
            e_are = exps[:, 1, :]
            dve.wait_ge(sem("s4_sin"), G + 1)
            dve.wait_ge(sem("s4_mag"), G * 2 + 2)
            link(V.tensor_tensor(cosn, turns, turns, ALU.mult))
            s0, s1, s2, s3, s4_, s5, s6, s7, cd_re, c2_im, c2_re, cd_im = small
            link(V.tensor_copy(s0, cosn[:, :, ONE]))
            link(V.tensor_scalar(cosn, cosn, -2.0, 1.0, ALU.mult, ALU.add))
            V.tensor_tensor(anc_re, mag, cosn[:, :, 0:NEAR], ALU.mult)
            V.tensor_tensor(anc_im, mag, sn[:, :, 0:NEAR], ALU.mult).then_inc(sem("s4_anchors"), 1)
            dve.wait_ge(sem("s4_anchors"), G + 1)
            link(V.scalar_tensor_tensor(s1, mag[:, :, ONE], 1.0, tanh, ALU.add, ALU.mult))
            link(V.tensor_tensor(s1, s1, cosn[:, :, ONE], ALU.mult))
            link(V.scalar_tensor_tensor(s1, s0, -2.0, s1, ALU.mult, ALU.add))
            e_re, e_im = s1, anc_im[:, :, ONE]
            V.tensor_tensor(s2, e_are, e_are, ALU.mult)
            link(V.tensor_tensor(s3, a_im, a_im, ALU.mult))
            link(V.tensor_tensor(s2, s2, s3, ALU.add))
            link(V.reciprocal(s2, s2))
            V.tensor_tensor(s3, e_im, a_im, ALU.mult)
            V.tensor_tensor(s4_, e_re, e_are, ALU.mult)
            V.tensor_tensor(s5, e_im, e_are, ALU.mult)
            link(V.tensor_tensor(s6, e_re, a_im, ALU.mult))
            V.tensor_tensor(s3, s3, s4_, ALU.subtract)
            link(V.scalar_tensor_tensor(s5, s5, -1.0, s6, ALU.mult, ALU.subtract))
            V.scalar_tensor_tensor(s3, s3, 2.0, s2, ALU.mult, ALU.mult)
            link(V.scalar_tensor_tensor(s5, s5, 2.0, s2, ALU.mult, ALU.mult))
            V.tensor_tensor(s4_, c_re, s3, ALU.mult)
            V.tensor_tensor(s6, c_im, s5, ALU.mult)
            V.tensor_tensor(s7, c_re, s5, ALU.mult)
            link(V.tensor_tensor(s0, c_im, s3, ALU.mult))
            V.tensor_tensor(cd_re, s4_, s6, ALU.subtract).then_inc(sem("s4_cd"), 1)
            link(V.tensor_tensor(cd_im, s7, s0, ALU.add))
            dve.wait_ge(sem("s4_cd"), G + 1)
            w_re, w_im = anc_re[:, :, ONE], anc_im[:, :, ONE]
            V.tensor_tensor(s3, cd_re, w_re, ALU.mult)
            V.tensor_tensor(s4_, cd_im, w_im, ALU.mult)
            V.tensor_tensor(s5, cd_re, w_im, ALU.mult)
            link(V.tensor_tensor(s6, cd_im, w_re, ALU.mult))
            V.tensor_tensor(c2_re, s3, s4_, ALU.subtract)
            V.tensor_tensor(c2_im, s5, s6, ALU.add).then_inc(sem("s4_coef"), 1)
            dve.wait_ge(sem("s4_coef"), G + 1)
            V.tensor_tensor(four(pow_re), hi(anc_re), lo(anc_re), ALU.mult)
            link(V.tensor_tensor(four(k_re), hi(anc_im), lo(anc_im), ALU.mult))
            V.tensor_tensor(pow_re, pow_re, k_re, ALU.subtract).then_inc(sem("s4_pow_re"), 1)
            dve.wait_ge(sem("s4_pow_re"), G + 1)
            V.tensor_tensor(k_re, pow_re, c2_re.unsqueeze(2).to_broadcast([P, HG, CHUNK]), ALU.mult).then_inc(sem("s4_k_re"), 1)
            cc = [P, HG, CHUNKS]
            phi_c, phi_s = cosn[:, :, NEAR:N_EXP], sn[:, :, NEAR:N_EXP]
            c2r, c2i = c2_re.unsqueeze(2).to_broadcast(cc), c2_im.unsqueeze(2).to_broadcast(cc)
            V.tensor_copy(decay[:, :, 1:CHUNKS], r_chunk.unsqueeze(2).to_broadcast([P, HG, CHUNKS - 1]))
            V.tensor_tensor(g_re, phi_c, c2r, ALU.mult)
            V.tensor_tensor(g_im, phi_c, c2i, ALU.mult)
            V.tensor_tensor(g_x, phi_s, c2i, ALU.mult)
            link(V.tensor_tensor(g_y, phi_s, c2r, ALU.mult))
            V.tensor_tensor(g_re, g_re, g_x, ALU.subtract)
            link(V.tensor_tensor(g_im, g_im, g_y, ALU.add))

        def s4_dve_layer(dve, chain, L, more):
            V = nc.vector
            link = chain.link
            if more:
                s4_dve_angles(dve, L + 1)
            ln_dve_stats(dve, LN_S4 + L)
            dve.wait_ge(sem("s4_layer_in"), L * 64 + 64)
            V.memset(turn_mark[:, 1:2], 0.0)
            dve.wait_ge(sem("ln_aggr"), (LN_S4 + L + 1) * TILES)
            for c in range(TILES):
                last = V.scalar_tensor_tensor(z_tok[:, c, :], bank[c // 4][:, (c % 4) * P:(c % 4 + 1) * P], mean_var[:, c, 0:1],
                                              ln_wb[:, 0, :], ALU.subtract, ALU.mult)
            link(last)
            dve.wait_ge(sem("ln_rstd"), LN_S4 + L + 1)
            V.memset(turn_mark[:, 2:3], 0.0)
            for c in range(TILES):
                for half in range(2):
                    r = slice(CHUNK * half, CHUNK * half + CHUNK)
                    last = V.scalar_tensor_tensor(zu[0:CHUNK, :, 2 * c + half], z_tok[r, c, :], rstd[r, c:c + 1],
                                                  ln_wb[r, 1, :], ALU.mult, ALU.add)
            last.then_inc(sem("s4_z"), 1)
            if more:
                s4_dve_reduce(dve, chain, L + 1)
            for k in range(PIECES):
                dve.wait_ge(sem("s4_in_ps"), L * PIECES + k + 1)
                last = V.transpose(glu_sig[:, 512 * k:512 * k + 512], bank[k][:, :])
            link(last)
            phi_c, phi_s = cosn[:, :, NEAR:N_EXP], sn[:, :, NEAR:N_EXP]
            in_re, in_im = states[:, :, 0, :], states[:, :, 1, :]
            V.tensor_tensor(b_re, in_re, phi_c, ALU.mult)
            V.tensor_tensor(s_a, in_im, phi_s, ALU.mult)
            V.tensor_tensor(b_im, in_im, phi_c, ALU.mult)
            link(V.tensor_tensor(s_b, in_re, phi_s, ALU.mult))
            V.tensor_tensor(b_re, b_re, s_a, ALU.add)
            link(V.tensor_tensor(b_im, b_im, s_b, ALU.subtract))
            flat = lambda t: t.rearrange("p h c -> p (h c)")
            V.tensor_tensor_scan(flat(s_a), flat(decay), flat(b_re), 0.0, ALU.mult, ALU.add)
            link(V.tensor_tensor_scan(flat(s_b), flat(decay), flat(b_im), 0.0, ALU.mult, ALU.add))
            c1 = CHUNKS - 1
            sa_, sb_, gr, gi = (t[:, :, 0:c1] for t in (s_a, s_b, g_re, g_im))
            V.tensor_tensor(b_re[:, :, 0:c1], sa_, gr, ALU.mult)
            V.tensor_tensor(b_im[:, :, 0:c1], sb_, gi, ALU.mult)
            V.tensor_tensor(sa_, sa_, gi, ALU.mult)
            link(V.tensor_tensor(sb_, sb_, gr, ALU.mult))
            V.memset(u_re[:, :, 0], 0.0)
            V.memset(u_im[:, :, 0], 0.0)
            V.tensor_tensor(u_re[:, :, 1:CHUNKS], b_re[:, :, 0:c1], b_im[:, :, 0:c1], ALU.subtract)
            V.scalar_tensor_tensor(u_im[:, :, 1:CHUNKS], sa_, -1.0, sb_, ALU.mult, ALU.subtract).then_inc(sem("s4_u"), 1)
            if more:
                dve.wait_ge(sem("s4_pow_moved"), L * 128 + 128)
                s4_dve_powers(dve, chain, L + 1)
            dve.wait_ge(sem("s4_y"), L * PIECES + PIECES)
            V.transpose(yT, glu_sig).then_inc(sem("s4_yT"), 1)
            for b in range(BLOCKS):
                dve.wait_ge(sem("s4_sig"), L * BLOCKS + b + 1)
                sl = slice(512 * b, 512 * b + 512)
                link(V.scalar_tensor_tensor(glu_sig[:, sl], bank[4 + 2 * (b % 2)][:, :], b_out[:, 0:1],
                                            glu_sig[:, sl], ALU.add, ALU.mult))
                V.tensor_tensor(hT[:, sl], hT[:, sl], glu_sig[:, sl], ALU.add).then_inc(sem("s4_h"), 1)

        def s4_pe_layer(pe, L, first):
            T = nc.tensor
            ln_pe_tokens(pe, hT, "lnA_out" if first else "s4_h", 0 if first else (L - 1) * BLOCKS)
            pe.wait_ge(sem("s4_pow_re"), L + 1)
            pe.wait_ge(sem("s4_pow_im"), L + 1)
            pe.sem_inc(sem("pe_turn"), 1)
            for q in range(HG // 2):
                if q >= 4:
                    pe.wait_ge(sem("s4_back"), L * (HG // 2) + q - 3)
                    pe.sem_inc(sem("pe_turn"), 1)
                for i in range(4):
                    last = T.transpose(bank[4 + q % 4][0:CHUNK, i * P:(i + 1) * P], (pow_re, pow_im)[i % 2][:, 2 * q + i // 2, :], ident)
                last.then_inc(sem("s4_back_ps"), 1)
            pe.wait_ge(sem("s4_k_re"), L + 1)
            pe.wait_ge(sem("s4_k_im"), L + 1)
            for k in range(PIECES):
                pe.wait_ge(sem("s4_back"), L * (HG // 2) + HG // 2 - 3 + k)
                T.matmul(bank[4 + k][0:GROUPS, :], sel[:, 0, :], k_re[:, PIECE * k:PIECE * (k + 1), :], start=True, stop=False)
                T.matmul(bank[4 + k][0:GROUPS, :], sel[:, 1, :], k_im[:, PIECE * k:PIECE * (k + 1), :], start=False, stop=True).then_inc(sem("s4_k_ps"), 1)
            pe.wait_ge(sem("s4_k_rows"), L * (PIECES + 1) + 1)
            pe.wait_ge(sem("s4_layer_in"), L * 64 + 64)
            T.matmul(bank[4][0:GROUPS, 0:HG], sel[:, 0, :], small[8], start=True, stop=False)
            T.matmul(bank[4][0:GROUPS, 0:HG], ident[0:GROUPS, 0:GROUPS], skip, start=False, stop=True).then_inc(sem("s4_k_ps"), 1)
            pe.wait_ge(sem("s4_z"), L + 1)
            pe.sem_inc(sem("pe_turn"), 1)
            for k in range(PIECES):
                for hh in range(PIECE * k, PIECE * (k + 1)):
                    for g in range(GROUPS):
                        last = T.matmul(bank[k][32 * g:32 * g + 32, 2 * MODES * (hh % PIECE):2 * MODES * (hh % PIECE + 1)],
                                        zu[0:CHUNK, HG * g + hh, :], back[:, hh, :, 32 * g:32 * g + 32], start=True, stop=True)
                last.then_inc(sem("s4_in_ps"), 1)
            pe.wait_ge(sem("s4_toep_in"), L * 16 * PIECES + 16 * PIECES)
            pe.wait_ge(sem("s4_pow_moved"), L * 128 + 128)
            pe.wait_ge(sem("s4_u_moved"), L * 128 + 128)
            pe.wait_ge(sem("s4_k_rows"), (L + 1) * (PIECES + 1))
            for k in range(PIECES):
                for hh in range(PIECE * k, PIECE * (k + 1)):
                    for g in range(GROUPS):
                        last = T.matmul(bank[4 + k][32 * g:32 * g + 32, CHUNK * (hh % PIECE):CHUNK * (hh % PIECE + 1)],
                                        zu[:, HG * g + hh, :], tp[:, HG * g + hh, :], start=True, stop=True)
                last.then_inc(sem("s4_y_ps"), 1)
            pe.wait_ge(sem("s4_y_ps"), (L + 1) * PIECES)
            pe.sem_inc(sem("s4_tp_free"), 1)
            pe.wait_ge(sem("s4_yT"), L + 1)
            for b in range(BLOCKS):
                if b >= 2:
                    pe.wait_ge(sem("s4_h"), L * BLOCKS + b - 1)
                rhs = yT.rearrange("p (i c) -> p c i", c=CHUNKS)[:, 8 * b:8 * b + 8, :]
                for k in range(2):
                    last = T.matmul(bank[4 + 2 * (b % 2) + k][:, :], w_out[:, k * P:(k + 1) * P], rhs, start=True, stop=True)
                last.then_inc(sem("s4_glu_ps"), 1)

        def s4_act_magnitudes(act, G):
            A = nc.scalar
            act.wait_ge(sem("s4_prm_in"), G * 16 + 16)
            A.activation(exps, prm[:, 0:2, :], ACT.Exp).then_inc(sem("s4_exps"), 1)
            act.wait_ge(sem("s4_dta"), G + 1)
            A.activation(tanh, dta[:, 0, :], ACT.Tanh, scale=0.5)
            A.activation(r_chunk, dta[:, 0, :], ACT.Exp, scale=float(CHUNK)).then_inc(sem("s4_mag"), 1)
            act.wait_ge(sem("s4_marg"), G + 1)
            A.activation(mag, mag, ACT.Exp).then_inc(sem("s4_mag"), 1)

        def s4_act_sines(act, G):
            A = nc.scalar
            act.wait_ge(sem("s4_theta"), G + 1)
            A.activation(sn, theta, ACT.Sin)
            A.activation(turns, theta, ACT.Sin, scale=0.5).then_inc(sem("s4_sin"), 1)

        def s4_act_layer(act, L, more):
            A = nc.scalar
            if more:
                s4_act_magnitudes(act, L + 1)
            for q in range(HG // 2):
                act.wait_ge(sem("s4_back_ps"), L * (HG // 2) + q + 1)
                A.activation(back[:, 2 * q:2 * q + 2], bank[4 + q % 4][0:CHUNK, :].rearrange("p (a b c) -> p a b c", a=2, b=2), ACT.Copy).then_inc(sem("s4_back"), 1)
            for k in range(PIECES):
                act.wait_ge(sem("s4_k_ps"), L * (PIECES + 1) + k + 1)
                src = bank[4 + k][0:GROUPS, :].rearrange("p (a b) -> p a b", a=PIECE)
                A.activation(k_rows[:, PIECE * k:PIECE * (k + 1), 0:CHUNK - 1], src[:, :, 1:CHUNK], ACT.Copy).then_inc(sem("s4_k_rows"), 1)
            act.wait_ge(sem("s4_k_ps"), (L + 1) * (PIECES + 1))
            A.activation(k_rows[:, :, CHUNK - 1], bank[4][0:GROUPS, 0:HG], ACT.Copy).then_inc(sem("s4_k_rows"), 1)
            act.wait_ge(sem("s4_u"), L + 1)
            if more:
                s4_act_sines(act, L + 1)
            for k in range(PIECES):
                act.wait_ge(sem("s4_y_ps"), L * PIECES + k + 1)
                A.activation(y_act.rearrange("p i h -> p h i")[:, PIECE * k:PIECE * (k + 1), :],
                             bank[4 + k][:, :].rearrange("p (h i) -> p h i", i=CHUNK)[:, :, ::-1],
                             ACT.Gelu_apprx_tanh).then_inc(sem("s4_y"), 1)
            act.wait_ge(sem("s4_yT"), L + 1)
            for b in range(BLOCKS):
                act.wait_ge(sem("s4_glu_ps"), L * BLOCKS + b + 1)
                A.activation(glu_sig[:, 512 * b:512 * b + 512], bank[5 + 2 * (b % 2)][:, :],
                             ACT.Sigmoid, bias=b_out[:, 1:2]).then_inc(sem("s4_sig"), 1)

        def s4_pool_powers(pool, chain, G):
            G_ = nc.gpsimd
            pool.wait_ge(sem("s4_anchors"), G + 1)
            G_.tensor_tensor(four(pow_im), hi(anc_re), lo(anc_im), ALU.mult)
            chain.link(G_.tensor_tensor(four(k_im), hi(anc_im), lo(anc_re), ALU.mult))
            G_.tensor_tensor(pow_im, pow_im, k_im, ALU.add).then_inc(sem("s4_pow_im"), 1)
            pool.wait_ge(sem("s4_coef"), G + 1)
            pool.wait_ge(sem("s4_pow_im"), G + 1)
            G_.tensor_tensor(k_im, pow_im, small[9].unsqueeze(2).to_broadcast([P, HG, CHUNK]), ALU.mult).then_inc(sem("s4_k_im"), 1)

        lo = lambda t: t[:, :, 0:LOW].unsqueeze(2).to_broadcast([P, HG, HIGH, LOW])
        hi = lambda t: t[:, :, LOW:NEAR].unsqueeze(3).to_broadcast([P, HG, HIGH, LOW])
        four = lambda t: t.rearrange("p h (a b) -> p h a b", a=HIGH)
        g_x, g_y = (y.rearrange("p a b -> p (a b)")[:, 0:HG * CHUNKS].rearrange("p (h c) -> p h c", c=CHUNKS) for y in (theta, turns))

        def s4_layer_loads(sp, L):
            for dst, name in ((skip, "skip"), (ln_wb, "ln_wb"), (w_out, "w_out"), (b_out, "b_out")):
                sp.dma_start(dst, dram[name][L]).then_inc(sem("s4_layer_in"), 16)

        def s4_sp_layer(sp, L, more):
            whole = (lambda x: x) if isinstance(L, int) else sp.snap
            one, rows, k_out = whole(L + 1), whole((L + 1) * (PIECES + 1)), whole(L * 16 + 16)
            toep_in, h = whole(L * 16 * PIECES), whole(L * BLOCKS + BLOCKS)

            def turn():
                sp.sem_inc(sem("sp_turn"), 1)

            for name in ("s4_tp_free", "s4_pow_re", "s4_pow_im"):
                sp.wait_ge(sem(name), one)
                turn()
            for ri, src in ((0, pow_re), (1, pow_im)):
                for g in range(GROUPS):
                    at = CHUNK + MODES * ri
                    sp.dma_start(tp[at:at + MODES, HG * g:HG * (g + 1), :], src[32 * g:32 * g + 32]).then_inc(sem("s4_pow_moved"), 16)
            if more:
                for name in ("s4_coef",):
                    sp.wait_ge(sem(name), one)
                    turn()
                sp.dma_start(prm, dram["prm"][L + 1]).then_inc(sem("s4_prm_in"), 16)
            sp.wait_ge(sem("s4_k_rows"), rows)
            turn()
            sp.dma_start(k_pad[:, 0:CHUNK].rearrange("(g h) m -> g h m", g=GROUPS), k_rows).then_inc(sem("s4_k_out"), 16)
            sp.wait_ge(sem("s4_k_out"), k_out)
            turn()
            for g in range(GROUPS):
                src = bass.AP(tensor=k_pad.tensor, offset=g * HG * 2 * CHUNK, ap=[[1, CHUNK], [2 * CHUNK, HG], [1, CHUNK]])
                sp.dma_start(tp[0:CHUNK, HG * g:HG * (g + 1), :], src).then_inc(sem("s4_toep_in"), 16)
            sp.wait_ge(sem("s4_u"), one)
            turn()
            for ri, src in ((0, u_re), (1, u_im)):
                for g in range(GROUPS):
                    at = CHUNK + MODES * ri
                    sp.dma_start(zu[at:at + MODES, HG * g:HG * (g + 1), :], src[32 * g:32 * g + 32]).then_inc(sem("s4_u_moved"), 16)
            if more:
                sp.wait_ge(sem("s4_h"), h)
                turn()
                s4_layer_loads(sp, L + 1)

        def moe_act(act):
            A = nc.scalar
            ln_act(act, LN_B, "lnB_out", hT, one_plus[:, 4:5], mod[:, 3:4])
            act.wait_ge(sem("moe_shifted"), 1)
            A.activation(weight, logit, ACT.Exp).then_inc(sem("moe_exp"), 1)
            with act.Fori(0, BLOCKS) as b:
                for m in range(HID_CHUNKS):
                    act.wait_ge(sem("moe_h"), b * HID_CHUNKS + m + 1)
                    A.activation(hid[:, m, :], bank[m][:, :], ACT.Gelu).then_inc(sem("moe_hid"), 1)

        def moe_dve(dve, link):
            V = nc.vector
            ln_dve(dve, LN_B, moe_norm)
            link(V.memset(fresh, 1.0))
            g3 = lambda t: t.rearrange("p c (r e) -> p (c r) e", r=ROUTERS)
            flat = lambda t: t.rearrange("p c e -> p (c e)")
            groups = TILES * ROUTERS
            wide = [P, groups, EXPERTS]
            V.memset(g3(fresh)[:, :, 0:1], 0.0)
            for b in range(BLOCKS):
                dve.wait_ge(sem("moe_addr_ps"), b + 1)
                V.tensor_copy(addr[:, 512 * b:512 * b + 512], bank[b][0:ADDR, :]).then_inc(sem("moe_addr"), 1)
            half = TILES // 2
            for i in range(2):
                dve.wait_ge(sem("moe_logit_ps"), i + 1)
                link(V.tensor_copy(logit[:, half * i:half * (i + 1), :],
                                   bank[4 + i][:, 0:half * 36].rearrange("p (c e) -> p c e", e=36)))
            for k in range(groups):
                last = V.max(top8[:, k, :], g3(logit)[:, k, :])
            link(last)
            third = top8[:, :, 2:3].to_broadcast(wide)
            V.tensor_tensor(g3(above), g3(logit), third, ALU.is_gt)
            link(V.tensor_tensor(g3(equal), g3(logit), third, ALU.is_equal))
            V.tensor_tensor_scan(flat(ranks), flat(fresh), flat(equal), 0.0, ALU.mult, ALU.add)
            V.tensor_tensor(g3(logit), g3(logit), top8[:, :, 0:1].to_broadcast(wide), ALU.subtract).then_inc(sem("moe_shifted"), 1)
            link(V.tensor_reduce(room, g3(above), AX.X, ALU.add))
            link(V.tensor_scalar(room, room, -1.0, float(TOP), ALU.mult, ALU.add))
            link(V.tensor_tensor(g3(ranks), g3(ranks), room.unsqueeze(2).to_broadcast(wide), ALU.is_le))
            link(V.tensor_tensor(equal, equal, ranks, ALU.mult))
            link(V.tensor_tensor(above, above, equal, ALU.add))
            dve.wait_ge(sem("moe_exp"), 1)
            link(V.tensor_tensor(weight, weight, above, ALU.mult))
            link(V.tensor_reduce(total, g3(weight), AX.X, ALU.add))
            link(V.reciprocal(total, total))
            V.tensor_tensor(g3(weight), g3(weight), total.unsqueeze(2).to_broadcast(wide), ALU.mult).then_inc(sem("moe_weight"), 1)
            for b in range(BLOCKS):
                dve.wait_ge(sem("moe_wT_ps"), b + 1)
                V.tensor_copy(weightT[:, 512 * b:512 * b + 512], bank[b][0:36, :]).then_inc(sem("moe_wT"), 1)
            dve.wait_ge(sem("lnB_out"), BLOCKS)

        def moe_dve_blocks(dve, chain):
            V = nc.vector
            for name in ("moe_share_free1", "moe_share_free2", "moe_x_free", "moe_x"):
                dve.sem_inc(sem(name), 1)
            with dve.Fori(0, BLOCKS) as b:
                chain.body(b, EXPERTS)
                dve.wait_ge(sem("moe_share_in1"), b * 16 + 16)
                dve.wait_ge(sem("moe_x_free"), b + 1)
                for e in range(EXPERTS):
                    V.tensor_tensor(x_exp[:, e, :], hT[:, bass.ts(b, 512)], share1[:, e, :], ALU.mult).then_inc(sem("moe_xe"), 1)
                dve.wait_ge(sem("moe_xe"), b * EXPERTS + EXPERTS)
                dve.sem_inc(sem("moe_share_free1"), 1)
                dve.wait_ge(sem("moe_share_in2"), b * 16 + 16)
                for e in range(EXPERTS):
                    dve.wait_ge(sem("moe_y_ps"), b * EXPERTS + e + 1)
                    part = y_acc if e == 0 else y_part[e % 2]
                    V.tensor_tensor(part, bank[4 + e % 2][:, :], share2[:, e, :], ALU.mult).then_inc(sem("moe_y_read"), 1)
                    if e:
                        dve.wait_ge(sem("moe_y_read"), b * EXPERTS + e + 1)
                        if e > 1:
                            chain.wait()
                        chain.mark(V.tensor_tensor(y_acc, y_acc, part, ALU.add))
                dve.sem_inc(sem("moe_share_free2"), 1)
                chain.wait()
                dve.wait_ge(sem("moe_b2_ps"), b + 1)
                chain.link(V.tensor_tensor(y_acc, y_acc, bank[6][:, :], ALU.add))
                V.scalar_tensor_tensor(xT[:, bass.ts(b, 512)], y_acc, gate[:, 5:6], xT[:, bass.ts(b, 512)],
                                       ALU.mult, ALU.add).then_inc(sem("moe_x"), 1)
                dve.wait_ge(sem("moe_x"), b + 2)
            chain.leave(BLOCKS)

        def moe_pe(pe):
            T = nc.tensor
            pe.wait_ge(sem("x_s4"), BLOCKS)
            ln_pe_tokens(pe, xT)
            ln_pe_back(pe, LN_B, moe_norm)
            pe.wait_ge(sem("moe_consts_in"), 48)
            for b in range(BLOCKS):
                pe.wait_ge(sem("lnB_out"), b + 1)
                T.matmul(bank[b][0:ADDR, :], pw_sb, hT[:, 512 * b:512 * b + 512], start=True, stop=True).then_inc(sem("moe_addr_ps"), 1)
            half = TILES // 2
            for c in range(TILES):
                pe.wait_ge(sem("moe_addr"), c // 4 + 1)
                last = T.matmul(bank[4 + c // half][:, 36 * (c % half):36 * (c % half) + 36],
                                addr[:, c * P:(c + 1) * P], u_sb, start=True, stop=True)
                if c % half == half - 1:
                    last.then_inc(sem("moe_logit_ps"), 1)
            pe.wait_ge(sem("moe_weight"), 1)
            for c in range(TILES):
                last = T.transpose(bank[c // 4][0:36, (c % 4) * P:(c % 4 + 1) * P], weight[:, c, :], ident)
                if c % 4 == 3:
                    last.then_inc(sem("moe_wT_ps"), 1)
            pe.wait_ge(sem("moe_wT"), BLOCKS)
            pe.wait_ge(sem("moe_w1_in"), 16)
            pe.wait_ge(sem("moe_w2_in"), 16)
            with pe.Fori(0, BLOCKS) as b:
                for m in range(HID_CHUNKS):
                    for e in range(EXPERTS):
                        if m == 0:
                            pe.wait_ge(sem("moe_xe"), b * EXPERTS + e + 1)
                        last = T.matmul(bank[m][:, :], w1_sb[:, e, m * P:(m + 1) * P], x_exp[:, e, :],
                                        start=(e == 0), stop=(e == EXPERTS - 1))
                    last.then_inc(sem("moe_h"), 1)
                pe.wait_ge(sem("moe_h"), b * HID_CHUNKS + HID_CHUNKS)
                pe.sem_inc(sem("moe_x_free"), 1)
                pe.wait_ge(sem("moe_x"), b + 1)
                T.matmul(bank[6][:, :], b2_sb, weightT[0:EXPERTS, bass.ts(b, 512)], start=True, stop=True).then_inc(sem("moe_b2_ps"), 1)
                pe.wait_ge(sem("moe_hid"), b * HID_CHUNKS + HID_CHUNKS)
                for e in range(EXPERTS):
                    if e >= 2:
                        pe.wait_ge(sem("moe_y_read"), b * EXPERTS + e - 1)
                    for m in range(HID_CHUNKS):
                        last = T.matmul(bank[4 + e % 2][:, :], w2_sb[:, e, m, :], hid[:, m, :],
                                        start=(m == 0), stop=(m == HID_CHUNKS - 1))
                    last.then_inc(sem("moe_y_ps"), 1)

        def gla_act(act):
            A = nc.scalar
            ln_act(act, LN_C, "lnC_out", hT, one_plus[:, 7:8], mod[:, 6:7])
            for k in range(8):
                act.wait_ge(sem("gla_max"), k + 1)
                for i in range(4):
                    c, j = 2 * k + i // 2, i % 2
                    last = A.activation(soft[:, c, j, :], bank[k][:, i * P:(i + 1) * P], ACT.Exp,
                                        bias=neg_max[:, c, j:j + 1], accum_out=soft_sum[:, c, j:j + 1])
                last.then_inc(sem("gla_exp"), 1)
            for b in range(BLOCKS):
                act.wait_ge(sem("gla_T_ps"), 2 * b + 2)
                sl = slice(512 * b, 512 * b + 512)
                A.activation(keepT[:, sl], bank[2 * b % 8 + 1][:, :], ACT.Copy)
                A.activation(kT[:, sl], bank[2 * b % 8 + 1][:, :], ACT.Copy, scale=-1.0, bias=1.0).then_inc(sem("gla_k"), 1)

        def gla_dve(dve, link):
            V = nc.vector
            ln_dve(dve, LN_C, gla_norm)
            for k in range(8):
                dve.wait_ge(sem("gla_logit_ps"), k + 1)
                V.tensor_reduce(neg_max[:, 2 * k:2 * k + 2, :].rearrange("p c j -> p (c j)"),
                                bank[k][:, :].rearrange("p (i d) -> p i d", i=4), AX.X, ALU.max,
                                negate=True).then_inc(sem("gla_max"), 1)
            for k in range(8):
                dve.wait_ge(sem("gla_exp"), k + 1)
                two = slice(2 * k, 2 * k + 2)
                link(V.reciprocal(soft_sum[:, two, :], soft_sum[:, two, :]))
                link(V.tensor_scalar(soft_sum[:, two, 0:1], soft_sum[:, two, 0:1], LIN_DIM ** -0.5, None, ALU.mult))
                V.tensor_tensor(soft[:, two].rearrange("p c j d -> p (c j) d"), soft[:, two].rearrange("p c j d -> p (c j) d"),
                                soft_sum[:, two, :].rearrange("p c j -> p (c j)").unsqueeze(2).to_broadcast([P, 4, P]),
                                ALU.mult).then_inc(sem("gla_soft"), 1)
            for b in range(BLOCKS):
                dve.wait_ge(sem("gla_T_ps"), 2 * b + 1)
                V.tensor_copy(qT[:, 512 * b:512 * b + 512], bank[2 * b % 8][:, :]).then_inc(sem("gla_q"), 1)
            dve.wait_ge(sem("gla_k"), BLOCKS)
            for v in range(LIN_DIM):
                i = v % 2
                for b in range(BLOCKS):
                    dve.wait_ge(sem("gla_v_ps"), BLOCKS * v + b + 1)
                    sl = slice(512 * b, 512 * b + 512)
                    V.tensor_tensor(kv[i][:, sl], bank[b][:, :], kT[:, sl], ALU.mult).then_inc(sem("gla_kv"), 1)
                dve.wait_ge(sem("gla_kv"), BLOCKS * (v + 1))
                if v >= 2:
                    dve.wait_ge(sem("gla_read"), v - 1)
                V.tensor_tensor_scan(state[i], keepT, kv[i], 0.0, ALU.mult, ALU.add).then_inc(sem("gla_state"), 1)
            for b in range(BLOCKS):
                dve.wait_ge(sem("gla_o_ps"), b + 1)
                sl = slice(512 * b, 512 * b + 512)
                V.scalar_tensor_tensor(xT[:, sl], bank[4 + b][:, :], gate[:, 8:9], xT[:, sl], ALU.mult, ALU.add).then_inc(sem("gla_x"), 1)

        def gla_pe(pe):
            T = nc.tensor
            pe.wait_ge(sem("moe_x"), BLOCKS + 1)
            ln_pe_tokens(pe, xT)
            ln_pe_back(pe, LN_C, gla_norm)
            pe.wait_ge(sem("gla_w_in"), 48)
            pe.wait_ge(sem("lnC_out"), BLOCKS)
            for c in range(TILES):
                last = T.matmul(bank[c // 2][:, 256 * (c % 2):256 * (c % 2) + 256], hT[:, c * P:(c + 1) * P], wqf_sb, start=True, stop=True)
                if c % 2:
                    last.then_inc(sem("gla_logit_ps"), 1)
            pe.wait_ge(sem("gla_exp"), 8)
            for b in range(BLOCKS):
                pe.wait_ge(sem("gla_soft"), 2 * b + 2)
                for j in range(2):
                    for t in range(4):
                        last = T.transpose(bank[2 * b + j][:, t * P:(t + 1) * P], soft[:, 4 * b + t, j, :], ident)
                    last.then_inc(sem("gla_T_ps"), 1)

            def values(v):
                for b in range(BLOCKS):
                    if v:
                        pe.wait_ge(sem("gla_kv"), BLOCKS * (v - 1) + b + 1)
                    T.matmul(bank[b][:, :], wi_sb[:, v, :], hT[:, 512 * b:512 * b + 512], start=True, stop=True).then_inc(sem("gla_v_ps"), 1)

            pe.wait_ge(sem("gla_q"), BLOCKS)
            pe.wait_ge(sem("gla_k"), BLOCKS)
            values(0)
            for v in range(LIN_DIM):
                if v + 1 < LIN_DIM:
                    values(v + 1)
                pe.wait_ge(sem("gla_read"), v + 1)
                for b in range(BLOCKS):
                    last = T.matmul(bank[4 + b][:, :], wo8_sb[:, v, :], read[v % 2][:, 512 * b:512 * b + 512],
                                    start=(v == 0), stop=(v == LIN_DIM - 1))
                    if v == LIN_DIM - 1:
                        last.then_inc(sem("gla_o_ps"), 1)
                if v < LIN_DIM - 1:
                    last.then_inc(sem("gla_read_used"), 1)

        def ff_act(act):
            A = nc.scalar
            ln_act(act, LN_D, "lnD_out", hT, one_plus[:, 10:11], mod[:, 9:10])
            with act.Fori(0, DEPTH) as L:
                for c in range(TILES):
                    i = c % 2
                    act.wait_ge(sem("ff_qk_ps"), L * TILES + c + 1)
                    if c:
                        act.wait_ge(sem("ff_norm2"), L * TILES + c)
                    for j in range(2):
                        A.activation(squares[:, j], bank[j][:, :], ACT.Square).then_inc(sem("ff_sq"), 1)
                    act.wait_ge(sem("ff_v_ps"), L * TILES + c + 1)
                    A.activation(v_tok[:, c, :], bank[2][:, :], ACT.Copy).then_inc(sem("ff_v"), 1)
                    act.wait_ge(sem("ff_norm2"), L * TILES + c + 1)
                    A.activation(norms[:, c], norms[:, c], ACT.Sqrt).then_inc(sem("ff_norm"), 1)
                    act.wait_ge(sem("ff_qT_ps"), L * TILES + c + 1)
                    A.activation(qhT[:, :, c * P:(c + 1) * P], bank[4][:, :].rearrange("p (j t) -> p j t", j=4), ACT.Copy).then_inc(sem("ff_qT"), 1)
                    act.wait_ge(sem("ff_kT_ps"), L * TILES + c + 1)
                    A.activation(khT[:, :, c * P:(c + 1) * P], bank[5][:, :].rearrange("p (j t) -> p j t", j=4), ACT.Copy).then_inc(sem("ff_kT"), 1)
                for c in range(TILES):
                    act.wait_ge(sem("at_bias"), L * TILES + c + 1)
                    if c:
                        act.wait_ge(sem("at_P_used"), L * TILES + c)
                    for h in range(HEADS):
                        first = WINDOW if c == 0 else 0
                        A.activation(probs[:, h, WINDOW + first:2 * P], scores[:, h, first:KEYS], ACT.Exp,
                                     scale=row_scale[:, h:h + 1], bias=row_bias[:, h:h + 1],
                                     accum_out=row_sum[:, h:h + 1]).then_inc(sem("at_exp"), 1)
                    for k in range(1, 4, 2):
                        act.wait_ge(sem("at_PT_ps"), L * 4 * TILES + 4 * c + k + 1)
                        A.activation(probsT[:, 4 * k:4 * k + 4, :], bank[4 + k % 2][:, :].rearrange("p (a b) -> p a b", a=4),
                                     ACT.Copy).then_inc(sem("at_PT_act"), 1)
                    act.wait_ge(sem("at_o_ps"), L * TILES + c + 1)
                    if c % 4 == 0 and c:
                        act.wait_ge(sem("at_wo_ps"), L * BLOCKS + c // 4)
                    A.activation(oT[:, :, (c % 4) * P:(c % 4 + 1) * P], bank[6][:, :].rearrange("p (j t) -> p j t", j=4), ACT.Copy).then_inc(sem("at_o"), 1)
                for b in range(BLOCKS):
                    act.wait_ge(sem("ln_back"), (LN_FF - S4_LAYERS) * BLOCKS + L * BLOCKS + b + 1)
                    A.activation(nT[:, 512 * b:512 * b + 512], bank[4 + b][:, :], ACT.Identity, bias=cols[:, 8:9],
                                 scale=cols[:, 7:8]).then_inc(sem("ff_nT"), 1)
                n = len(FF_CHUNKS)
                for b in range(BLOCKS):
                    for i, (at, size) in enumerate(FF_CHUNKS):
                        k = n * b + i
                        act.wait_ge(sem("ff_ag_ps"), L * n * BLOCKS + k + 1)
                        if k >= 2:
                            act.wait_ge(sem("ff_act"), L * n * BLOCKS + k - 1)
                        A.activation(ff_g[0:size, k % 2, :], bank[2 * (k % 2) + 1][0:size, :], ACT.Gelu,
                                     bias=cols[0:size, 3 + i:4 + i]).then_inc(sem("ff_gelu"), 1)

        def ff_dve(dve, chain):
            V = nc.vector
            link = chain.link
            ln_dve(dve, LN_D, ff_norm)
            link(V.memset(probs, 0.0))
            dve.wait_ge(sem("ff_consts_in"), 32)
            dve.wait_ge(sem("lnD_out"), BLOCKS)
            dve.sem_inc(sem("ff_wqkv_free"), 1)
            dve.sem_inc(sem("ff_w_free"), 1)

            def shift(name):
                V.memset(sT[HEAD_DIM:P, 0:1], 0.0)
                V.tensor_copy(sT[0:HEAD_DIM, :], hT[0:HEAD_DIM, :])
                V.tensor_copy(sT[HEAD_DIM:P, 1:N_TOK], hT[HEAD_DIM:P, 0:N_TOK - 1]).then_inc(sem(name), 1)

            with dve.Fori(0, DEPTH) as L:
                chain.body(L, FF_DVE_LINKS)
                shift("ff_s")
                dve.wait_ge(sem("ff_tables"), L + 1)
                for c in range(TILES):
                    i = c % 2
                    for j, dst in ((0, q_rot), (1, k_rot)):
                        dve.wait_ge(sem("ff_sq"), L * 2 * TILES + 2 * c + j + 1)
                        x4 = bank[j][:, :].rearrange("p (h s d) -> p h s d", h=HEADS, s=2)
                        if c:
                            dve.wait_ge(sem("ff_q" if j == 0 else "ff_k"), L * TILES + c)
                        if c >= 2:
                            dve.wait_ge(sem("ff_qT_ps" if j == 0 else "ff_kT_ps"), L * TILES + c - 1)
                        row = scaled[:, 2 * j, c, :].unsqueeze(1).to_broadcast([P, HEADS, HEAD_DIM])
                        V.tensor_tensor(dst[:, i].rearrange("p (h d) -> p h d", h=HEADS),
                                        bank[j][:, :].rearrange("p (h d) -> p h d", h=HEADS), row, ALU.mult)
                        row = scaled[:, 2 * j + 1, c, :].rearrange("p (s d) -> p s d", s=2).unsqueeze(1).to_broadcast([P, HEADS, 2, HEAD_DIM // 2])
                        V.tensor_tensor(rot_tmp[:, j].rearrange("p (h s d) -> p h s d", h=HEADS, s=2),
                                        x4[:, :, ::-1, :], row, ALU.mult).then_inc(sem("ff_rot"), 1)
                    link(V.tensor_reduce(norms[:, c].rearrange("p j h -> p (j h)"),
                                         squares.rearrange("p j (h d) -> p (j h) d", h=HEADS), AX.X, ALU.add))
                    V.tensor_scalar(norms[:, c], norms[:, c], 1e-24, None, ALU.max).then_inc(sem("ff_norm2"), 1)
                    dve.wait_ge(sem("ff_norm"), L * TILES + c + 1)
                    V.reciprocal(inv_norm[:, c], norms[:, c]).then_inc(sem("ff_inv"), 1)
                dve.wait_ge(sem("ff_v"), L * TILES + TILES)
                dve.wait_ge(sem("ff_inv"), L * TILES + TILES)
                dve.sem_inc(sem("ff_wqkv_free"), 1)
                for c in range(TILES):
                    first = WINDOW if c == 0 else 0
                    if c:
                        dve.wait_ge(sem("at_exp"), L * HEADS * TILES + HEADS * c)
                    for k in range(4):
                        dve.wait_ge(sem("at_s_ps"), L * 4 * TILES + 4 * c + k + 1)
                        s2 = bank[k][:, 0:2 * KEYS].rearrange("p (h j) -> p h j", h=2)
                        h0 = 4 * (k // 2) + k % 2
                        V.tensor_tensor(scores[:, h0:h0 + 3:2, first:KEYS], s2[:, :, first:KEYS],
                                        mask_sb[:, first:KEYS].unsqueeze(1).to_broadcast([P, 2, KEYS - first]),
                                        ALU.add).then_inc(sem("at_s"), 1)
                    V.tensor_scalar(row_scale, inv_norm[:, c, 0, :], QK_SCALE, None, ALU.mult)
                    dve.wait_ge(sem("at_s"), L * 4 * TILES + 4 * c + 4)
                    link(V.tensor_reduce(row_max, scores[:, :, first:KEYS], AX.X, ALU.max))
                    V.scalar_tensor_tensor(row_bias, row_max, -1.0, row_scale, ALU.mult, ALU.mult).then_inc(sem("at_bias"), 1)
                    dve.wait_ge(sem("at_exp"), L * HEADS * TILES + HEADS * (c + 1))
                    link(V.reciprocal(row_inv, row_sum))
                    V.tensor_tensor(probs[:, :, WINDOW + first:2 * P], probs[:, :, WINDOW + first:2 * P],
                                    row_inv.unsqueeze(2).to_broadcast([P, HEADS, KEYS - first]), ALU.mult).then_inc(sem("at_P"), 1)
                    for k in range(0, 4, 2):
                        dve.wait_ge(sem("at_PT_ps"), L * 4 * TILES + 4 * c + k + 1)
                        V.tensor_copy(probsT[:, 4 * k:4 * k + 4, :], bank[4 + k % 2][:, :].rearrange("p (a b) -> p a b", a=4)).then_inc(sem("at_PT_dve"), 1)
                    if c % 4 == 3:
                        b = c // 4
                        dve.wait_ge(sem("at_wo_ps"), L * BLOCKS + b + 1)
                        sl = slice(512 * b, 512 * b + 512)
                        link(V.tensor_tensor(hT[:, sl], hT[:, sl], bank[7][:, :], ALU.add))
                dve.wait_ge(sem("at_o"), L * TILES + TILES)
                shift("ff_s2")
                ln_dve(dve, LN_FF + L, ff_norm)
                n = len(FF_CHUNKS)
                for b in range(BLOCKS):
                    for i, (at, size) in enumerate(FF_CHUNKS):
                        k = n * b + i
                        dve.wait_ge(sem("ff_gelu"), L * n * BLOCKS + k + 1)
                        if b and i == 0:
                            dve.wait_ge(sem("ff_y_ps"), L * BLOCKS + b)
                        V.scalar_tensor_tensor(ff_h[0:size, i, :], bank[2 * (k % 2)][0:size, :], cols[0:size, i:i + 1],
                                               ff_g[0:size, k % 2, :], ALU.add, ALU.mult).then_inc(sem("ff_act"), 1)
                    dve.wait_ge(sem("ff_y_ps"), L * BLOCKS + b + 1)
                    sl = slice(512 * b, 512 * b + 512)
                    V.scalar_tensor_tensor(hT[:, sl], bank[4 + b % 2][:, :], cols[:, 6:7], hT[:, sl], ALU.add, ALU.add).then_inc(sem("ff_x"), 1)
                dve.wait_ge(sem("ff_x"), L * BLOCKS + BLOCKS)
                dve.sem_inc(sem("ff_w_free"), 1)
            chain.leave(DEPTH)
            for b in range(BLOCKS):
                sl = slice(512 * b, 512 * b + 512)
                V.scalar_tensor_tensor(xT[:, sl], hT[:, sl], gate[:, 11:12], xT[:, sl], ALU.mult, ALU.add).then_inc(sem("x_ff"), 1)

        def ff_pe(pe):
            T = nc.tensor
            pe.wait_ge(sem("gla_x"), BLOCKS)
            ln_pe_tokens(pe, xT)
            ln_pe_back(pe, LN_D, ff_norm)
            pe.wait_ge(sem("lnD_out"), BLOCKS)
            with pe.Fori(0, DEPTH) as L:
                pe.wait_ge(sem("ff_s"), L + 1)
                pe.wait_ge(sem("ff_wqkv_in"), L * 32 + 32)

                def project(c):
                    if c:
                        pe.wait_ge(sem("ff_rot"), L * 2 * TILES + 2 * c)
                        pe.wait_ge(sem("ff_sq"), L * 2 * TILES + 2 * c)
                    x = sT[:, c * P:(c + 1) * P]
                    T.matmul(bank[0][:, :], x, wqkv_sb[:, 0:512], start=True, stop=True)
                    T.matmul(bank[1][:, :], x, wqkv_sb[:, 512:1024], start=True, stop=True).then_inc(sem("ff_qk_ps"), 1)
                    if c:
                        pe.wait_ge(sem("ff_v"), L * TILES + c)
                    T.matmul(bank[2][:, :], x, wqkv_sb[:, 1024:1536], start=True, stop=True).then_inc(sem("ff_v_ps"), 1)

                project(0)
                for c in range(TILES):
                    if c + 1 < TILES:
                        project(c + 1)
                    for name, src, bk in (("q", q_rot, 4), ("k", k_rot, 5)):
                        pe.wait_ge(sem("ff_" + name), L * TILES + c + 1)
                        if c:
                            pe.wait_ge(sem(f"ff_{name}T"), L * TILES + c)
                        for j in range(4):
                            last = T.transpose(bank[bk][:, j * P:(j + 1) * P], src[:, c % 2, j * P:(j + 1) * P], ident)
                        last.then_inc(sem(f"ff_{name}T_ps"), 1)

                def score(c):
                    first = WINDOW if c == 0 else 0
                    for k in range(4):
                        for i in range(2):
                            bk, slot = 2 * (k // 2) + i, k % 2
                            if c and slot == 0:
                                pe.wait_ge(sem("at_s"), L * 4 * TILES + 4 * (c - 1) + bk + 1)
                            r = slice(64 * i, 64 * i + 64)
                            last = T.matmul(bank[bk][:, KEYS * slot + first:KEYS * (slot + 1)], qhT[r, k, c * P:(c + 1) * P],
                                            khT[r, k, c * P - WINDOW + first:(c + 1) * P], start=True, stop=True)
                            if slot == 1:
                                last.then_inc(sem("at_s_ps"), 1)

                pe.wait_ge(sem("ff_qT"), L * TILES + TILES)
                pe.wait_ge(sem("ff_kT"), L * TILES + TILES)
                pe.wait_ge(sem("ff_w_in"), L * 64 + 64)
                score(0)
                for c in range(TILES):
                    if c + 1 < TILES:
                        score(c + 1)
                    pe.wait_ge(sem("at_P"), L * TILES + c + 1)
                    for k in range(4):
                        if k >= 2:
                            pe.wait_ge(sem("at_PT_dve" if k == 2 else "at_PT_act"), L * 2 * TILES + 2 * c + 1)
                        for i in range(2):
                            for part in range(2):
                                last = T.transpose(bank[4 + k % 2][:, (2 * i + part) * P:(2 * i + part + 1) * P],
                                                   probs[:, 2 * k + i, part * P:(part + 1) * P], ident)
                        last.then_inc(sem("at_PT_ps"), 1)
                    pe.wait_ge(sem("at_PT_ps"), L * 4 * TILES + 4 * c + 4)
                    pe.sem_inc(sem("at_P_used"), 1)
                    if c:
                        pe.wait_ge(sem("at_o"), L * TILES + c)
                    for k in range(4):
                        if k % 2 == 0:
                            pe.wait_ge(sem("at_PT_dve"), L * 2 * TILES + 2 * c + k // 2 + 1)
                        else:
                            pe.wait_ge(sem("at_PT_act"), L * 2 * TILES + 2 * c + k // 2 + 1)
                        for i in range(2):
                            h = 2 * k + i
                            dst = bank[6][64 * i:64 * i + 64, k * P:(k + 1) * P]
                            last = T.matmul(dst, v_tok[:, c, 64 * h:64 * h + 64], probsT[:, 2 * h + 1, :], start=True, stop=(c == 0))
                            if c:
                                last = T.matmul(dst, v_tok[64:128, c - 1, 64 * h:64 * h + 64], probsT[64:128, 2 * h, :], start=False, stop=True)
                    last.then_inc(sem("at_o_ps"), 1)
                    if c % 4 == 3:
                        pe.wait_ge(sem("at_o"), L * TILES + c + 1)
                        for j in range(4):
                            last = T.matmul(bank[7][:, :], wo_sb[:, j, :], oT[:, j, :], start=(j == 0), stop=(j == 3))
                        last.then_inc(sem("at_wo_ps"), 1)
                pe.wait_ge(sem("ff_s2"), L + 1)
                ln_pe_tokens(pe, sT)
                ln_pe_back(pe, LN_FF + L, ff_norm)
                n = len(FF_CHUNKS)
                pe.wait_ge(sem("ff_nT"), L * BLOCKS + BLOCKS)
                for b in range(BLOCKS):
                    rhs = nT[:, 512 * b:512 * b + 512]
                    for i, (at, size) in enumerate(FF_CHUNKS):
                        k = n * b + i
                        if k >= 2:
                            pe.wait_ge(sem("ff_act"), L * n * BLOCKS + k - 1)
                        T.matmul(bank[2 * (k % 2)][0:size, :], wf1_sb[:, at:at + size], rhs, start=True, stop=True)
                        T.matmul(bank[2 * (k % 2) + 1][0:size, :], wf1_sb[:, FF + at:FF + at + size], rhs,
                                 start=True, stop=True).then_inc(sem("ff_ag_ps"), 1)
                    pe.wait_ge(sem("ff_act"), L * n * BLOCKS + n * (b + 1))
                    if b >= 2:
                        pe.wait_ge(sem("ff_x"), L * BLOCKS + b - 1)
                    for i, (at, size) in enumerate(FF_CHUNKS):
                        last = T.matmul(bank[4 + b % 2][:, :], wf2_sb[0:size, i, :], ff_h[0:size, i, :],
                                        start=(i == 0), stop=(i == n - 1))
                    last.then_inc(sem("ff_y_ps"), 1)
                pe.wait_ge(sem("ff_x"), L * BLOCKS + BLOCKS)

        @block.sync
        def _(sp):
            sp.dma_start(ident, dram["ident"]).then_inc(sem("consts_in"), 16)
            sp.dma_start(cond, dram["cond"]).then_inc(sem("consts_in"), 16)
            sp.dma_start(wmod_sb, dram["wmod"]).then_inc(sem("consts_in"), 16)
            sp.dma_start(xT, dram["xT"]).then_inc(sem("x_in"), 16)
            sp.dma_start(sel, dram["sel"]).then_inc(sem("s4_consts_in"), 16)
            sp.dma_start(expo, dram["expo"].to_broadcast([P, N_EXP])).then_inc(sem("s4_consts_in"), 16)
            sp.wait_ge(sem("zero_set"), 1)
            sp.dma_start(k_pad[:, CHUNK:2 * CHUNK], k_im[:, 0, :]).then_inc(sem("s4_zero_out"), 16)
            sp.dma_start(prm, dram["prm"][0]).then_inc(sem("s4_prm_in"), 16)
            s4_layer_loads(sp, 0)
            s4_sp_layer(sp, 0, more=True)
            with sp.Fori(1, S4_LAYERS - 1) as L:
                s4_sp_layer(sp, L, more=True)
            s4_sp_layer(sp, S4_LAYERS - 1, more=False)
            if stage != "s4d":
                sp.wait_ge(sem("x_s4"), BLOCKS)
                for dst, name in ((pw_sb, "pw"), (u_sb, "u"), (b2_sb, "b2")):
                    sp.dma_start(dst, dram[name]).then_inc(sem("moe_consts_in"), 16)
                sp.dma_start(w1_sb, dram["w1"]).then_inc(sem("moe_w1_in"), 16)
                sp.dma_start(w2_sb, dram["w2"]).then_inc(sem("moe_w2_in"), 16)
                sp.wait_ge(sem("moe_wT"), BLOCKS)
                sp.dma_start(share_d, weightT).then_inc(sem("moe_wT_out"), 16)
                sp.wait_ge(sem("moe_wT_out"), 16)
                with sp.Fori(0, BLOCKS) as b:
                    free = sp.snap(b + 1)
                    for r, (dst, name) in enumerate(((share1, "1"), (share2, "2"))):
                        sp.wait_ge(sem("moe_share_free" + name), free)
                        sp.sem_inc(sem("sp_turn"), 1)
                        rows = share_d[(r + 1) * EXPERTS:(r + 2) * EXPERTS, bass.ts(b, 512)]
                        sp.dma_start(dst, rows.partition_broadcast(P)).then_inc(sem("moe_share_in" + name), 16)
            if stage not in ("s4d", "moe"):
                sp.wait_ge(sem("moe_x"), BLOCKS + 1)
                for dst, name in ((wqf_sb, "wqf"), (wi_sb, "wi"), (wo8_sb, "wo8")):
                    sp.dma_start(dst, dram[name]).then_inc(sem("gla_w_in"), 16)
            if stage == "full":
                sp.wait_ge(sem("gla_x"), BLOCKS)
                sp.dma_start(mask_sb, dram["mask"]).then_inc(sem("ff_consts_in"), 16)
                sp.dma_start(tables, dram["tables"]).then_inc(sem("ff_consts_in"), 16)
                with sp.Fori(0, DEPTH) as L:
                    one = sp.snap(L + 1)
                    sp.wait_ge(sem("ff_wqkv_free"), one)
                    sp.sem_inc(sem("sp_turn"), 1)
                    sp.dma_start(wqkv_sb, dram["wqkv"][L]).then_inc(sem("ff_wqkv_in"), 16)
                    sp.dma_start(qk_rows, dram["qk_rows"][L]).then_inc(sem("ff_wqkv_in"), 16)
                    sp.wait_ge(sem("ff_w_free"), one)
                    sp.sem_inc(sem("sp_turn"), 1)
                    for dst, name in ((wo_sb, "wo"), (wf1_sb, "wf1"), (wf2_sb, "wf2"), (cols, "cols")):
                        sp.dma_start(dst, dram[name][L]).then_inc(sem("ff_w_in"), 16)
            sp.wait_ge(sem("result"), BLOCKS)
            sp.dma_start(out.rearrange("o (c i) d -> i (o c) d", i=P), ff_norm).then_inc(sem("stored"), 16)
            sp.wait_ge(sem("stored"), 16)

        @block.gpsimd
        def _(pool):
            nc.gpsimd.memset(eps_col, EPS_LN)
            nc.gpsimd.memset(neg_half, -0.5).then_inc(sem("p_set"), 1)
            pool.wait_ge(sem("p_set"), 1)
            ln_pool(pool, LN_A)
            chain = Chain(pool, sem("p_chain"))
            pool.wait_ge(sem("s4_consts_in"), 32)
            s4_pool_powers(pool, chain, 0)
            with pool.Fori(0, S4_LAYERS - 1) as L:
                chain.body(L, 1)
                ln_pool(pool, LN_S4 + L)
                pool.wait_ge(sem("s4_pow_moved"), L * 128 + 128)
                pool.wait_ge(sem("s4_u"), L + 1)
                s4_pool_powers(pool, chain, L + 1)
            chain.leave(S4_LAYERS - 1)
            ln_pool(pool, LN_S4 + S4_LAYERS - 1)
            if stage != "s4d":
                ln_pool(pool, LN_B)
            if stage not in ("s4d", "moe"):
                ln_pool(pool, LN_C)
                for v in range(LIN_DIM):
                    i = v % 2
                    pool.wait_ge(sem("gla_state"), v + 1)
                    if v >= 2:
                        pool.wait_ge(sem("gla_read_used"), v - 1)
                    nc.gpsimd.tensor_tensor(read[i], state[i], qT, ALU.mult).then_inc(sem("gla_read"), 1)
            if stage == "full":
                ln_pool(pool, LN_D)
                pool.wait_ge(sem("ff_consts_in"), 32)
                with pool.Fori(0, DEPTH) as L:
                    chain.body(L, TILES)
                    pool.wait_ge(sem("ff_wqkv_in"), L * 32 + 32)
                    for i in range(4):
                        row = qk_rows[:, i, :].unsqueeze(1).to_broadcast([P, TILES, HEAD_DIM])
                        last = nc.gpsimd.tensor_tensor(scaled[:, i], tables[:, i], row, ALU.mult)
                    last.then_inc(sem("ff_tables"), 1)
                    for c in range(TILES):
                        i = c % 2
                        pool.wait_ge(sem("ff_rot"), L * 2 * TILES + 2 * c + 1)
                        nc.gpsimd.tensor_tensor(q_rot[:, i], q_rot[:, i], rot_tmp[:, 0], ALU.add).then_inc(sem("ff_q"), 1)
                        pool.wait_ge(sem("ff_rot"), L * 2 * TILES + 2 * c + 2)
                        chain.link(nc.gpsimd.tensor_tensor(k_rot[:, i], k_rot[:, i], rot_tmp[:, 1], ALU.add))
                        pool.wait_ge(sem("ff_inv"), L * TILES + c + 1)
                        k8 = k_rot[:, i].rearrange("p (h d) -> p h d", h=HEADS)
                        nc.gpsimd.tensor_tensor(k8, k8, inv_norm[:, c, 1, :].unsqueeze(2).to_broadcast([P, HEADS, HEAD_DIM]),
                                                ALU.mult).then_inc(sem("ff_k"), 1)
                    ln_pool(pool, LN_FF + L)
                chain.leave(DEPTH)

        @block.scalar
        def _(act):
            act.wait_ge(sem("consts_in"), 48)
            nc.scalar.activation(cond_sig, cond, ACT.Sigmoid).then_inc(sem("cond_sig"), 1)
            act.wait_ge(sem("mod_ready"), 1)
            s4_act_magnitudes(act, 0)
            s4_act_sines(act, 0)
            ln_act(act, LN_A, "lnA_out", hT, one_plus[:, 1:2], mod[:, 0:1])
            with act.Fori(0, S4_LAYERS - 1) as L:
                s4_act_layer(act, L, more=True)
            s4_act_layer(act, S4_LAYERS - 1, more=False)
            if stage != "s4d":
                moe_act(act)
            if stage not in ("s4d", "moe"):
                gla_act(act)
            if stage == "full":
                ff_act(act)
            for b in range(BLOCKS):
                act.wait_ge(sem("result_ps"), b + 1)
                nc.scalar.activation(ff_norm[:, 4 * b:4 * b + 4, :], bank[b][:, :].rearrange("p (a b) -> p a b", a=4), ACT.Copy).then_inc(sem("result"), 1)

        @block.vector
        def _(dve):
            chain = Chain(dve, sem("v_chain"))
            link = chain.link
            V = nc.vector
            V.memset(k_im[:, 0, :], 0.0).then_inc(sem("zero_set"), 1)
            V.memset(decay, 0.0)
            dve.wait_ge(sem("cond_sig"), 1)
            V.tensor_tensor(cond_silu, cond, cond_sig, ALU.mult).then_inc(sem("cond_silu"), 1)
            dve.wait_ge(sem("mod_ps"), 1)
            link(V.tensor_copy(mod, bank[7][:, 0:12]))
            V.tensor_scalar(mod_sign, mod, 0.0, 2.0, ALU.is_ge, ALU.mult)
            V.tensor_scalar(one_plus, mod, 1.0, None, ALU.add)
            link(V.scalar_tensor_tensor(mod_abs, mod, -1.0, mod, ALU.mult, ALU.max))
            link(V.tensor_scalar(mod_abs, mod_abs, 0.25, None, ALU.max))
            V.scalar_tensor_tensor(gate, mod_sign, -1.0, mod_abs, ALU.add, ALU.mult).then_inc(sem("mod_ready"), 1)
            dve.wait_ge(sem("s4_zero_out"), 16)
            dve.wait_ge(sem("s4_consts_in"), 32)
            ln_dve(dve, LN_A, z_tok)
            s4_dve_angles(dve, 0)
            s4_dve_reduce(dve, chain, 0)
            s4_dve_powers(dve, chain, 0)
            with dve.Fori(0, S4_LAYERS - 1) as L:
                chain.body(L, S4_DVE_LINKS)
                s4_dve_layer(dve, chain, L, more=True)
            chain.leave(S4_LAYERS - 1)
            s4_dve_layer(dve, chain, S4_LAYERS - 1, more=False)
            dve.wait_ge(sem("s4_h"), S4_LAYERS * BLOCKS)
            for b in range(BLOCKS):
                sl = slice(512 * b, 512 * b + 512)
                V.scalar_tensor_tensor(xT[:, sl], hT[:, sl], gate[:, 2:3], xT[:, sl], ALU.mult, ALU.add).then_inc(sem("x_s4"), 1)
            if stage != "s4d":
                moe_dve(dve, link)
                moe_dve_blocks(dve, chain)
            if stage not in ("s4d", "moe"):
                gla_dve(dve, link)
            if stage == "full":
                ff_dve(dve, chain)

        @block.tensor
        def _(pe):
            T = nc.tensor
            pe.wait_ge(sem("cond_silu"), 1)
            for i in range(12):
                last = T.matmul(bank[7][:, i:i + 1], wmod_sb[:, i // 6, (i % 6) * P:(i % 6 + 1) * P],
                                cond_silu[:, i // 6:i // 6 + 1], start=True, stop=True)
            last.then_inc(sem("mod_ps"), 1)
            pe.wait_ge(sem("mod_ps"), 1)
            pe.sem_inc(sem("s4_tp_free"), 1)
            pe.wait_ge(sem("x_in"), 16)
            ln_pe_tokens(pe, xT)
            pe.wait_ge(sem("mod_ready"), 1)
            ln_pe_back(pe, LN_A, z_tok)
            pe.wait_ge(sem("s4_consts_in"), 32)
            s4_pe_layer(pe, 0, first=True)
            with pe.Fori(1, S4_LAYERS) as L:
                s4_pe_layer(pe, L, first=False)
            if stage != "s4d":
                moe_pe(pe)
            if stage not in ("s4d", "moe"):
                gla_pe(pe)
            if stage == "full":
                ff_pe(pe)
            final, more = {"s4d": ("x_s4", 0), "moe": ("moe_x", 1), "gla": ("gla_x", 0), "full": ("x_ff", 0)}[stage]
            for b in range(BLOCKS):
                pe.wait_ge(sem(final), b + 1 + more)
                for t in range(4):
                    last = T.transpose(bank[b][:, t * P:(t + 1) * P], xT[:, (4 * b + t) * P:(4 * b + t + 1) * P], ident)
                last.then_inc(sem("result_ps"), 1)


S4_DVE_LINKS = 34
FF_DVE_LINKS = 52


def kernel(**inputs):
    import concourse.bacc as bacc
    from concourse.bass_utils import run_bass_kernel_spmd

    def arr(name):
        return np.ascontiguousarray(inputs[name])

    def modes(a):
        return a.reshape(S4_LAYERS, GROUPS, HG, MODES).transpose(0, 1, 3, 2).reshape(S4_LAYERS, P, HG)

    log_dt = np.repeat(arr("L0_attn_log_dt").reshape(S4_LAYERS, GROUPS, 1, HG), MODES, axis=2)
    prm = np.stack([log_dt.reshape(S4_LAYERS, P, HG)] + [modes(arr("L0_attn_" + n)) for n in ("A_re_log", "A_im", "C_re", "C_im")], axis=2)
    ln_wb = np.stack([arr("L0_attn_ln_w"), arr("L0_attn_ln_b")], axis=1)
    laid = {
        "ident": np.eye(P, dtype=np.float32),
        "cond": np.stack([arr("L0_c").reshape(P), arr("L1_c").reshape(P)], axis=1),
        "wmod": np.stack([arr("L0_wmod"), arr("L1_wmod")], axis=1),
        "xT": arr("L0_attn_x").reshape(N_TOK, P).T,
        "sel": np.stack([np.repeat(s * np.eye(GROUPS, dtype=np.float32), MODES, axis=0) for s in (1, -1)], axis=1),
        "expo": exponents().reshape(1, N_EXP),
        "prm": prm,
        "skip": arr("L0_attn_D_skip").reshape(S4_LAYERS, GROUPS, HG),
        "ln_wb": np.repeat(ln_wb.reshape(S4_LAYERS, 1, 2, P), P, axis=1),
        "w_out": arr("L0_attn_W_out").transpose(0, 2, 1),
        "b_out": arr("L0_attn_b_out").reshape(S4_LAYERS, 2, P).transpose(0, 2, 1),
    }
    order = [2, 0, 1]
    u = np.stack([arr("L0_ffn_U1"), arr("L0_ffn_U2"), arr("L0_ffn_U3")])[order]
    qs, ks = arr("L1_ffn_q_scale"), arr("L1_ffn_k_scale")
    swap = lambda a: np.concatenate([a[:, HEAD_DIM // 2:], a[:, :HEAD_DIM // 2]], axis=1)
    qk_rows = np.stack([qs, swap(qs), ks, swap(ks)], axis=1)
    b1 = arr("L1_ffn_b1")
    cols = np.zeros((DEPTH, P, 9), np.float32)
    for i, (at, size) in enumerate(FF_CHUNKS):
        cols[:, :size, i] = b1[:, at:at + size]
        cols[:, :size, 3 + i] = b1[:, FF + at:FF + at + size]
    cols[:, :, 6], cols[:, :, 7], cols[:, :, 8] = arr("L1_ffn_b2"), arr("L1_ffn_ln_g"), arr("L1_ffn_ln_b")
    wf2 = np.zeros((DEPTH, P, 3, P), np.float32)
    for i, (at, size) in enumerate(FF_CHUNKS):
        wf2[:, :size, i] = arr("L1_ffn_w2")[:, at:at + size]
    wi = arr("L1_attn_Wi").reshape(P, LIN_HEADS, 1, LIN_DIM)
    wo8 = arr("L1_attn_Wo").reshape(LIN_HEADS, LIN_DIM, 1, P)
    laid.update({
        "pw": arr("L0_ffn_P_w").T,
        "u": u.reshape(ROUTERS * EXPERTS, ADDR).T,
        "b2": arr("L0_ffn_b2"),
        "w1": arr("L0_ffn_W1").transpose(2, 0, 1),
        "w2": arr("L0_ffn_W2").reshape(EXPERTS, P, HID_CHUNKS, P).transpose(3, 0, 2, 1),
        "wqf": np.concatenate([arr("L1_attn_Wq"), arr("L1_attn_Wf")], axis=1),
        "wi": np.repeat(wi, LIN_DIM, axis=2).transpose(0, 3, 1, 2).reshape(P, LIN_DIM, P),
        "wo8": np.repeat(wo8, LIN_DIM, axis=2).transpose(0, 2, 1, 3).reshape(P, LIN_DIM, P),
        "mask": window_mask(),
        "tables": rotary_tables().reshape(4, TILES, P, HEAD_DIM).transpose(2, 0, 1, 3),
        "wqkv": arr("L1_ffn_wqkv"),
        "qk_rows": np.repeat(qk_rows.reshape(DEPTH, 1, 4, HEAD_DIM), P, axis=1),
        "wo": arr("L1_ffn_wo").reshape(DEPTH, 4, P, P).transpose(0, 2, 1, 3),
        "wf1": arr("L1_ffn_w1"),
        "wf2": wf2,
        "cols": cols,
    })
    nc = bacc.Bacc("TRN2", target_bir_lowering=False, num_devices=1)
    arrays, dram = {}, {}
    for name, a in laid.items():
        a = np.ascontiguousarray(a)
        arrays[name + "_dram"] = a
        dram[name] = nc.dram_tensor(name + "_dram", a.shape, F32, kind="ExternalInput").ap()
    out = nc.dram_tensor("out_0_dram", (1, N_TOK, P), F32, kind="ExternalOutput").ap()
    program(nc, dram, out, STAGE)
    r = run_bass_kernel_spmd(nc, [arrays], core_ids=[0])
    return r.results[0]["out_0_dram"]
```

```python
import math
from contextlib import ExitStack

import numpy as np

import concourse.bass as bass
from concourse import mybir

STAGE = "full"

F32 = mybir.dt.float32
F32R = mybir.dt.float32r
ALU = mybir.AluOpType
ACT = mybir.ActivationFunctionType
AX = mybir.AxisListType

P = 128
N_TOK = 2048
TILES = N_TOK // P
BLOCKS = N_TOK // 512
EPS_LN = 1e-5

S4_LAYERS = 4
MODES = 32
GROUPS = P // MODES
HG = P // GROUPS
CHUNK = 64
CHUNKS = N_TOK // CHUNK
LOW = 16
HIGH = CHUNK // LOW
NEAR = LOW + HIGH
ONE = LOW - 2
N_EXP = NEAR + CHUNKS
MAGIC = 1.5 * 2.0 ** 23
TWO_PI_1 = 6.28125
TWO_PI_2 = float(np.float32(np.round((2 * math.pi - TWO_PI_1) * 2 ** 21) / 2 ** 21))
TWO_PI_3 = 2 * math.pi - TWO_PI_1 - TWO_PI_2
PIECES = 4
PIECE = HG // PIECES

EXPERTS, TOP, HIDDEN, ADDR = 12, 3, 512, 64
ROUTERS = 3
HID_CHUNKS = HIDDEN // P
AHEAD = 3

LIN_HEADS, LIN_DIM = 16, 8

DEPTH, HEADS, HEAD_DIM, WINDOW = 2, 8, 64, 64
FF = int(P * 4 * 2 / 3)
FF_CHUNKS = [(0, P), (P, P), (2 * P, FF - 2 * P)]
KEYS = WINDOW + P
QK_SCALE = 8.0
MASKED = -1e30


def rotary_tables():
    half = np.arange(0, HEAD_DIM, 2, dtype=np.float32)
    inv = (1.0 / 10000.0 ** (half / HEAD_DIM)).astype(np.float32)
    t = np.arange(N_TOK, dtype=np.float32)
    freqs = (t[:, None] * inv[None, :]).astype(np.float32).astype(np.float64)
    base = (half.astype(np.float64) + 0.4 * HEAD_DIM) / (1.4 * HEAD_DIM)
    power = (t.astype(np.float64) - N_TOK // 2) / float(WINDOW // 2)
    scale = base[None, :] ** power[:, None]
    cos, sin = np.cos(freqs), np.sin(freqs)
    two = lambda a, b: np.concatenate([a, b], axis=1).astype(np.float32)
    return np.stack([two(cos * scale, cos * scale), two(-sin * scale, sin * scale),
                     two(cos / scale, cos / scale), two(-sin / scale, sin / scale)])


def window_mask():
    i = np.arange(P)[:, None] + WINDOW
    j = np.arange(KEYS)[None, :]
    return np.where((i < j) | (i > j + WINDOW), MASKED, 0.0).astype(np.float32)


def exponents():
    e = [LOW - 1 - b for b in range(LOW)] + [LOW * (HIGH - 1 - a) for a in range(HIGH)] + [CHUNK * c for c in range(CHUNKS)]
    return np.array(e, np.float32)


class Chain:

    def __init__(self, engine, semaphore):
        self.engine, self.semaphore = engine, semaphore
        self.n = self.base = self.seen = 0

    def mark(self, instruction):
        instruction.then_inc(self.semaphore, 1)
        self.seen += 1
        self.n = self.base + self.seen

    def wait(self):
        self.engine.wait_ge(self.semaphore, self.n)

    def link(self, instruction):
        self.mark(instruction)
        self.wait()

    def body(self, step, per_step):
        self.start, self.per_step = self.n, per_step
        self.base, self.seen = step * per_step + self.start, 0
        self.n = self.base

    def leave(self, steps):
        assert self.seen == self.per_step, (self.seen, self.per_step)
        self.n = self.base = self.start + steps * self.per_step
        self.seen = 0


def program(nc, dram, out, stage):
    ctx = ExitStack()
    with ctx:
        sems = {}

        def sem(name):
            if name not in sems:
                sems[name] = ctx.enter_context(nc.semaphore(name))
            return sems[name]

        KEPT, MAIN, ARENA = 4608, 32768, 53000
        kept = ctx.enter_context(nc.sbuf_tensor("kept", [P, KEPT], F32))
        with nc.sbuf_tensor("main", [P, MAIN], F32) as main:
            pass
        short = {}
        for name, n in (("w1_high", EXPERTS * HIDDEN), ("w1_low", EXPERTS * HIDDEN),
                        ("w2_high", EXPERTS * HIDDEN), ("w2_low", EXPERTS * HIDDEN),
                        ("x_high", AHEAD * 512), ("x_low", AHEAD * 512),
                        ("hid_high", HID_CHUNKS * 512), ("hid_low", HID_CHUNKS * 512)):
            short[name] = ctx.enter_context(nc.sbuf_tensor(name, [P, n], F32R))
        rest_of_main = MAIN - 4 * EXPERTS * HIDDEN - 2 * (AHEAD + HID_CHUNKS) * 512
        ctx.enter_context(nc.sbuf_tensor("main_end", [P, rest_of_main], F32))
        rest = ctx.enter_context(nc.sbuf_tensor("rest", [P, ARENA - KEPT - MAIN], F32))
        stretches = ((0, KEPT, kept), (KEPT, KEPT + MAIN, main), (KEPT + MAIN, ARENA, rest))
        bank = [ctx.enter_context(nc.psum_tensor(f"bank{i}", [P, 512], F32)) for i in range(8)]

        def shaped(v, dims):
            if len(dims) == 2:
                v = v.rearrange("p (a b) -> p a b", a=dims[0])
            if len(dims) == 3:
                v = v.rearrange("p (a b c) -> p a b c", a=dims[0], b=dims[1])
            return v

        def carve(at, *dims, parts=P):
            n = int(np.prod(dims))
            for start, end, tensor in stretches:
                if start <= at and at + n <= end:
                    return shaped(tensor[0:parts, at - start:at - start + n], dims)
            raise ValueError(f"{dims} at {at} is not within a stretch")

        top = [0]

        def keep(*dims, parts=P):
            n = int(np.prod(dims))
            for start, end, tensor in stretches:
                if top[0] < end < top[0] + n:
                    top[0] = end
            at = top[0]
            top[0] += n
            return carve(at, *dims, parts=parts)

        def keep_both(name, *dims):
            return keep(*dims), shaped(short[name][:, :], dims)

        xT = keep(N_TOK)
        hT = keep(N_TOK)
        ident = keep(P)
        cond = keep(2)
        cond_sig = keep(2)
        cond_silu = keep(2)
        mod = keep(12)
        one_plus = keep(12)
        mod_sign = keep(12)
        mod_abs = keep(12)
        gate = keep(12)
        neg_half = keep(TILES)
        stats = keep(TILES, 6)
        mean_var = keep(TILES, 2)
        rstd = keep(TILES)
        var_eps = keep(TILES)
        eps_col = keep(TILES)
        turn_mark = keep(3)
        pool_mark = keep(1)
        top[0] = phase_base = KEPT

        zu = keep(P, CHUNKS)
        tp = keep(P, CHUNK)
        wmod_sb = tp.rearrange("p a b -> p (a b)")[:, 0:2 * 768].rearrange("p (a b) -> p a b", a=2)
        back = keep(HG, 2, P, parts=CHUNK)
        pow_re = keep(HG, CHUNK)
        pow_im = keep(HG, CHUNK)
        k_re = keep(HG, CHUNK)
        k_im = keep(HG, CHUNK)
        b_re, b_im = (k_re.rearrange("p a b -> p (a b)")[:, i * HG * CHUNKS:(i + 1) * HG * CHUNKS].rearrange("p (h c) -> p h c", c=CHUNKS) for i in (0, 1))
        s_a, s_b = (k_im.rearrange("p a b -> p (a b)")[:, i * HG * CHUNKS:(i + 1) * HG * CHUNKS].rearrange("p (h c) -> p h c", c=CHUNKS) for i in (0, 1))
        z_tok = keep(TILES, P)
        yT = z_tok.rearrange("p a b -> p (a b)")
        states = keep(HG, 2, CHUNKS)
        y_act = states.rearrange("p a b c -> p (a b c)").rearrange("p (i h) -> p i h", h=HG)
        glu_sig = states.rearrange("p a b c -> p (a b c)")
        k_rows = keep(HG, CHUNK, parts=GROUPS)
        prm = keep(5, HG)
        skip = keep(HG, parts=GROUPS)
        ln_wb = keep(2, P)
        w_out = keep(2 * P)
        b_out = keep(2)
        sel = keep(2, GROUPS)
        expo = keep(N_EXP)
        exps = keep(2, HG)
        dta = keep(2, HG)
        theta = keep(HG, N_EXP)
        turns = keep(HG, N_EXP)
        sn = keep(HG, N_EXP)
        cosn = keep(HG, N_EXP)
        anc_re = keep(HG, NEAR)
        anc_im = keep(HG, NEAR)
        mag = keep(HG, NEAR)
        tanh = keep(HG)
        r_chunk = keep(HG)
        small = [keep(HG) for _ in range(12)]
        g_re = keep(HG, CHUNKS)
        g_im = keep(HG, CHUNKS)
        decay = keep(HG, CHUNKS)
        ones = keep(CHUNKS - 1)
        u_re, u_im = (glu_sig[:, i * HG * CHUNKS:(i + 1) * HG * CHUNKS].rearrange("p (h c) -> p h c", c=CHUNKS) for i in (0, 1))

        top[0] = phase_base
        w1_high, w1_high_s = keep_both("w1_high", EXPERTS, HIDDEN)
        w1_low, w1_low_s = keep_both("w1_low", EXPERTS, HIDDEN)
        w2_high, w2_high_s = keep_both("w2_high", EXPERTS, HID_CHUNKS, P)
        w2_low, w2_low_s = keep_both("w2_low", EXPERTS, HID_CHUNKS, P)
        x_high, x_high_s = keep_both("x_high", AHEAD, 512)
        x_low, x_low_s = keep_both("x_low", AHEAD, 512)
        hid_high, hid_high_s = keep_both("hid_high", HID_CHUNKS, 512)
        hid_low, hid_low_s = keep_both("hid_low", HID_CHUNKS, 512)
        y_acc = keep(512)
        y_part = [keep(512) for _ in range(2)]
        weightT = keep(N_TOK, parts=ROUTERS * EXPERTS)
        pw_sb = keep(ADDR)
        u_sb = keep(ROUTERS * EXPERTS, parts=ADDR)
        b2_sb = keep(P, parts=EXPERTS)
        at_shares = top[0]
        share1 = keep(EXPERTS, 512)
        share2 = keep(EXPERTS, 512)
        top[0] = at_shares
        moe_norm = keep(TILES, P)
        addr = keep(N_TOK, parts=ADDR)
        logit = keep(TILES, ROUTERS * EXPERTS)
        weight = keep(TILES, ROUTERS * EXPERTS)
        above = keep(TILES, ROUTERS * EXPERTS)
        equal = keep(TILES, ROUTERS * EXPERTS)
        ranks = keep(TILES, ROUTERS * EXPERTS)
        fresh = keep(TILES, ROUTERS * EXPERTS)
        top8 = keep(TILES * ROUTERS, 8)
        room = keep(TILES * ROUTERS)
        total = keep(TILES * ROUTERS)

        top[0] = phase_base
        gla_norm = keep(TILES, P)
        wqf_sb = keep(2 * P)
        wi_sb = keep(LIN_DIM, P)
        wo8_sb = keep(LIN_DIM, P)
        soft = keep(TILES, 2, P)
        neg_max = keep(TILES, 2)
        soft_sum = keep(TILES, 2)
        qT = keep(N_TOK)
        keepT = keep(N_TOK)
        kT = keep(N_TOK)
        kv = [keep(N_TOK) for _ in range(2)]
        state = [keep(N_TOK) for _ in range(2)]
        read = [keep(N_TOK) for _ in range(2)]

        top[0] = phase_base
        sT = keep(N_TOK)
        nT = sT
        wqkv_sb = keep(3 * HEADS * HEAD_DIM)
        wo_sb = keep(4, P)
        wf1_sb = keep(2 * FF)
        wf2_sb = keep(3, P)
        cols = keep(9)
        qk_rows = keep(4, HEAD_DIM)
        mask_sb = keep(KEYS)
        norms = keep(TILES, 2, HEADS)
        inv_norm = keep(TILES, 2, HEADS)
        row_max = keep(2, HEADS)
        row_scale = keep(2, HEADS)
        row_bias = keep(2, HEADS)
        row_sum = keep(2, HEADS)
        row_inv = keep(2, HEADS)
        at_heads = top[0]
        qhT = keep(4, N_TOK)
        khT = keep(4, N_TOK)
        ff_norm = carve(at_heads, TILES, P)
        v_tok = keep(TILES, 512)
        v_low = keep(TILES, 256, parts=HEAD_DIM)
        at_work = top[0]
        scaled = keep(4, TILES, HEAD_DIM)
        q_rot = keep(2, 512)
        k_rot = keep(2, 512)
        rot_tmp = keep(4, 512)
        squares = keep(4, 512)
        top[0] = at_work
        scores = keep(2 * HEADS, KEYS)
        probs_own = keep(2 * HEADS, P)
        probs_before = keep(2 * HEADS * WINDOW)
        probsT = keep(3 * 4, P)
        oT = keep(4, 512)
        top[0] = at_work + 4 * TILES * HEAD_DIM
        ff_g = keep(2, 512)
        ff_h = keep(3, 512)
        share_d = nc.dram_tensor("share_d", [ROUTERS * EXPERTS, N_TOK], F32, kind="Internal").ap()
        k_pad = nc.dram_tensor("k_pad", [P, 2 * CHUNK], F32, kind="Internal").ap()

        block = ctx.enter_context(nc.Block())

        LN_A, LN_B, LN_C, LN_D = 0, 1 + S4_LAYERS, 2 + S4_LAYERS, 3 + S4_LAYERS
        LN_S4, LN_FF = 1, 4 + S4_LAYERS

        def going_back(n):
            return n if isinstance(n, int) and n == LN_A else n - S4_LAYERS

        def ln_pe_tokens(pe, src, written=None, base=0):
            for b in range(BLOCKS):
                if written is not None:
                    pe.wait_ge(sem(written), base + b + 1)
                for t in range(4):
                    c = 4 * b + t
                    last = nc.tensor.transpose(bank[b][:, t * P:(t + 1) * P], src[:, c * P:(c + 1) * P], ident)
                last.then_inc(sem("ln_tokens"), 1)

        def ln_pe_back(pe, n, normed):
            for b in range(BLOCKS):
                pe.wait_ge(sem("ln_normed"), going_back(n) * BLOCKS + b + 1)
                for t in range(4):
                    c = 4 * b + t
                    last = nc.tensor.transpose(bank[4 + b][:, t * P:(t + 1) * P], normed[:, c, :], ident)
                last.then_inc(sem("ln_back"), 1)

        def ln_dve_stats(dve, n):
            for b in range(BLOCKS):
                dve.wait_ge(sem("ln_tokens"), n * BLOCKS + b + 1)
                for t in range(4):
                    c = 4 * b + t
                    nc.vector.bn_stats(stats[:, c, :], bank[b][:, t * P:(t + 1) * P]).then_inc(sem("ln_stats"), 1)
            dve.wait_ge(sem("ln_stats"), n * TILES + TILES)
            nc.vector.memset(turn_mark[:, 0:1], 0.0)
            for c in range(TILES):
                nc.vector.bn_aggr(mean_var[:, c, :], stats[:, c, :]).then_inc(sem("ln_aggr"), 1)

        def ln_dve(dve, n, normed):
            ln_dve_stats(dve, n)
            dve.wait_ge(sem("ln_rstd"), n + 1)
            for b in range(BLOCKS):
                for t in range(4):
                    c = 4 * b + t
                    last = nc.vector.tensor_scalar(normed[:, c, :], bank[b][:, t * P:(t + 1) * P],
                                                   mean_var[:, c, 0:1], rstd[:, c:c + 1],
                                                   ALU.subtract, ALU.mult)
                    if t == 3:
                        last.then_inc(sem("ln_normed"), 1)

        def ln_pool(pool, n):
            pool.wait_ge(sem("ln_aggr"), n * TILES + TILES)
            nc.gpsimd.tensor_tensor(var_eps, mean_var[:, :, 1], eps_col, ALU.add).then_inc(sem("ln_eps"), 1)
            pool.wait_ge(sem("ln_eps"), n + 1)
            nc.gpsimd.tensor_tensor(rstd, var_eps, neg_half, ALU.pow).then_inc(sem("ln_rstd"), 1)

        def ln_act(act, n, out_name, dst, scale, bias):
            for b in range(BLOCKS):
                act.wait_ge(sem("ln_back"), going_back(n) * BLOCKS + b + 1)
                nc.scalar.activation(dst[:, 512 * b:512 * b + 512], bank[4 + b][:, :], ACT.Identity,
                                     bias=bias, scale=scale).then_inc(sem(out_name), 1)

        CLOSE, FAR = slice(0, NEAR), slice(NEAR, N_EXP)

        def s4_dve_angles(dve, G):
            V = nc.vector
            dve.wait_ge(sem("s4_exps"), G + 1)
            V.scalar_tensor_tensor(dta[:, 0, :], exps[:, 1, :], -1.0, exps[:, 0, :], ALU.mult, ALU.mult)
            V.tensor_tensor(dta[:, 1, :], prm[:, 2, :], exps[:, 0, :], ALU.mult).then_inc(sem("s4_dta"), 1)
            dve.wait_ge(sem("s4_dta"), G + 1)
            V.tensor_tensor(mag, dta[:, 0, :].unsqueeze(2).to_broadcast([P, HG, NEAR]),
                            expo[:, 0:NEAR].unsqueeze(1).to_broadcast([P, HG, NEAR]), ALU.mult).then_inc(sem("s4_marg"), 1)

        def s4_dve_reduce(dve, chain, G):
            V = nc.vector
            link = chain.link
            dve.wait_ge(sem("s4_turns"), G + 1)
            for part in (TWO_PI_1, TWO_PI_2, TWO_PI_3):
                link(V.scalar_tensor_tensor(theta, turns, -part, theta, ALU.mult, ALU.add))
            V.tensor_scalar(theta, theta, 3.1415925, -3.1415925, ALU.min, ALU.max).then_inc(sem("s4_theta"), 1)

        def s4_dve_powers(dve, chain, G):
            V = nc.vector
            link = chain.link
            a_im, c_re, c_im = (prm[:, i, :] for i in (2, 3, 4))
            e_are = exps[:, 1, :]
            dve.wait_ge(sem("s4_sin"), G * 3 + 3)
            dve.wait_ge(sem("s4_mag"), G * 2 + 2)
            s0, s1, s2, s3, s4_, s5, s6, s7, cd_re, c2_im, c2_re, cd_im = small
            V.tensor_copy(s0, theta[:, :, ONE])
            V.tensor_tensor(anc_re, mag, cosn[:, :, 0:NEAR], ALU.mult)
            V.tensor_tensor(anc_im, mag, sn[:, :, 0:NEAR], ALU.mult).then_inc(sem("s4_anchors"), 1)
            dve.wait_ge(sem("s4_anchors"), G + 1)
            link(V.scalar_tensor_tensor(s1, mag[:, :, ONE], 1.0, tanh, ALU.add, ALU.mult))
            link(V.tensor_tensor(s1, s1, cosn[:, :, ONE], ALU.mult))
            link(V.scalar_tensor_tensor(s1, s0, -2.0, s1, ALU.mult, ALU.add))
            e_re, e_im = s1, anc_im[:, :, ONE]
            V.tensor_tensor(s2, e_are, e_are, ALU.mult)
            link(V.tensor_tensor(s3, a_im, a_im, ALU.mult))
            link(V.tensor_tensor(s2, s2, s3, ALU.add))
            link(V.reciprocal(s2, s2))
            V.tensor_tensor(s3, e_im, a_im, ALU.mult)
            V.tensor_tensor(s4_, e_re, e_are, ALU.mult)
            V.tensor_tensor(s5, e_im, e_are, ALU.mult)
            link(V.tensor_tensor(s6, e_re, a_im, ALU.mult))
            V.tensor_tensor(s3, s3, s4_, ALU.subtract)
            link(V.scalar_tensor_tensor(s5, s5, -1.0, s6, ALU.mult, ALU.subtract))
            V.scalar_tensor_tensor(s3, s3, 2.0, s2, ALU.mult, ALU.mult)
            link(V.scalar_tensor_tensor(s5, s5, 2.0, s2, ALU.mult, ALU.mult))
            V.tensor_tensor(s4_, c_re, s3, ALU.mult)
            V.tensor_tensor(s6, c_im, s5, ALU.mult)
            V.tensor_tensor(s7, c_re, s5, ALU.mult)
            link(V.tensor_tensor(s0, c_im, s3, ALU.mult))
            V.tensor_tensor(cd_re, s4_, s6, ALU.subtract).then_inc(sem("s4_cd"), 1)
            link(V.tensor_tensor(cd_im, s7, s0, ALU.add))
            dve.wait_ge(sem("s4_cd"), G + 1)
            w_re, w_im = anc_re[:, :, ONE], anc_im[:, :, ONE]
            V.tensor_tensor(s3, cd_re, w_re, ALU.mult)
            V.tensor_tensor(s4_, cd_im, w_im, ALU.mult)
            V.tensor_tensor(s5, cd_re, w_im, ALU.mult)
            link(V.tensor_tensor(s6, cd_im, w_re, ALU.mult))
            V.tensor_tensor(c2_re, s3, s4_, ALU.subtract)
            V.tensor_tensor(c2_im, s5, s6, ALU.add).then_inc(sem("s4_coef"), 1)
            dve.wait_ge(sem("s4_coef"), G + 1)
            V.tensor_tensor(four(pow_re), hi(anc_re), lo(anc_re), ALU.mult)
            link(V.tensor_tensor(four(k_re), hi(anc_im), lo(anc_im), ALU.mult))
            V.tensor_tensor(pow_re, pow_re, k_re, ALU.subtract).then_inc(sem("s4_pow_re"), 1)
            dve.wait_ge(sem("s4_pow_re"), G + 1)
            V.tensor_tensor(k_re, pow_re, c2_re.unsqueeze(2).to_broadcast([P, HG, CHUNK]), ALU.mult).then_inc(sem("s4_k_re"), 1)

        def s4_dve_layer(dve, chain, L, more):
            V = nc.vector
            link = chain.link
            if more:
                s4_dve_angles(dve, L + 1)
            ln_dve_stats(dve, LN_S4 + L)
            dve.wait_ge(sem("s4_layer_in"), L * 64 + 64)
            V.memset(turn_mark[:, 1:2], 0.0)
            dve.wait_ge(sem("ln_aggr"), (LN_S4 + L + 1) * TILES)
            for c in range(TILES):
                last = V.scalar_tensor_tensor(z_tok[:, c, :], bank[c // 4][:, (c % 4) * P:(c % 4 + 1) * P], mean_var[:, c, 0:1],
                                              ln_wb[:, 0, :], ALU.subtract, ALU.mult)
            link(last)
            dve.wait_ge(sem("ln_rstd"), LN_S4 + L + 1)
            V.memset(turn_mark[:, 2:3], 0.0)
            for c in range(TILES):
                for half in range(2):
                    r = slice(CHUNK * half, CHUNK * half + CHUNK)
                    last = V.scalar_tensor_tensor(zu[0:CHUNK, :, 2 * c + half], z_tok[r, c, :], rstd[r, c:c + 1],
                                                  ln_wb[r, 1, :], ALU.mult, ALU.add)
            last.then_inc(sem("s4_z"), 1)
            if more:
                s4_dve_reduce(dve, chain, L + 1)
            for k in range(PIECES):
                dve.wait_ge(sem("s4_in_ps"), L * PIECES + k + 1)
                last = V.transpose(glu_sig[:, 512 * k:512 * k + 512], bank[k][:, :])
            link(last)
            dve.wait_ge(sem("s4_phases"), L + 1)
            phi_c, phi_s = cosn[:, :, NEAR:N_EXP], sn[:, :, NEAR:N_EXP]
            in_re, in_im = states[:, :, 0, :], states[:, :, 1, :]
            V.tensor_tensor(b_re, in_re, phi_c, ALU.mult)
            V.tensor_tensor(s_a, in_im, phi_s, ALU.mult)
            V.tensor_tensor(b_im, in_im, phi_c, ALU.mult)
            link(V.tensor_tensor(s_b, in_re, phi_s, ALU.mult))
            V.tensor_tensor(b_re, b_re, s_a, ALU.add)
            link(V.tensor_tensor(b_im, b_im, s_b, ALU.subtract))
            flat = lambda t: t.rearrange("p h c -> p (h c)")
            V.tensor_tensor_scan(flat(s_a), flat(decay), flat(b_re), 0.0, ALU.mult, ALU.add)
            link(V.tensor_tensor_scan(flat(s_b), flat(decay), flat(b_im), 0.0, ALU.mult, ALU.add))
            c1 = CHUNKS - 1
            sa_, sb_, gr, gi = (t[:, :, 0:c1] for t in (s_a, s_b, g_re, g_im))
            V.tensor_tensor(b_re[:, :, 0:c1], sa_, gr, ALU.mult)
            V.tensor_tensor(b_im[:, :, 0:c1], sb_, gi, ALU.mult)
            V.tensor_tensor(sa_, sa_, gi, ALU.mult)
            link(V.tensor_tensor(sb_, sb_, gr, ALU.mult))
            V.memset(u_re[:, :, 0], 0.0)
            V.memset(u_im[:, :, 0], 0.0)
            V.tensor_tensor(u_re[:, :, 1:CHUNKS], b_re[:, :, 0:c1], b_im[:, :, 0:c1], ALU.subtract)
            V.scalar_tensor_tensor(u_im[:, :, 1:CHUNKS], sa_, -1.0, sb_, ALU.mult, ALU.subtract).then_inc(sem("s4_u"), 1)
            if more:
                dve.wait_ge(sem("s4_pow_moved"), L * 128 + 128)
                s4_dve_powers(dve, chain, L + 1)
            dve.wait_ge(sem("s4_y"), L * PIECES + PIECES)
            V.transpose(yT, glu_sig).then_inc(sem("s4_yT"), 1)
            for b in range(BLOCKS):
                dve.wait_ge(sem("s4_sig"), L * BLOCKS + b + 1)
                sl = slice(512 * b, 512 * b + 512)
                link(V.scalar_tensor_tensor(glu_sig[:, sl], bank[4 + 2 * (b % 2)][:, :], b_out[:, 0:1],
                                            glu_sig[:, sl], ALU.add, ALU.mult))
                V.tensor_tensor(hT[:, sl], hT[:, sl], glu_sig[:, sl], ALU.add).then_inc(sem("s4_h"), 1)

        def s4_pe_layer(pe, L, first):
            T = nc.tensor
            ln_pe_tokens(pe, hT, "lnA_out" if first else "s4_h", 0 if first else (L - 1) * BLOCKS)
            pe.wait_ge(sem("s4_pow_re"), L + 1)
            pe.wait_ge(sem("s4_pow_im"), L + 1)
            pe.sem_inc(sem("pe_turn"), 1)
            for q in range(HG // 2):
                if q >= 4:
                    pe.wait_ge(sem("s4_back"), L * (HG // 2) + q - 3)
                    pe.sem_inc(sem("pe_turn"), 1)
                for i in range(4):
                    last = T.transpose(bank[4 + q % 4][0:CHUNK, i * P:(i + 1) * P], (pow_re, pow_im)[i % 2][:, 2 * q + i // 2, :], ident)
                last.then_inc(sem("s4_back_ps"), 1)
            pe.wait_ge(sem("s4_k_re"), L + 1)
            pe.wait_ge(sem("s4_k_im"), L + 1)
            for k in range(PIECES):
                pe.wait_ge(sem("s4_back"), L * (HG // 2) + HG // 2 - 3 + k)
                T.matmul(bank[4 + k][0:GROUPS, :], sel[:, 0, :], k_re[:, PIECE * k:PIECE * (k + 1), :], start=True, stop=False)
                T.matmul(bank[4 + k][0:GROUPS, :], sel[:, 1, :], k_im[:, PIECE * k:PIECE * (k + 1), :], start=False, stop=True).then_inc(sem("s4_k_ps"), 1)
            pe.wait_ge(sem("s4_k_rows"), L * (PIECES + 1) + 1)
            pe.wait_ge(sem("s4_layer_in"), L * 64 + 64)
            T.matmul(bank[4][0:GROUPS, 0:HG], sel[:, 0, :], small[8], start=True, stop=False)
            T.matmul(bank[4][0:GROUPS, 0:HG], ident[0:GROUPS, 0:GROUPS], skip, start=False, stop=True).then_inc(sem("s4_k_ps"), 1)
            pe.wait_ge(sem("s4_z"), L + 1)
            pe.sem_inc(sem("pe_turn"), 1)
            for k in range(PIECES):
                for hh in range(PIECE * k, PIECE * (k + 1)):
                    for g in range(GROUPS):
                        last = T.matmul(bank[k][32 * g:32 * g + 32, 2 * MODES * (hh % PIECE):2 * MODES * (hh % PIECE + 1)],
                                        zu[0:CHUNK, HG * g + hh, :], back[:, hh, :, 32 * g:32 * g + 32], start=True, stop=True)
                last.then_inc(sem("s4_in_ps"), 1)
            pe.wait_ge(sem("s4_toep_in"), L * 16 * PIECES + 16 * PIECES)
            pe.wait_ge(sem("s4_pow_moved"), L * 128 + 128)
            pe.wait_ge(sem("s4_u_moved"), L * 128 + 128)
            pe.wait_ge(sem("s4_k_rows"), (L + 1) * (PIECES + 1))
            for k in range(PIECES):
                for hh in range(PIECE * k, PIECE * (k + 1)):
                    for g in range(GROUPS):
                        last = T.matmul(bank[4 + k][32 * g:32 * g + 32, CHUNK * (hh % PIECE):CHUNK * (hh % PIECE + 1)],
                                        zu[:, HG * g + hh, :], tp[:, HG * g + hh, :], start=True, stop=True)
                last.then_inc(sem("s4_y_ps"), 1)
            pe.wait_ge(sem("s4_y_ps"), (L + 1) * PIECES)
            pe.sem_inc(sem("s4_tp_free"), 1)
            pe.wait_ge(sem("s4_yT"), L + 1)
            for b in range(BLOCKS):
                if b >= 2:
                    pe.wait_ge(sem("s4_h"), L * BLOCKS + b - 1)
                rhs = yT.rearrange("p (i c) -> p c i", c=CHUNKS)[:, 8 * b:8 * b + 8, :]
                for k in range(2):
                    last = T.matmul(bank[4 + 2 * (b % 2) + k][:, :], w_out[:, k * P:(k + 1) * P], rhs, start=True, stop=True)
                last.then_inc(sem("s4_glu_ps"), 1)

        def s4_act_magnitudes(act, G):
            A = nc.scalar
            act.wait_ge(sem("s4_prm_in"), G * 16 + 16)
            A.activation(exps, prm[:, 0:2, :], ACT.Exp).then_inc(sem("s4_exps"), 1)
            act.wait_ge(sem("s4_dta"), G + 1)
            A.activation(tanh, dta[:, 0, :], ACT.Tanh, scale=0.5)
            act.wait_ge(sem("s4_marg"), G + 1)
            A.activation(mag, mag, ACT.Exp).then_inc(sem("s4_mag"), 1)

        def s4_act_decay(act, G):
            nc.scalar.activation(r_chunk, dta[:, 0, :], ACT.Exp, scale=float(CHUNK)).then_inc(sem("s4_mag"), 1)

        def s4_act_sines(act, G, which, done):
            A = nc.scalar
            act.wait_ge(sem("s4_theta"), G + 1)
            A.activation(sn[:, :, which], theta[:, :, which], ACT.Sin)
            A.activation(turns[:, :, which], theta[:, :, which], ACT.Sin, scale=0.5).then_inc(sem(done), 1)
            act.wait_ge(sem(done), G * 3 + 1)
            A.activation(theta[:, :, which], turns[:, :, which], ACT.Square).then_inc(sem(done), 1)
            act.wait_ge(sem(done), G * 3 + 2)
            A.activation(cosn[:, :, which], theta[:, :, which], ACT.Copy, scale=-2.0, bias=1.0).then_inc(sem(done), 1)

        def s4_act_layer(act, L, more):
            A = nc.scalar
            if more:
                s4_act_magnitudes(act, L + 1)
            for q in range(HG // 2):
                act.wait_ge(sem("s4_back_ps"), L * (HG // 2) + q + 1)
                A.activation(back[:, 2 * q:2 * q + 2], bank[4 + q % 4][0:CHUNK, :].rearrange("p (a b c) -> p a b c", a=2, b=2), ACT.Copy).then_inc(sem("s4_back"), 1)
            for k in range(PIECES):
                act.wait_ge(sem("s4_k_ps"), L * (PIECES + 1) + k + 1)
                src = bank[4 + k][0:GROUPS, :].rearrange("p (a b) -> p a b", a=PIECE)
                A.activation(k_rows[:, PIECE * k:PIECE * (k + 1), 0:CHUNK - 1], src[:, :, 1:CHUNK], ACT.Copy).then_inc(sem("s4_k_rows"), 1)
            act.wait_ge(sem("s4_k_ps"), (L + 1) * (PIECES + 1))
            A.activation(k_rows[:, :, CHUNK - 1], bank[4][0:GROUPS, 0:HG], ACT.Copy).then_inc(sem("s4_k_rows"), 1)
            if more:
                act.wait_ge(sem("s4_phases"), L + 1)
                s4_act_decay(act, L + 1)
            if more:
                s4_act_sines(act, L + 1, CLOSE, "s4_sin")
            act.wait_ge(sem("s4_u"), L + 1)
            if more:
                s4_act_sines(act, L + 1, FAR, "s4_sin_far")
            for k in range(PIECES):
                act.wait_ge(sem("s4_y_ps"), L * PIECES + k + 1)
                A.activation(y_act.rearrange("p i h -> p h i")[:, PIECE * k:PIECE * (k + 1), :],
                             bank[4 + k][:, :].rearrange("p (h i) -> p h i", i=CHUNK)[:, :, ::-1],
                             ACT.Gelu_apprx_tanh).then_inc(sem("s4_y"), 1)
            act.wait_ge(sem("s4_yT"), L + 1)
            for b in range(BLOCKS):
                act.wait_ge(sem("s4_glu_ps"), L * BLOCKS + b + 1)
                A.activation(glu_sig[:, 512 * b:512 * b + 512], bank[5 + 2 * (b % 2)][:, :],
                             ACT.Sigmoid, bias=b_out[:, 1:2]).then_inc(sem("s4_sig"), 1)

        def s4_pool_powers(pool, chain, G):
            G_ = nc.gpsimd
            pool.wait_ge(sem("s4_anchors"), G + 1)
            G_.tensor_tensor(four(pow_im), hi(anc_re), lo(anc_im), ALU.mult)
            chain.link(G_.tensor_tensor(four(k_im), hi(anc_im), lo(anc_re), ALU.mult))
            G_.tensor_tensor(pow_im, pow_im, k_im, ALU.add).then_inc(sem("s4_pow_im"), 1)
            pool.wait_ge(sem("s4_coef"), G + 1)
            pool.wait_ge(sem("s4_pow_im"), G + 1)
            G_.tensor_tensor(k_im, pow_im, small[9].unsqueeze(2).to_broadcast([P, HG, CHUNK]), ALU.mult).then_inc(sem("s4_k_im"), 1)
            pool.wait_ge(sem("s4_sin_far"), G * 3 + 3)
            cc = [P, HG, CHUNKS]
            phi_c, phi_s = cosn[:, :, NEAR:N_EXP], sn[:, :, NEAR:N_EXP]
            c2r, c2i = small[10].unsqueeze(2).to_broadcast(cc), small[9].unsqueeze(2).to_broadcast(cc)
            G_.tensor_tensor(decay[:, :, 1:CHUNKS], r_chunk.unsqueeze(2).to_broadcast([P, HG, CHUNKS - 1]),
                             ones.unsqueeze(1).to_broadcast([P, HG, CHUNKS - 1]), ALU.mult)
            G_.tensor_tensor(g_re, phi_c, c2r, ALU.mult)
            G_.tensor_tensor(g_im, phi_c, c2i, ALU.mult)
            G_.tensor_tensor(g_x, phi_s, c2i, ALU.mult)
            chain.link(G_.tensor_tensor(g_y, phi_s, c2r, ALU.mult))
            G_.tensor_tensor(g_re, g_re, g_x, ALU.subtract)
            G_.tensor_tensor(g_im, g_im, g_y, ALU.add).then_inc(sem("s4_phases"), 1)

        def s4_pool_angles(pool, chain, G):
            G_ = nc.gpsimd
            wide = [P, HG, N_EXP]

            def link(instruction):
                chain.link(instruction)
                pool.sem_inc(sem("pool_turn"), 1)

            pool.wait_ge(sem("s4_dta"), G + 1)
            link(G_.tensor_tensor(theta, dta[:, 1, :].unsqueeze(2).to_broadcast(wide),
                                  expo.unsqueeze(1).to_broadcast(wide), ALU.mult))
            link(G_.tensor_scalar(turns, theta, 1.0 / (2 * math.pi), MAGIC, ALU.mult, ALU.add))
            G_.tensor_scalar(turns, turns, MAGIC, None, ALU.subtract).then_inc(sem("s4_turns"), 1)

        lo = lambda t: t[:, :, 0:LOW].unsqueeze(2).to_broadcast([P, HG, HIGH, LOW])
        hi = lambda t: t[:, :, LOW:NEAR].unsqueeze(3).to_broadcast([P, HG, HIGH, LOW])
        four = lambda t: t.rearrange("p h (a b) -> p h a b", a=HIGH)
        g_x, g_y = (y.rearrange("p a b -> p (a b)")[:, 0:HG * CHUNKS].rearrange("p (h c) -> p h c", c=CHUNKS) for y in (theta, turns))

        def s4_sp_layer(sp, L, first, more):
            whole = (lambda x: x) if isinstance(L, int) else sp.snap
            one, rows, k_out = whole(L + 1), whole((L + 1) * (PIECES + 1)), whole(L * 16 + 16)
            toep_in, h = whole(L * 16 * PIECES), L if first else whole(L * BLOCKS)

            def turn():
                sp.sem_inc(sem("sp_turn"), 1)

            if more:
                sp.wait_ge(sem("s4_coef"), one)
                turn()
                sp.dma_start(prm, dram["prm"][L + 1]).then_inc(sem("s4_prm_in"), 16)
            if not first:
                sp.wait_ge(sem("s4_h"), h)
                turn()
            for dst, name in ((skip, "skip"), (ln_wb, "ln_wb"), (w_out, "w_out"), (b_out, "b_out")):
                sp.dma_start(dst, dram[name][L]).then_inc(sem("s4_layer_in"), 16)
            for name in ("s4_tp_free", "s4_pow_re", "s4_pow_im"):
                sp.wait_ge(sem(name), one)
                turn()
            for ri, src in ((0, pow_re), (1, pow_im)):
                for g in range(GROUPS):
                    at = CHUNK + MODES * ri
                    sp.dma_start(tp[at:at + MODES, HG * g:HG * (g + 1), :], src[32 * g:32 * g + 32]).then_inc(sem("s4_pow_moved"), 16)
            sp.wait_ge(sem("s4_k_rows"), rows)
            turn()
            sp.dma_start(k_pad[:, 0:CHUNK].rearrange("(g h) m -> g h m", g=GROUPS), k_rows).then_inc(sem("s4_k_out"), 16)
            sp.wait_ge(sem("s4_k_out"), k_out)
            turn()
            for g in range(GROUPS):
                src = bass.AP(tensor=k_pad.tensor, offset=g * HG * 2 * CHUNK, ap=[[1, CHUNK], [2 * CHUNK, HG], [1, CHUNK]])
                sp.dma_start(tp[0:CHUNK, HG * g:HG * (g + 1), :], src).then_inc(sem("s4_toep_in"), 16)
            sp.wait_ge(sem("s4_u"), one)
            turn()
            for ri, src in ((0, u_re), (1, u_im)):
                for g in range(GROUPS):
                    at = CHUNK + MODES * ri
                    sp.dma_start(zu[at:at + MODES, HG * g:HG * (g + 1), :], src[32 * g:32 * g + 32]).then_inc(sem("s4_u_moved"), 16)

        def moe_act(act):
            A = nc.scalar
            ln_act(act, LN_B, "lnB_out", hT, one_plus[:, 4:5], mod[:, 3:4])
            act.wait_ge(sem("moe_w1_in"), 16)
            for e in range(EXPERTS):
                A.activation(w1_high_s[:, e, :], w1_low[:, e, :], ACT.Copy).then_inc(sem("moe_w1_high"), 1)
            act.wait_ge(sem("moe_shifted"), 1)
            A.activation(weight, logit, ACT.Exp).then_inc(sem("moe_exp"), 1)
            act.wait_ge(sem("moe_w2_in"), 16)
            for e in range(EXPERTS):
                A.activation(w2_high_s[:, e], w2_low[:, e], ACT.Copy).then_inc(sem("moe_w2_high"), 1)

            def high(b, e):
                act.wait_ge(sem("moe_raw"), b * EXPERTS + e + 1)
                A.activation(x_high_s[:, e % AHEAD, :], x_low[:, e % AHEAD, :], ACT.Copy).then_inc(sem("moe_x_high"), 1)

            def block_of_tokens(b, more):
                for e in range(AHEAD, EXPERTS):
                    high(b, e)
                for m in range(HID_CHUNKS):
                    act.wait_ge(sem("moe_h"), b * HID_CHUNKS + m + 1)
                    A.activation(hid_low[:, m, :], bank[m][:, :], ACT.Gelu)
                    A.activation(hid_high_s[:, m, :], bank[m][:, :], ACT.Gelu).then_inc(sem("moe_hid_high"), 1)
                if more:
                    for e in range(AHEAD):
                        high(b + 1, e)

            for e in range(AHEAD):
                high(0, e)
            with act.Fori(0, BLOCKS - 1) as b:
                block_of_tokens(b, more=True)
            block_of_tokens(BLOCKS - 1, more=False)

        def moe_dve(dve, link):
            V = nc.vector
            ln_dve(dve, LN_B, moe_norm)
            link(V.memset(fresh, 1.0))
            g3 = lambda t: t.rearrange("p c (r e) -> p (c r) e", r=ROUTERS)
            flat = lambda t: t.rearrange("p c e -> p (c e)")
            groups = TILES * ROUTERS
            wide = [P, groups, EXPERTS]
            V.memset(g3(fresh)[:, :, 0:1], 0.0)
            for b in range(BLOCKS):
                dve.wait_ge(sem("moe_addr_ps"), b + 1)
                V.tensor_copy(addr[:, 512 * b:512 * b + 512], bank[b][0:ADDR, :]).then_inc(sem("moe_addr"), 1)
            half = TILES // 2
            for i in range(2):
                dve.wait_ge(sem("moe_logit_ps"), i + 1)
                link(V.tensor_copy(logit[:, half * i:half * (i + 1), :],
                                   bank[4 + i][:, 0:half * 36].rearrange("p (c e) -> p c e", e=36)))
            for k in range(groups):
                last = V.max(top8[:, k, :], g3(logit)[:, k, :])
            link(last)
            third = top8[:, :, 2:3].to_broadcast(wide)
            V.tensor_tensor(g3(above), g3(logit), third, ALU.is_gt)
            link(V.tensor_tensor(g3(equal), g3(logit), third, ALU.is_equal))
            V.tensor_tensor_scan(flat(ranks), flat(fresh), flat(equal), 0.0, ALU.mult, ALU.add)
            V.tensor_tensor(g3(logit), g3(logit), top8[:, :, 0:1].to_broadcast(wide), ALU.subtract).then_inc(sem("moe_shifted"), 1)
            link(V.tensor_reduce(room, g3(above), AX.X, ALU.add))
            link(V.tensor_scalar(room, room, -1.0, float(TOP), ALU.mult, ALU.add))
            link(V.tensor_tensor(g3(ranks), g3(ranks), room.unsqueeze(2).to_broadcast(wide), ALU.is_le))
            link(V.tensor_tensor(equal, equal, ranks, ALU.mult))
            link(V.tensor_tensor(above, above, equal, ALU.add))
            dve.wait_ge(sem("moe_exp"), 1)
            link(V.tensor_tensor(weight, weight, above, ALU.mult))
            link(V.tensor_reduce(total, g3(weight), AX.X, ALU.add))
            link(V.reciprocal(total, total))
            V.tensor_tensor(g3(weight), g3(weight), total.unsqueeze(2).to_broadcast(wide), ALU.mult).then_inc(sem("moe_weight"), 1)
            for b in range(BLOCKS):
                dve.wait_ge(sem("moe_wT_ps"), b + 1)
                V.tensor_copy(weightT[:, 512 * b:512 * b + 512], bank[b][0:36, :]).then_inc(sem("moe_wT"), 1)
            dve.wait_ge(sem("lnB_out"), BLOCKS)

        def moe_dve_blocks(dve, chain):
            V = nc.vector
            for name, n in (("moe_share_free1", 1), ("moe_share_free2", 1), ("moe_y_read", 2), ("moe_x", 1)):
                dve.sem_inc(sem(name), n)

            def raw(b, e):
                n = b * EXPERTS + e
                if e == 0:
                    dve.wait_ge(sem("moe_share_in1"), b * 16 + 16)
                if not isinstance(n, int) or n >= AHEAD:
                    dve.wait_ge(sem("moe_x_used"), n - AHEAD + 1)
                cols = slice(512 * b, 512 * b + 512) if isinstance(b, int) else bass.ts(b, 512)
                V.tensor_tensor(x_low[:, e % AHEAD, :], hT[:, cols], share1[:, e, :], ALU.mult).then_inc(sem("moe_raw"), 1)

            def low(b, e):
                dve.wait_ge(sem("moe_x_high"), b * EXPERTS + e + 1)
                V.tensor_tensor(x_low_s[:, e % AHEAD, :], x_low[:, e % AHEAD, :], x_high_s[:, e % AHEAD, :],
                                ALU.subtract).then_inc(sem("moe_x_low"), 1)

            def block_of_tokens(b, more):
                for e in range(AHEAD, EXPERTS):
                    raw(b, e)
                    low(b, e - 1)
                low(b, EXPERTS - 1)
                dve.wait_ge(sem("moe_x_low"), (b + 1) * EXPERTS)
                dve.sem_inc(sem("moe_share_free1"), 1)
                for m in range(HID_CHUNKS):
                    dve.wait_ge(sem("moe_hid_high"), b * HID_CHUNKS + m + 1)
                    V.tensor_tensor(hid_low_s[:, m, :], hid_low[:, m, :], hid_high_s[:, m, :],
                                    ALU.subtract).then_inc(sem("moe_hid_low"), 1)
                dve.wait_ge(sem("moe_share_in2"), b * 16 + 16)
                for e in range(EXPERTS):
                    dve.wait_ge(sem("moe_y_ps"), b * EXPERTS + e + 1)
                    part = y_acc if e == 0 else y_part[e % 2]
                    V.tensor_tensor(part, bank[4 + e % 2][:, :], share2[:, e, :], ALU.mult).then_inc(sem("moe_y_read"), 1)
                    if e:
                        dve.wait_ge(sem("moe_y_read"), b * EXPERTS + e + 3)
                        if e > 1:
                            chain.wait()
                        chain.mark(V.tensor_tensor(y_acc, y_acc, part, ALU.add))
                    if more and e >= EXPERTS - AHEAD - 1 and e < EXPERTS - 1:
                        k = e - (EXPERTS - AHEAD - 1)
                        raw(b + 1, k)
                        if k:
                            low(b + 1, k - 1)
                dve.sem_inc(sem("moe_share_free2"), 1)
                chain.wait()
                dve.wait_ge(sem("moe_b2_ps"), b + 1)
                chain.link(V.tensor_tensor(y_acc, y_acc, bank[6][:, :], ALU.add))
                cols = slice(512 * b, 512 * b + 512) if isinstance(b, int) else bass.ts(b, 512)
                V.scalar_tensor_tensor(xT[:, cols], y_acc, gate[:, 5:6], xT[:, cols],
                                       ALU.mult, ALU.add).then_inc(sem("moe_x"), 1)
                dve.wait_ge(sem("moe_x"), b + 2)

            raw(0, 0)
            for e in range(1, AHEAD):
                raw(0, e)
                low(0, e - 1)
            with dve.Fori(0, BLOCKS - 1) as b:
                chain.body(b, EXPERTS)
                block_of_tokens(b, more=True)
            chain.leave(BLOCKS - 1)
            block_of_tokens(BLOCKS - 1, more=False)

        def moe_pe(pe):
            T = nc.tensor
            pe.wait_ge(sem("x_s4"), BLOCKS)
            ln_pe_tokens(pe, xT)
            ln_pe_back(pe, LN_B, moe_norm)
            pe.wait_ge(sem("moe_consts_in"), 48)
            for b in range(BLOCKS):
                pe.wait_ge(sem("lnB_out"), b + 1)
                T.matmul(bank[b][0:ADDR, :], pw_sb, hT[:, 512 * b:512 * b + 512], start=True, stop=True).then_inc(sem("moe_addr_ps"), 1)
            half = TILES // 2
            for c in range(TILES):
                pe.wait_ge(sem("moe_addr"), c // 4 + 1)
                last = T.matmul(bank[4 + c // half][:, 36 * (c % half):36 * (c % half) + 36],
                                addr[:, c * P:(c + 1) * P], u_sb, start=True, stop=True)
                if c % half == half - 1:
                    last.then_inc(sem("moe_logit_ps"), 1)
            pe.wait_ge(sem("moe_weight"), 1)
            for c in range(TILES):
                last = T.transpose(bank[c // 4][0:36, (c % 4) * P:(c % 4 + 1) * P], weight[:, c, :], ident)
                if c % 4 == 3:
                    last.then_inc(sem("moe_wT_ps"), 1)
            pe.wait_ge(sem("moe_wT"), BLOCKS)
            def thrice(dst, w_large, w_small, x_large, x_small, first, last):
                T.matmul(dst, w_small, x_large, start=first, stop=False)
                T.matmul(dst, w_large, x_small, start=False, stop=False)
                return T.matmul(dst, w_large, x_large, start=False, stop=last)

            pe.wait_ge(sem("moe_w1_low"), EXPERTS)
            with pe.Fori(0, BLOCKS) as b:
                for e in range(EXPERTS):
                    pe.wait_ge(sem("moe_x_low"), b * EXPERTS + e + 1)
                    for m in range(HID_CHUNKS):
                        cols = slice(m * P, (m + 1) * P)
                        last = thrice(bank[m][:, :], w1_high_s[:, e, cols], w1_low_s[:, e, cols],
                                      x_high_s[:, e % AHEAD, :], x_low_s[:, e % AHEAD, :], e == 0, e == EXPERTS - 1)
                        if e == EXPERTS - 1:
                            last.then_inc(sem("moe_h"), 1)
                    if e == EXPERTS - 1:
                        pe.wait_ge(sem("moe_h"), b * HID_CHUNKS + HID_CHUNKS)
                        pe.sem_inc(sem("moe_x_used"), 1)
                    else:
                        last.then_inc(sem("moe_x_used"), 1)
                pe.wait_ge(sem("moe_x"), b + 1)
                T.matmul(bank[6][:, :], b2_sb, weightT[0:EXPERTS, bass.ts(b, 512)], start=True, stop=True).then_inc(sem("moe_b2_ps"), 1)
                pe.wait_ge(sem("moe_w2_low"), EXPERTS)

                def output(e, m):
                    return thrice(bank[4 + e % 2][:, :], w2_high_s[:, e, m, :], w2_low_s[:, e, m, :],
                                  hid_high_s[:, m, :], hid_low_s[:, m, :], m == 0, m == HID_CHUNKS - 1)

                pe.wait_ge(sem("moe_y_read"), b * EXPERTS + 2)
                for m in range(HID_CHUNKS):
                    pe.wait_ge(sem("moe_hid_low"), b * HID_CHUNKS + m + 1)
                    for e in range(2):
                        last = output(e, m)
                        if m == HID_CHUNKS - 1:
                            last.then_inc(sem("moe_y_ps"), 1)
                for e in range(2, EXPERTS):
                    pe.wait_ge(sem("moe_y_read"), b * EXPERTS + e + 1)
                    for m in range(HID_CHUNKS):
                        last = output(e, m)
                    last.then_inc(sem("moe_y_ps"), 1)

        def gla_act(act):
            A = nc.scalar
            ln_act(act, LN_C, "lnC_out", hT, one_plus[:, 7:8], mod[:, 6:7])
            for k in range(8):
                act.wait_ge(sem("gla_max"), k + 1)
                for i in range(4):
                    c, j = 2 * k + i // 2, i % 2
                    last = A.activation(soft[:, c, j, :], bank[k][:, i * P:(i + 1) * P], ACT.Exp,
                                        bias=neg_max[:, c, j:j + 1], accum_out=soft_sum[:, c, j:j + 1])
                last.then_inc(sem("gla_exp"), 1)
            for b in range(BLOCKS):
                act.wait_ge(sem("gla_T_ps"), 2 * b + 2)
                sl = slice(512 * b, 512 * b + 512)
                A.activation(keepT[:, sl], bank[2 * b % 8 + 1][:, :], ACT.Copy)
                A.activation(kT[:, sl], bank[2 * b % 8 + 1][:, :], ACT.Copy, scale=-1.0, bias=1.0).then_inc(sem("gla_k"), 1)

        def gla_dve(dve, link):
            V = nc.vector
            ln_dve(dve, LN_C, gla_norm)
            for k in range(8):
                dve.wait_ge(sem("gla_logit_ps"), k + 1)
                V.tensor_reduce(neg_max[:, 2 * k:2 * k + 2, :].rearrange("p c j -> p (c j)"),
                                bank[k][:, :].rearrange("p (i d) -> p i d", i=4), AX.X, ALU.max,
                                negate=True).then_inc(sem("gla_max"), 1)
            for k in range(8):
                dve.wait_ge(sem("gla_exp"), k + 1)
                two = slice(2 * k, 2 * k + 2)
                link(V.reciprocal(soft_sum[:, two, :], soft_sum[:, two, :]))
                link(V.tensor_scalar(soft_sum[:, two, 0:1], soft_sum[:, two, 0:1], LIN_DIM ** -0.5, None, ALU.mult))
                V.tensor_tensor(soft[:, two].rearrange("p c j d -> p (c j) d"), soft[:, two].rearrange("p c j d -> p (c j) d"),
                                soft_sum[:, two, :].rearrange("p c j -> p (c j)").unsqueeze(2).to_broadcast([P, 4, P]),
                                ALU.mult).then_inc(sem("gla_soft"), 1)
            for b in range(BLOCKS):
                dve.wait_ge(sem("gla_T_ps"), 2 * b + 1)
                V.tensor_copy(qT[:, 512 * b:512 * b + 512], bank[2 * b % 8][:, :]).then_inc(sem("gla_q"), 1)
            dve.wait_ge(sem("gla_k"), BLOCKS)
            for v in range(LIN_DIM):
                i = v % 2
                for b in range(BLOCKS):
                    dve.wait_ge(sem("gla_v_ps"), BLOCKS * v + b + 1)
                    sl = slice(512 * b, 512 * b + 512)
                    V.tensor_tensor(kv[i][:, sl], bank[b][:, :], kT[:, sl], ALU.mult).then_inc(sem("gla_kv"), 1)
                dve.wait_ge(sem("gla_kv"), BLOCKS * (v + 1))
                if v >= 2:
                    dve.wait_ge(sem("gla_read"), v - 1)
                V.tensor_tensor_scan(state[i], keepT, kv[i], 0.0, ALU.mult, ALU.add).then_inc(sem("gla_state"), 1)
            for b in range(BLOCKS):
                dve.wait_ge(sem("gla_o_ps"), b + 1)
                sl = slice(512 * b, 512 * b + 512)
                V.scalar_tensor_tensor(xT[:, sl], bank[4 + b][:, :], gate[:, 8:9], xT[:, sl], ALU.mult, ALU.add).then_inc(sem("gla_x"), 1)

        def gla_pe(pe):
            T = nc.tensor
            pe.wait_ge(sem("moe_x"), BLOCKS + 1)
            ln_pe_tokens(pe, xT)
            ln_pe_back(pe, LN_C, gla_norm)
            pe.wait_ge(sem("gla_w_in"), 48)
            pe.wait_ge(sem("lnC_out"), BLOCKS)
            for c in range(TILES):
                last = T.matmul(bank[c // 2][:, 256 * (c % 2):256 * (c % 2) + 256], hT[:, c * P:(c + 1) * P], wqf_sb, start=True, stop=True)
                if c % 2:
                    last.then_inc(sem("gla_logit_ps"), 1)
            pe.wait_ge(sem("gla_exp"), 8)
            for b in range(BLOCKS):
                pe.wait_ge(sem("gla_soft"), 2 * b + 2)
                for j in range(2):
                    for t in range(4):
                        last = T.transpose(bank[2 * b + j][:, t * P:(t + 1) * P], soft[:, 4 * b + t, j, :], ident)
                    last.then_inc(sem("gla_T_ps"), 1)

            def values(v):
                for b in range(BLOCKS):
                    if v:
                        pe.wait_ge(sem("gla_kv"), BLOCKS * (v - 1) + b + 1)
                    T.matmul(bank[b][:, :], wi_sb[:, v, :], hT[:, 512 * b:512 * b + 512], start=True, stop=True).then_inc(sem("gla_v_ps"), 1)

            pe.wait_ge(sem("gla_q"), BLOCKS)
            pe.wait_ge(sem("gla_k"), BLOCKS)
            values(0)
            for v in range(LIN_DIM):
                if v + 1 < LIN_DIM:
                    values(v + 1)
                pe.wait_ge(sem("gla_read"), v + 1)
                for b in range(BLOCKS):
                    last = T.matmul(bank[4 + b][:, :], wo8_sb[:, v, :], read[v % 2][:, 512 * b:512 * b + 512],
                                    start=(v == 0), stop=(v == LIN_DIM - 1))
                    if v == LIN_DIM - 1:
                        last.then_inc(sem("gla_o_ps"), 1)
                if v < LIN_DIM - 1:
                    last.then_inc(sem("gla_read_used"), 1)

        PROJECTED = ((0, 1, 2), (3, 6, 7))

        def ff_act(act):
            A = nc.scalar
            ln_act(act, LN_D, "lnD_out", hT, one_plus[:, 10:11], mod[:, 9:10])
            with act.Fori(0, DEPTH) as L:
                for c in range(TILES + 1):
                    if c:
                        act.wait_ge(sem("ff_norm2"), L * TILES + c)
                        A.activation(norms[:, c - 1], norms[:, c - 1], ACT.Sqrt).then_inc(sem("ff_norm"), 1)
                    if c < TILES:
                        q, k, v = PROJECTED[c % 2]
                        act.wait_ge(sem("ff_qk_ps"), L * TILES + c + 1)
                        if c >= 2:
                            act.wait_ge(sem("ff_norm2"), L * TILES + c - 1)
                        A.activation(squares[:, 2 * (c % 2)], bank[q][:, :], ACT.Square).then_inc(sem("ff_sq"), 1)
                        A.activation(squares[:, 2 * (c % 2) + 1], bank[k][:, :], ACT.Square).then_inc(sem("ff_sq"), 1)
                        act.wait_ge(sem("ff_v_ps"), L * TILES + c + 1)
                        A.activation(v_low[:, c, :].rearrange("p (a b) -> p a b", a=4),
                                     bank[v][HEAD_DIM:P, :].rearrange("p (a b) -> p a b", a=4)[:, :, 0:HEAD_DIM], ACT.Copy)
                        A.activation(v_tok[:, c, :], bank[v][:, :], ACT.Copy).then_inc(sem("ff_v"), 1)
                    if c:
                        for name, dst, bk in (("q", qhT, 4), ("k", khT, 5)):
                            act.wait_ge(sem(f"ff_{name}T_ps"), L * TILES + c)
                            A.activation(dst[:, :, (c - 1) * P:c * P], bank[bk][:, :].rearrange("p (j t) -> p j t", j=4),
                                         ACT.Copy).then_inc(sem(f"ff_{name}T"), 1)

                def exponentials(c):
                    act.wait_ge(sem("at_bias"), L * TILES + c + 1)
                    first = WINDOW if c == 0 else 0
                    for h in range(HEADS):
                        i = HEADS * (c % 2) + h
                        A.activation(scores[:, i, first:KEYS], scores[:, i, first:KEYS], ACT.Exp,
                                     scale=row_scale[:, c % 2, h:h + 1], bias=row_bias[:, c % 2, h:h + 1],
                                     accum_out=row_sum[:, c % 2, h:h + 1]).then_inc(sem("at_exp"), 1)

                exponentials(0)
                for c in range(TILES):
                    if c + 1 < TILES:
                        exponentials(c + 1)
                    act.wait_ge(sem("at_PT_ps"), L * 3 * TILES + 3 * c + 3)
                    A.activation(probsT[:, 4:8, :], bank[4][:, :].rearrange("p (a b) -> p a b", a=4), ACT.Copy).then_inc(sem("at_PT_act"), 1)
                    act.wait_ge(sem("at_o_ps"), L * TILES + c + 1)
                    if c % 4 == 0 and c:
                        act.wait_ge(sem("at_wo_ps"), L * BLOCKS + c // 4)
                    A.activation(oT[0:HEAD_DIM, :, (c % 4) * P:(c % 4 + 1) * P], bank[6][0:HEAD_DIM, :].rearrange("p (j t) -> p j t", j=4),
                                 ACT.Copy).then_inc(sem("at_o_even"), 1)
                for b in range(BLOCKS):
                    act.wait_ge(sem("ln_back"), (LN_FF - S4_LAYERS) * BLOCKS + L * BLOCKS + b + 1)
                    A.activation(nT[:, 512 * b:512 * b + 512], bank[4 + b][:, :], ACT.Identity, bias=cols[:, 8:9],
                                 scale=cols[:, 7:8]).then_inc(sem("ff_nT"), 1)
                n = len(FF_CHUNKS)
                for b in range(BLOCKS):
                    for i, (at, size) in enumerate(FF_CHUNKS):
                        k = n * b + i
                        act.wait_ge(sem("ff_ag_ps"), L * n * BLOCKS + k + 1)
                        if k >= 2:
                            act.wait_ge(sem("ff_act"), L * n * BLOCKS + k - 1)
                        A.activation(ff_g[0:size, k % 2, :], bank[2 * (k % 2) + 1][0:size, :], ACT.Gelu,
                                     bias=cols[0:size, 3 + i:4 + i]).then_inc(sem("ff_gelu"), 1)

        def ff_dve(dve, chain):
            V = nc.vector
            link = chain.link
            ln_dve(dve, LN_D, ff_norm)
            dve.wait_ge(sem("ff_consts_in"), 16)
            dve.wait_ge(sem("lnD_out"), BLOCKS)
            dve.sem_inc(sem("ff_wqkv_free"), 1)
            dve.sem_inc(sem("ff_w_free"), 1)
            dve.sem_inc(sem("ff_tables_free"), 1)

            def shift(name):
                V.memset(sT[HEAD_DIM:P, 0:1], 0.0)
                V.tensor_copy(sT[0:HEAD_DIM, :], hT[0:HEAD_DIM, :])
                V.tensor_copy(sT[HEAD_DIM:P, 1:N_TOK], hT[HEAD_DIM:P, 0:N_TOK - 1]).then_inc(sem(name), 1)

            with dve.Fori(0, DEPTH) as L:
                chain.body(L, FF_DVE_LINKS)
                shift("ff_s")
                dve.wait_ge(sem("ff_tables"), L + 1)
                for c in range(TILES + 1):
                    i = c % 2
                    for j, dst in ((0, q_rot), (1, k_rot)):
                        if c < TILES:
                            dve.wait_ge(sem("ff_sq"), L * 2 * TILES + 2 * c + j + 1)
                            if c >= 2:
                                dve.wait_ge(sem("ff_qT_ps" if j == 0 else "ff_kT_ps"), L * TILES + c - 1)
                            src = bank[PROJECTED[i][j]]
                            row = scaled[:, 2 * j, c, :].unsqueeze(1).to_broadcast([P, HEADS, HEAD_DIM])
                            V.tensor_tensor(dst[:, i].rearrange("p (h d) -> p h d", h=HEADS),
                                            src[:, :].rearrange("p (h d) -> p h d", h=HEADS), row, ALU.mult)
                            row = scaled[:, 2 * j + 1, c, :].rearrange("p (s d) -> p s d", s=2).unsqueeze(1).to_broadcast([P, HEADS, 2, HEAD_DIM // 2])
                            V.tensor_tensor(rot_tmp[:, 2 * i + j].rearrange("p (h s d) -> p h s d", h=HEADS, s=2),
                                            src[:, :].rearrange("p (h s d) -> p h s d", h=HEADS, s=2)[:, :, ::-1, :],
                                            row, ALU.mult).then_inc(sem("ff_rot"), 1)
                        if j == 0 and c:
                            dve.wait_ge(sem("ff_norm"), L * TILES + c)
                            V.reciprocal(inv_norm[:, c - 1], norms[:, c - 1]).then_inc(sem("ff_inv"), 1)
                    if c < TILES:
                        link(V.tensor_reduce(norms[:, c].rearrange("p j h -> p (j h)"),
                                             squares[:, 2 * i:2 * i + 2].rearrange("p j (h d) -> p (j h) d", h=HEADS), AX.X, ALU.add))
                        V.tensor_scalar(norms[:, c], norms[:, c], 1e-24, None, ALU.max).then_inc(sem("ff_norm2"), 1)
                dve.wait_ge(sem("ff_v"), L * TILES + TILES)
                dve.wait_ge(sem("ff_inv"), L * TILES + TILES)
                dve.sem_inc(sem("ff_wqkv_free"), 1)

                def maxima(c):
                    i = c % 2
                    first = WINDOW if c == 0 else 0
                    if c >= 2:
                        dve.wait_ge(sem("at_P"), L * TILES + c - 1)
                    for k in range(4):
                        dve.wait_ge(sem("at_s_ps"), L * 4 * TILES + 4 * c + k + 1)
                        s2 = bank[k][:, 0:2 * KEYS].rearrange("p (h j) -> p h j", h=2)
                        h0 = HEADS * i + 4 * (k // 2) + k % 2
                        V.tensor_tensor(scores[:, h0:h0 + 3:2, first:KEYS], s2[:, :, first:KEYS],
                                        mask_sb[:, first:KEYS].unsqueeze(1).to_broadcast([P, 2, KEYS - first]),
                                        ALU.add).then_inc(sem("at_s"), 1)
                    V.tensor_scalar(row_scale[:, i], inv_norm[:, c, 0, :], QK_SCALE, None, ALU.mult)
                    dve.wait_ge(sem("at_s"), L * 4 * TILES + 4 * c + 4)
                    link(V.tensor_reduce(row_max[:, i], scores[:, HEADS * i:HEADS * (i + 1), first:KEYS], AX.X, ALU.max))
                    V.scalar_tensor_tensor(row_bias[:, i], row_max[:, i], -1.0, row_scale[:, i], ALU.mult, ALU.mult).then_inc(sem("at_bias"), 1)

                def inverse_sums(c):
                    dve.wait_ge(sem("at_exp"), L * HEADS * TILES + HEADS * (c + 1))
                    if c >= 2:
                        dve.wait_ge(sem("at_P"), L * TILES + c - 1)
                    V.reciprocal(row_inv[:, c % 2], row_sum[:, c % 2]).then_inc(sem("at_inv"), 1)

                def attended(b):
                    dve.wait_ge(sem("at_wo_ps"), L * BLOCKS + b + 1)
                    sl = slice(512 * b, 512 * b + 512)
                    V.tensor_tensor(hT[:, sl], hT[:, sl], bank[5][:, :], ALU.add).then_inc(sem("at_h"), 1)

                maxima(0)
                maxima(1)
                inverse_sums(0)
                for c in range(TILES):
                    for k, bk, to in ((0, 4, 0), (1, 5, 8)):
                        dve.wait_ge(sem("at_PT_ps"), L * 3 * TILES + 3 * c + k + 1)
                        V.tensor_copy(probsT[:, to:to + 4, :], bank[bk][:, :].rearrange("p (a b) -> p a b", a=4)).then_inc(sem("at_PT_dve"), 1)
                    if c + 1 < TILES:
                        inverse_sums(c + 1)
                    if c + 2 < TILES:
                        maxima(c + 2)
                    dve.wait_ge(sem("at_o_ps"), L * TILES + c + 1)
                    if c % 4 == 0 and c:
                        dve.wait_ge(sem("at_wo_ps"), L * BLOCKS + c // 4)
                    V.tensor_copy(oT[HEAD_DIM:P, :, (c % 4) * P:(c % 4 + 1) * P],
                                  bank[7][HEAD_DIM:P, :].rearrange("p (j t) -> p j t", j=4)).then_inc(sem("at_o_odd"), 1)
                    if c % 4 == 0 and c:
                        attended(c // 4 - 1)
                attended(BLOCKS - 1)
                dve.wait_ge(sem("at_h"), L * BLOCKS + BLOCKS)
                dve.wait_ge(sem("at_o_even"), L * TILES + TILES)
                dve.sem_inc(sem("ff_tables_free"), 1)
                shift("ff_s2")
                ln_dve(dve, LN_FF + L, ff_norm)
                n = len(FF_CHUNKS)
                for b in range(BLOCKS):
                    for i, (at, size) in enumerate(FF_CHUNKS):
                        k = n * b + i
                        dve.wait_ge(sem("ff_gelu"), L * n * BLOCKS + k + 1)
                        if b and i == 0:
                            dve.wait_ge(sem("ff_y_ps"), L * BLOCKS + b)
                        V.scalar_tensor_tensor(ff_h[0:size, i, :], bank[2 * (k % 2)][0:size, :], cols[0:size, i:i + 1],
                                               ff_g[0:size, k % 2, :], ALU.add, ALU.mult).then_inc(sem("ff_act"), 1)
                    dve.wait_ge(sem("ff_y_ps"), L * BLOCKS + b + 1)
                    sl = slice(512 * b, 512 * b + 512)
                    V.scalar_tensor_tensor(hT[:, sl], bank[4 + b % 2][:, :], cols[:, 6:7], hT[:, sl], ALU.add, ALU.add).then_inc(sem("ff_x"), 1)
                dve.wait_ge(sem("ff_x"), L * BLOCKS + BLOCKS)
                dve.sem_inc(sem("ff_w_free"), 1)
            chain.leave(DEPTH)
            for b in range(BLOCKS):
                sl = slice(512 * b, 512 * b + 512)
                V.scalar_tensor_tensor(xT[:, sl], hT[:, sl], gate[:, 11:12], xT[:, sl], ALU.mult, ALU.add).then_inc(sem("x_ff"), 1)

        def ff_pe(pe):
            T = nc.tensor
            pe.wait_ge(sem("gla_x"), BLOCKS)
            ln_pe_tokens(pe, xT)
            ln_pe_back(pe, LN_D, ff_norm)
            pe.wait_ge(sem("lnD_out"), BLOCKS)
            with pe.Fori(0, DEPTH) as L:
                pe.wait_ge(sem("ff_s"), L + 1)
                pe.wait_ge(sem("ff_wqkv_in"), L * 48 + 48)

                def project(c):
                    q, k, v = PROJECTED[c % 2]
                    if c >= 2:
                        pe.wait_ge(sem("ff_rot"), L * 2 * TILES + 2 * (c - 1))
                        pe.wait_ge(sem("ff_sq"), L * 2 * TILES + 2 * (c - 1))
                    x = sT[:, c * P:(c + 1) * P]
                    T.matmul(bank[q][:, :], x, wqkv_sb[:, 0:512], start=True, stop=True)
                    T.matmul(bank[k][:, :], x, wqkv_sb[:, 512:1024], start=True, stop=True).then_inc(sem("ff_qk_ps"), 1)
                    if c >= 2:
                        pe.wait_ge(sem("ff_v"), L * TILES + c - 1)
                    T.matmul(bank[v][:, :], x, wqkv_sb[:, 1024:1536], start=True, stop=True).then_inc(sem("ff_v_ps"), 1)

                project(0)
                for c in range(TILES + 1):
                    if c + 1 < TILES:
                        project(c + 1)
                    if c:
                        for name, src, bk in (("q", q_rot, 4), ("k", k_rot, 5)):
                            pe.wait_ge(sem("ff_" + name), L * TILES + c)
                            if c >= 2:
                                pe.wait_ge(sem(f"ff_{name}T"), L * TILES + c - 1)
                            for j in range(4):
                                last = T.transpose(bank[bk][:, j * P:(j + 1) * P], src[:, (c - 1) % 2, j * P:(j + 1) * P], ident)
                            last.then_inc(sem(f"ff_{name}T_ps"), 1)

                def score(c):
                    first = WINDOW if c == 0 else 0
                    for k in range(4):
                        for i in range(2):
                            bk, slot = 2 * (k // 2) + i, k % 2
                            if c and slot == 0:
                                pe.wait_ge(sem("at_s"), L * 4 * TILES + 4 * (c - 1) + bk + 1)
                            r = slice(64 * i, 64 * i + 64)
                            last = T.matmul(bank[bk][:, KEYS * slot + first:KEYS * (slot + 1)], qhT[r, k, c * P:(c + 1) * P],
                                            khT[r, k, c * P - WINDOW + first:(c + 1) * P], start=True, stop=True)
                            if slot == 1:
                                last.then_inc(sem("at_s_ps"), 1)

                def output():
                    for j in range(4):
                        last = T.matmul(bank[5][:, :], wo_sb[:, j, :], oT[:, j, :], start=(j == 0), stop=(j == 3))
                    last.then_inc(sem("at_wo_ps"), 1)

                def turn_probs(c, bk, pieces):
                    for j, piece in enumerate(pieces):
                        last = T.transpose(bank[bk][:, j * P:(j + 1) * P], piece, ident)
                    last.then_inc(sem("at_PT_ps"), 1)

                pe.wait_ge(sem("ff_qT"), L * TILES + TILES)
                pe.wait_ge(sem("ff_kT"), L * TILES + TILES)
                pe.wait_ge(sem("ff_w_in"), L * 64 + 64)
                score(0)
                score(1)
                for c in range(TILES):
                    at = HEADS * (c % 2)
                    own = [probs_own[:, at + h, :] for h in range(HEADS)]
                    before = [probs_before[:, (at + 2 * m) * WINDOW:(at + 2 * m + 2) * WINDOW] for m in range(HEADS // 2)]
                    pe.wait_ge(sem("at_P"), L * TILES + c + 1)
                    turn_probs(c, 4, own[0:4])
                    if c % 4 == 1 and c > 1:
                        pe.wait_ge(sem("at_h"), L * BLOCKS + c // 4)
                    turn_probs(c, 5, before)
                    if c + 2 < TILES:
                        score(c + 2)
                    pe.wait_ge(sem("at_PT_dve"), L * 2 * TILES + 2 * c + 1)
                    turn_probs(c, 4, own[4:8])
                    pe.wait_ge(sem("at_PT_dve"), L * 2 * TILES + 2 * c + 2)
                    if c:
                        pe.wait_ge(sem("at_o_even"), L * TILES + c)
                        pe.wait_ge(sem("at_o_odd"), L * TILES + c)
                    if c % 4 == 0 and c:
                        output()
                    for m in range(HEADS // 2):
                        if m == 2:
                            pe.wait_ge(sem("at_PT_act"), L * TILES + c + 1)
                        cols_ = slice(m * P, (m + 1) * P)
                        even, odd = bank[6][0:HEAD_DIM, cols_], bank[7][HEAD_DIM:P, cols_]
                        T.matmul(even, v_tok[:, c, P * m:P * m + HEAD_DIM], probsT[:, 2 * m, :], start=True, stop=(c == 0))
                        last = T.matmul(odd, v_tok[:, c, P * m + HEAD_DIM:P * (m + 1)], probsT[:, 2 * m + 1, :], start=True, stop=(c == 0))
                        if c:
                            T.matmul(even, v_low[:, c - 1, HEAD_DIM * m:HEAD_DIM * (m + 1)], probsT[0:WINDOW, 8 + m, :], start=False, stop=True)
                            last = T.matmul(odd, v_tok[HEAD_DIM:P, c - 1, P * m + HEAD_DIM:P * (m + 1)], probsT[WINDOW:P, 8 + m, :], start=False, stop=True)
                    last.then_inc(sem("at_o_ps"), 1)
                pe.wait_ge(sem("at_o_even"), L * TILES + TILES)
                pe.wait_ge(sem("at_o_odd"), L * TILES + TILES)
                output()
                pe.wait_ge(sem("ff_s2"), L + 1)
                ln_pe_tokens(pe, sT)
                ln_pe_back(pe, LN_FF + L, ff_norm)
                n = len(FF_CHUNKS)
                pe.wait_ge(sem("ff_nT"), L * BLOCKS + BLOCKS)
                for b in range(BLOCKS):
                    rhs = nT[:, 512 * b:512 * b + 512]
                    for i, (at, size) in enumerate(FF_CHUNKS):
                        k = n * b + i
                        if k >= 2:
                            pe.wait_ge(sem("ff_act"), L * n * BLOCKS + k - 1)
                        T.matmul(bank[2 * (k % 2)][0:size, :], wf1_sb[:, at:at + size], rhs, start=True, stop=True)
                        T.matmul(bank[2 * (k % 2) + 1][0:size, :], wf1_sb[:, FF + at:FF + at + size], rhs,
                                 start=True, stop=True).then_inc(sem("ff_ag_ps"), 1)
                    pe.wait_ge(sem("ff_act"), L * n * BLOCKS + n * (b + 1))
                    if b >= 2:
                        pe.wait_ge(sem("ff_x"), L * BLOCKS + b - 1)
                    for i, (at, size) in enumerate(FF_CHUNKS):
                        last = T.matmul(bank[4 + b % 2][:, :], wf2_sb[0:size, i, :], ff_h[0:size, i, :],
                                        start=(i == 0), stop=(i == n - 1))
                    last.then_inc(sem("ff_y_ps"), 1)
                pe.wait_ge(sem("ff_x"), L * BLOCKS + BLOCKS)

        @block.sync
        def _(sp):
            sp.dma_start(ident, dram["ident"]).then_inc(sem("consts_in"), 16)
            sp.dma_start(cond, dram["cond"]).then_inc(sem("consts_in"), 16)
            sp.dma_start(wmod_sb, dram["wmod"]).then_inc(sem("consts_in"), 16)
            sp.dma_start(xT, dram["xT"]).then_inc(sem("x_in"), 16)
            sp.dma_start(sel, dram["sel"]).then_inc(sem("s4_consts_in"), 16)
            sp.dma_start(expo, dram["expo"].to_broadcast([P, N_EXP])).then_inc(sem("s4_consts_in"), 16)
            sp.wait_ge(sem("zero_set"), 1)
            sp.dma_start(k_pad[:, CHUNK:2 * CHUNK], k_im[:, 0, :]).then_inc(sem("s4_zero_out"), 16)
            sp.dma_start(prm, dram["prm"][0]).then_inc(sem("s4_prm_in"), 16)
            s4_sp_layer(sp, 0, first=True, more=True)
            with sp.Fori(1, S4_LAYERS - 1) as L:
                s4_sp_layer(sp, L, first=False, more=True)
            s4_sp_layer(sp, S4_LAYERS - 1, first=False, more=False)
            if stage != "s4d":
                sp.wait_ge(sem("x_s4"), BLOCKS)
                for dst, name in ((pw_sb, "pw"), (u_sb, "u"), (b2_sb, "b2")):
                    sp.dma_start(dst, dram[name]).then_inc(sem("moe_consts_in"), 16)
                sp.dma_start(w1_low, dram["w1"]).then_inc(sem("moe_w1_in"), 16)
                sp.dma_start(w2_low, dram["w2"]).then_inc(sem("moe_w2_in"), 16)
                sp.wait_ge(sem("moe_wT"), BLOCKS)
                sp.dma_start(share_d, weightT).then_inc(sem("moe_wT_out"), 16)
                sp.wait_ge(sem("moe_wT_out"), 16)
                with sp.Fori(0, BLOCKS) as b:
                    free = sp.snap(b + 1)
                    for r, (dst, name) in enumerate(((share1, "1"), (share2, "2"))):
                        sp.wait_ge(sem("moe_share_free" + name), free)
                        sp.sem_inc(sem("sp_turn"), 1)
                        rows = share_d[(r + 1) * EXPERTS:(r + 2) * EXPERTS, bass.ts(b, 512)]
                        sp.dma_start(dst, rows.partition_broadcast(P)).then_inc(sem("moe_share_in" + name), 16)
            if stage not in ("s4d", "moe"):
                sp.wait_ge(sem("moe_x"), BLOCKS + 1)
                for dst, name in ((wqf_sb, "wqf"), (wi_sb, "wi"), (wo8_sb, "wo8")):
                    sp.dma_start(dst, dram[name]).then_inc(sem("gla_w_in"), 16)
            if stage == "full":
                sp.wait_ge(sem("gla_x"), BLOCKS)
                sp.dma_start(mask_sb, dram["mask"]).then_inc(sem("ff_consts_in"), 16)
                with sp.Fori(0, DEPTH) as L:
                    one = sp.snap(L + 1)
                    sp.wait_ge(sem("ff_wqkv_free"), one)
                    sp.sem_inc(sem("sp_turn"), 1)
                    sp.dma_start(wqkv_sb, dram["wqkv"][L]).then_inc(sem("ff_wqkv_in"), 16)
                    sp.dma_start(qk_rows, dram["qk_rows"][L]).then_inc(sem("ff_wqkv_in"), 16)
                    sp.wait_ge(sem("ff_tables_free"), one)
                    sp.sem_inc(sem("sp_turn"), 1)
                    sp.dma_start(scaled, dram["tables"]).then_inc(sem("ff_wqkv_in"), 16)
                    sp.wait_ge(sem("ff_w_free"), one)
                    sp.sem_inc(sem("sp_turn"), 1)
                    for dst, name in ((wo_sb, "wo"), (wf1_sb, "wf1"), (wf2_sb, "wf2"), (cols, "cols")):
                        sp.dma_start(dst, dram[name][L]).then_inc(sem("ff_w_in"), 16)
            sp.wait_ge(sem("result"), BLOCKS)
            sp.dma_start(out.rearrange("o (c i) d -> i (o c) d", i=P), ff_norm).then_inc(sem("stored"), 16)
            sp.wait_ge(sem("stored"), 16)

        @block.gpsimd
        def _(pool):
            nc.gpsimd.memset(eps_col, EPS_LN)
            nc.gpsimd.memset(ones, 1.0)
            nc.gpsimd.memset(neg_half, -0.5).then_inc(sem("p_set"), 1)
            pool.wait_ge(sem("p_set"), 1)
            ln_pool(pool, LN_A)
            chain = Chain(pool, sem("p_chain"))
            pool.wait_ge(sem("s4_consts_in"), 32)
            s4_pool_angles(pool, chain, 0)
            s4_pool_powers(pool, chain, 0)
            with pool.Fori(0, S4_LAYERS - 1) as L:
                chain.body(L, 4)
                ln_pool(pool, LN_S4 + L)
                s4_pool_angles(pool, chain, L + 1)
                pool.wait_ge(sem("s4_pow_moved"), L * 128 + 128)
                pool.wait_ge(sem("s4_u"), L + 1)
                s4_pool_powers(pool, chain, L + 1)
            chain.leave(S4_LAYERS - 1)
            ln_pool(pool, LN_S4 + S4_LAYERS - 1)
            if stage != "s4d":
                ln_pool(pool, LN_B)
                for w_high_s, w_low, w_low_s, n in ((w1_high_s, w1_low, w1_low_s, "1"), (w2_high_s, w2_low, w2_low_s, "2")):
                    for e in range(EXPERTS):
                        pool.wait_ge(sem(f"moe_w{n}_high"), e + 1)
                        nc.gpsimd.tensor_tensor(w_low_s[:, e], w_low[:, e], w_high_s[:, e], ALU.subtract).then_inc(sem(f"moe_w{n}_low"), 1)
            if stage not in ("s4d", "moe"):
                ln_pool(pool, LN_C)
                for v in range(LIN_DIM):
                    i = v % 2
                    pool.wait_ge(sem("gla_state"), v + 1)
                    if v >= 2:
                        pool.wait_ge(sem("gla_read_used"), v - 1)
                    nc.gpsimd.tensor_tensor(read[i], state[i], qT, ALU.mult).then_inc(sem("gla_read"), 1)
            if stage == "full":
                ln_pool(pool, LN_D)
                with pool.Fori(0, DEPTH) as L:
                    chain.body(L, TILES)
                    pool.wait_ge(sem("ff_wqkv_in"), L * 48 + 48)
                    for i in range(4):
                        row = qk_rows[:, i, :].unsqueeze(1).to_broadcast([P, TILES, HEAD_DIM])
                        last = nc.gpsimd.tensor_tensor(scaled[:, i], scaled[:, i], row, ALU.mult)
                    last.then_inc(sem("ff_tables"), 1)
                    for c in range(TILES + 1):
                        if c:
                            pool.wait_ge(sem("ff_inv"), L * TILES + c)
                            chain.wait()
                            k8 = k_rot[:, (c - 1) % 2].rearrange("p (h d) -> p h d", h=HEADS)
                            nc.gpsimd.tensor_tensor(k8, k8, inv_norm[:, c - 1, 1, :].unsqueeze(2).to_broadcast([P, HEADS, HEAD_DIM]),
                                                    ALU.mult).then_inc(sem("ff_k"), 1)
                        if c < TILES:
                            i = c % 2
                            pool.wait_ge(sem("ff_rot"), L * 2 * TILES + 2 * c + 1)
                            nc.gpsimd.tensor_tensor(q_rot[:, i], q_rot[:, i], rot_tmp[:, 2 * i], ALU.add).then_inc(sem("ff_q"), 1)
                            pool.wait_ge(sem("ff_rot"), L * 2 * TILES + 2 * c + 2)
                            chain.mark(nc.gpsimd.tensor_tensor(k_rot[:, i], k_rot[:, i], rot_tmp[:, 2 * i + 1], ALU.add))
                    for c in range(TILES):
                        pool.wait_ge(sem("at_inv"), L * TILES + c + 1)
                        if c >= 2:
                            pool.wait_ge(sem("at_PT_ps"), L * 3 * TILES + 3 * (c - 1))
                        two = slice(HEADS * (c % 2), HEADS * (c % 2 + 1))
                        inv = lambda n: row_inv[:, c % 2].unsqueeze(2).to_broadcast([P, HEADS, n])
                        if c:
                            nc.gpsimd.tensor_tensor(probs_before.rearrange("p (h j) -> p h j", j=WINDOW)[:, two],
                                                    scores[:, two, 0:WINDOW], inv(WINDOW), ALU.mult)
                        nc.gpsimd.tensor_tensor(probs_own[:, two], scores[:, two, WINDOW:KEYS], inv(P),
                                                ALU.mult).then_inc(sem("at_P"), 1)
                    ln_pool(pool, LN_FF + L)
                chain.leave(DEPTH)

        @block.scalar
        def _(act):
            act.wait_ge(sem("consts_in"), 48)
            nc.scalar.activation(cond_sig, cond, ACT.Sigmoid).then_inc(sem("cond_sig"), 1)
            act.wait_ge(sem("mod_ready"), 1)
            s4_act_magnitudes(act, 0)
            s4_act_decay(act, 0)
            s4_act_sines(act, 0, CLOSE, "s4_sin")
            s4_act_sines(act, 0, FAR, "s4_sin_far")
            ln_act(act, LN_A, "lnA_out", hT, one_plus[:, 1:2], mod[:, 0:1])
            with act.Fori(0, S4_LAYERS - 1) as L:
                s4_act_layer(act, L, more=True)
            s4_act_layer(act, S4_LAYERS - 1, more=False)
            if stage != "s4d":
                moe_act(act)
            if stage not in ("s4d", "moe"):
                gla_act(act)
            if stage == "full":
                ff_act(act)
            for b in range(BLOCKS):
                act.wait_ge(sem("result_ps"), b + 1)
                nc.scalar.activation(ff_norm[:, 4 * b:4 * b + 4, :], bank[b][:, :].rearrange("p (a b) -> p a b", a=4), ACT.Copy).then_inc(sem("result"), 1)

        @block.vector
        def _(dve):
            chain = Chain(dve, sem("v_chain"))
            link = chain.link
            V = nc.vector
            V.memset(k_im[:, 0, :], 0.0).then_inc(sem("zero_set"), 1)
            V.memset(decay, 0.0)
            dve.wait_ge(sem("cond_sig"), 1)
            V.tensor_tensor(cond_silu, cond, cond_sig, ALU.mult).then_inc(sem("cond_silu"), 1)
            dve.wait_ge(sem("mod_ps"), 1)
            link(V.tensor_copy(mod, bank[7][:, 0:12]))
            V.tensor_scalar(mod_sign, mod, 0.0, 2.0, ALU.is_ge, ALU.mult)
            V.tensor_scalar(one_plus, mod, 1.0, None, ALU.add)
            link(V.scalar_tensor_tensor(mod_abs, mod, -1.0, mod, ALU.mult, ALU.max))
            link(V.tensor_scalar(mod_abs, mod_abs, 0.25, None, ALU.max))
            V.scalar_tensor_tensor(gate, mod_sign, -1.0, mod_abs, ALU.add, ALU.mult).then_inc(sem("mod_ready"), 1)
            dve.wait_ge(sem("s4_zero_out"), 16)
            dve.wait_ge(sem("s4_consts_in"), 32)
            ln_dve(dve, LN_A, z_tok)
            s4_dve_angles(dve, 0)
            s4_dve_reduce(dve, chain, 0)
            s4_dve_powers(dve, chain, 0)
            with dve.Fori(0, S4_LAYERS - 1) as L:
                chain.body(L, S4_DVE_LINKS)
                s4_dve_layer(dve, chain, L, more=True)
            chain.leave(S4_LAYERS - 1)
            s4_dve_layer(dve, chain, S4_LAYERS - 1, more=False)
            dve.wait_ge(sem("s4_h"), S4_LAYERS * BLOCKS)
            for b in range(BLOCKS):
                sl = slice(512 * b, 512 * b + 512)
                V.scalar_tensor_tensor(xT[:, sl], hT[:, sl], gate[:, 2:3], xT[:, sl], ALU.mult, ALU.add).then_inc(sem("x_s4"), 1)
            if stage != "s4d":
                moe_dve(dve, link)
                moe_dve_blocks(dve, chain)
            if stage not in ("s4d", "moe"):
                gla_dve(dve, link)
            if stage == "full":
                ff_dve(dve, chain)

        @block.tensor
        def _(pe):
            T = nc.tensor
            pe.wait_ge(sem("cond_silu"), 1)
            for i in range(12):
                last = T.matmul(bank[7][:, i:i + 1], wmod_sb[:, i // 6, (i % 6) * P:(i % 6 + 1) * P],
                                cond_silu[:, i // 6:i // 6 + 1], start=True, stop=True)
            last.then_inc(sem("mod_ps"), 1)
            pe.wait_ge(sem("mod_ps"), 1)
            pe.sem_inc(sem("s4_tp_free"), 1)
            pe.wait_ge(sem("x_in"), 16)
            ln_pe_tokens(pe, xT)
            pe.wait_ge(sem("mod_ready"), 1)
            ln_pe_back(pe, LN_A, z_tok)
            pe.wait_ge(sem("s4_consts_in"), 32)
            s4_pe_layer(pe, 0, first=True)
            with pe.Fori(1, S4_LAYERS) as L:
                s4_pe_layer(pe, L, first=False)
            if stage != "s4d":
                moe_pe(pe)
            if stage not in ("s4d", "moe"):
                gla_pe(pe)
            if stage == "full":
                ff_pe(pe)
            final, more = {"s4d": ("x_s4", 0), "moe": ("moe_x", 1), "gla": ("gla_x", 0), "full": ("x_ff", 0)}[stage]
            for b in range(BLOCKS):
                pe.wait_ge(sem(final), b + 1 + more)
                for t in range(4):
                    last = T.transpose(bank[b][:, t * P:(t + 1) * P], xT[:, (4 * b + t) * P:(4 * b + t + 1) * P], ident)
                last.then_inc(sem("result_ps"), 1)


S4_DVE_LINKS = 26
FF_DVE_LINKS = 32


def kernel(**inputs):
    import concourse.bacc as bacc
    from concourse.bass_utils import run_bass_kernel_spmd

    def arr(name):
        return np.ascontiguousarray(inputs[name])

    def modes(a):
        return a.reshape(S4_LAYERS, GROUPS, HG, MODES).transpose(0, 1, 3, 2).reshape(S4_LAYERS, P, HG)

    log_dt = np.repeat(arr("L0_attn_log_dt").reshape(S4_LAYERS, GROUPS, 1, HG), MODES, axis=2)
    prm = np.stack([log_dt.reshape(S4_LAYERS, P, HG)] + [modes(arr("L0_attn_" + n)) for n in ("A_re_log", "A_im", "C_re", "C_im")], axis=2)
    ln_wb = np.stack([arr("L0_attn_ln_w"), arr("L0_attn_ln_b")], axis=1)
    laid = {
        "ident": np.eye(P, dtype=np.float32),
        "cond": np.stack([arr("L0_c").reshape(P), arr("L1_c").reshape(P)], axis=1),
        "wmod": np.stack([arr("L0_wmod"), arr("L1_wmod")], axis=1),
        "xT": arr("L0_attn_x").reshape(N_TOK, P).T,
        "sel": np.stack([np.repeat(s * np.eye(GROUPS, dtype=np.float32), MODES, axis=0) for s in (1, -1)], axis=1),
        "expo": exponents().reshape(1, N_EXP),
        "prm": prm,
        "skip": arr("L0_attn_D_skip").reshape(S4_LAYERS, GROUPS, HG),
        "ln_wb": np.repeat(ln_wb.reshape(S4_LAYERS, 1, 2, P), P, axis=1),
        "w_out": arr("L0_attn_W_out").transpose(0, 2, 1),
        "b_out": arr("L0_attn_b_out").reshape(S4_LAYERS, 2, P).transpose(0, 2, 1),
    }
    order = [2, 0, 1]
    u = np.stack([arr("L0_ffn_U1"), arr("L0_ffn_U2"), arr("L0_ffn_U3")])[order]
    qs, ks = arr("L1_ffn_q_scale"), arr("L1_ffn_k_scale")
    swap = lambda a: np.concatenate([a[:, HEAD_DIM // 2:], a[:, :HEAD_DIM // 2]], axis=1)
    qk_rows = np.stack([qs, swap(qs), ks, swap(ks)], axis=1)
    b1 = arr("L1_ffn_b1")
    cols = np.zeros((DEPTH, P, 9), np.float32)
    for i, (at, size) in enumerate(FF_CHUNKS):
        cols[:, :size, i] = b1[:, at:at + size]
        cols[:, :size, 3 + i] = b1[:, FF + at:FF + at + size]
    cols[:, :, 6], cols[:, :, 7], cols[:, :, 8] = arr("L1_ffn_b2"), arr("L1_ffn_ln_g"), arr("L1_ffn_ln_b")
    wf2 = np.zeros((DEPTH, P, 3, P), np.float32)
    for i, (at, size) in enumerate(FF_CHUNKS):
        wf2[:, :size, i] = arr("L1_ffn_w2")[:, at:at + size]
    wi = arr("L1_attn_Wi").reshape(P, LIN_HEADS, 1, LIN_DIM)
    wo8 = arr("L1_attn_Wo").reshape(LIN_HEADS, LIN_DIM, 1, P)
    laid.update({
        "pw": arr("L0_ffn_P_w").T,
        "u": u.reshape(ROUTERS * EXPERTS, ADDR).T,
        "b2": arr("L0_ffn_b2"),
        "w1": arr("L0_ffn_W1").transpose(2, 0, 1),
        "w2": arr("L0_ffn_W2").reshape(EXPERTS, P, HID_CHUNKS, P).transpose(3, 0, 2, 1),
        "wqf": np.concatenate([arr("L1_attn_Wq"), arr("L1_attn_Wf")], axis=1),
        "wi": np.repeat(wi, LIN_DIM, axis=2).transpose(0, 3, 1, 2).reshape(P, LIN_DIM, P),
        "wo8": np.repeat(wo8, LIN_DIM, axis=2).transpose(0, 2, 1, 3).reshape(P, LIN_DIM, P),
        "mask": window_mask(),
        "tables": rotary_tables().reshape(4, TILES, P, HEAD_DIM).transpose(2, 0, 1, 3),
        "wqkv": arr("L1_ffn_wqkv"),
        "qk_rows": np.repeat(qk_rows.reshape(DEPTH, 1, 4, HEAD_DIM), P, axis=1),
        "wo": arr("L1_ffn_wo").reshape(DEPTH, 4, P, P).transpose(0, 2, 1, 3),
        "wf1": arr("L1_ffn_w1"),
        "wf2": wf2,
        "cols": cols,
    })
    nc = bacc.Bacc("TRN2", target_bir_lowering=False, num_devices=1)
    arrays, dram = {}, {}
    for name, a in laid.items():
        a = np.ascontiguousarray(a)
        arrays[name + "_dram"] = a
        dram[name] = nc.dram_tensor(name + "_dram", a.shape, F32, kind="ExternalInput").ap()
    out = nc.dram_tensor("out_0_dram", (1, N_TOK, P), F32, kind="ExternalOutput").ap()
    program(nc, dram, out, STAGE)
    r = run_bass_kernel_spmd(nc, [arrays], core_ids=[0])
    return r.results[0]["out_0_dram"]
```

```python
import math
from contextlib import ExitStack

import numpy as np

import concourse.bass as bass
from concourse import mybir

F32 = mybir.dt.float32
F32R = mybir.dt.float32r
ALU = mybir.AluOpType
ACT = mybir.ActivationFunctionType
AX = mybir.AxisListType

P = 128
N_TOK = 2048
TILES = N_TOK // P
BLOCKS = N_TOK // 512
EPS_LN = 1e-5

S4_LAYERS = 4
MODES = 32
GROUPS = P // MODES
HG = P // GROUPS
CHUNK = 64
CHUNKS = N_TOK // CHUNK
LOW = 16
HIGH = CHUNK // LOW
NEAR = LOW + HIGH
ONE = LOW - 2
N_EXP = NEAR + CHUNKS
MAGIC = 1.5 * 2.0 ** 23
TWO_PI_1 = 6.28125
TWO_PI_2 = float(np.float32(np.round((2 * math.pi - TWO_PI_1) * 2 ** 21) / 2 ** 21))
TWO_PI_3 = 2 * math.pi - TWO_PI_1 - TWO_PI_2
PIECES = 4
PIECE = HG // PIECES

EXPERTS, TOP, HIDDEN, ADDR = 12, 3, 512, 64
ROUTERS = 3
HID_CHUNKS = HIDDEN // P
AHEAD = 3

LIN_HEADS, LIN_DIM = 16, 8

DEPTH, HEADS, HEAD_DIM, WINDOW = 2, 8, 64, 64
FF = int(P * 4 * 2 / 3)
FF_CHUNKS = [(0, P), (P, P), (2 * P, FF - 2 * P)]
KEYS = WINDOW + P
QK_SCALE = 8.0
MASKED = -1e30


def rotary_tables():
    half = np.arange(0, HEAD_DIM, 2, dtype=np.float32)
    inv = (1.0 / 10000.0 ** (half / HEAD_DIM)).astype(np.float32)
    t = np.arange(N_TOK, dtype=np.float32)
    freqs = (t[:, None] * inv[None, :]).astype(np.float32).astype(np.float64)
    base = (half.astype(np.float64) + 0.4 * HEAD_DIM) / (1.4 * HEAD_DIM)
    power = (t.astype(np.float64) - N_TOK // 2) / float(WINDOW // 2)
    scale = base[None, :] ** power[:, None]
    cos, sin = np.cos(freqs), np.sin(freqs)
    two = lambda a, b: np.concatenate([a, b], axis=1).astype(np.float32)
    return np.stack([two(cos * scale, cos * scale), two(-sin * scale, sin * scale),
                     two(cos / scale, cos / scale), two(-sin / scale, sin / scale)])


def window_mask():
    i = np.arange(P)[:, None] + WINDOW
    j = np.arange(KEYS)[None, :]
    return np.where((i < j) | (i > j + WINDOW), MASKED, 0.0).astype(np.float32)


def exponents():
    e = [LOW - 1 - b for b in range(LOW)] + [LOW * (HIGH - 1 - a) for a in range(HIGH)] + [CHUNK * c for c in range(CHUNKS)]
    return np.array(e, np.float32)


class Chain:

    def __init__(self, engine, semaphore):
        self.engine, self.semaphore = engine, semaphore
        self.n = self.base = self.seen = 0

    def mark(self, instruction):
        instruction.then_inc(self.semaphore, 1)
        self.seen += 1
        self.n = self.base + self.seen

    def wait(self):
        self.engine.wait_ge(self.semaphore, self.n)

    def link(self, instruction):
        self.mark(instruction)
        self.wait()

    def body(self, step, per_step):
        self.start, self.per_step = self.n, per_step
        self.base, self.seen = step * per_step + self.start, 0
        self.n = self.base

    def leave(self, steps):
        assert self.seen == self.per_step, (self.seen, self.per_step)
        self.n = self.base = self.start + steps * self.per_step
        self.seen = 0


def program(nc, dram, out):
    ctx = ExitStack()
    with ctx:
        sems = {}

        def sem(name):
            if name not in sems:
                sems[name] = ctx.enter_context(nc.semaphore(name))
            return sems[name]

        KEPT, MAIN, ARENA = 4608, 32768, 53000
        kept = ctx.enter_context(nc.sbuf_tensor("kept", [P, KEPT], F32))
        with nc.sbuf_tensor("main", [P, MAIN], F32) as main:
            pass
        short = {}
        for name, n in (("w1_high", EXPERTS * HIDDEN), ("w1_low", EXPERTS * HIDDEN),
                        ("w2_high", EXPERTS * HIDDEN), ("w2_low", EXPERTS * HIDDEN),
                        ("x_high", AHEAD * 512), ("x_low", AHEAD * 512),
                        ("hid_high", HID_CHUNKS * 512), ("hid_low", HID_CHUNKS * 512)):
            short[name] = ctx.enter_context(nc.sbuf_tensor(name, [P, n], F32R))
        rest_of_main = MAIN - 4 * EXPERTS * HIDDEN - 2 * (AHEAD + HID_CHUNKS) * 512
        ctx.enter_context(nc.sbuf_tensor("main_end", [P, rest_of_main], F32))
        rest = ctx.enter_context(nc.sbuf_tensor("rest", [P, ARENA - KEPT - MAIN], F32))
        stretches = ((0, KEPT, kept), (KEPT, KEPT + MAIN, main), (KEPT + MAIN, ARENA, rest))
        bank = [ctx.enter_context(nc.psum_tensor(f"bank{i}", [P, 512], F32)) for i in range(8)]

        def shaped(v, dims):
            if len(dims) == 2:
                v = v.rearrange("p (a b) -> p a b", a=dims[0])
            if len(dims) == 3:
                v = v.rearrange("p (a b c) -> p a b c", a=dims[0], b=dims[1])
            return v

        def carve(at, *dims, parts=P):
            n = int(np.prod(dims))
            for start, end, tensor in stretches:
                if start <= at and at + n <= end:
                    return shaped(tensor[0:parts, at - start:at - start + n], dims)
            raise ValueError(f"{dims} at {at} is not within a stretch")

        top = [0]

        def keep(*dims, parts=P):
            n = int(np.prod(dims))
            for start, end, tensor in stretches:
                if top[0] < end < top[0] + n:
                    top[0] = end
            at = top[0]
            top[0] += n
            return carve(at, *dims, parts=parts)

        def keep_both(name, *dims):
            return keep(*dims), shaped(short[name][:, :], dims)

        xT = keep(N_TOK)
        hT = keep(N_TOK)
        ident = keep(P)
        cond = keep(2)
        cond_sig = keep(2)
        cond_silu = keep(2)
        mod = keep(12)
        one_plus = keep(12)
        mod_sign = keep(12)
        mod_abs = keep(12)
        gate = keep(12)
        neg_half = keep(TILES)
        stats = keep(TILES, 6)
        mean_var = keep(TILES, 2)
        rstd = keep(TILES)
        var_eps = keep(TILES)
        eps_col = keep(TILES)
        neg_mean = keep(TILES // 2)
        neg_one = keep(TILES // 2)
        shift = keep(TILES // 2)
        turn_mark = keep(3)
        pool_mark = keep(1)
        top[0] = phase_base = KEPT

        zu = keep(P, CHUNKS)
        tp = keep(P, CHUNK)
        wmod_sb = tp.rearrange("p a b -> p (a b)")[:, 0:2 * 768].rearrange("p (a b) -> p a b", a=2)
        back = keep(HG, 2, P, parts=CHUNK)
        pow_re = keep(HG, CHUNK)
        pow_im = keep(HG, CHUNK)
        k_re = keep(HG, CHUNK)
        k_im = keep(HG, CHUNK)
        b_re, b_im = (k_re.rearrange("p a b -> p (a b)")[:, i * HG * CHUNKS:(i + 1) * HG * CHUNKS].rearrange("p (h c) -> p h c", c=CHUNKS) for i in (0, 1))
        s_a, s_b = (k_im.rearrange("p a b -> p (a b)")[:, i * HG * CHUNKS:(i + 1) * HG * CHUNKS].rearrange("p (h c) -> p h c", c=CHUNKS) for i in (0, 1))
        z_tok = keep(TILES, P)
        yT = z_tok.rearrange("p a b -> p (a b)")
        states = keep(HG, 2, CHUNKS)
        y_act = states.rearrange("p a b c -> p (a b c)").rearrange("p (i h) -> p i h", h=HG)
        glu_sig = states.rearrange("p a b c -> p (a b c)")
        k_rows = keep(HG, CHUNK, parts=GROUPS)
        prm = keep(5, HG)
        skip = keep(HG, parts=GROUPS)
        ln_wb = keep(2, P)
        w_out = keep(2 * P)
        b_out = keep(2)
        sel = keep(2, GROUPS)
        expo = keep(N_EXP)
        exps = keep(2, HG)
        dta = keep(2, HG)
        theta = keep(HG, N_EXP)
        turns = keep(HG, N_EXP)
        sn = keep(HG, N_EXP)
        cosn = keep(HG, N_EXP)
        anc_re = keep(HG, NEAR)
        anc_im = keep(HG, NEAR)
        mag = keep(HG, NEAR)
        tanh = keep(HG)
        r_chunk = keep(HG)
        small = [keep(HG) for _ in range(12)]
        g_re = keep(HG, CHUNKS)
        g_im = keep(HG, CHUNKS)
        decay = keep(HG, CHUNKS)
        ones = keep(CHUNKS - 1)
        u_re, u_im = (glu_sig[:, i * HG * CHUNKS:(i + 1) * HG * CHUNKS].rearrange("p (h c) -> p h c", c=CHUNKS) for i in (0, 1))

        top[0] = phase_base
        w1_high, w1_high_s = keep_both("w1_high", EXPERTS, HIDDEN)
        w1_low, w1_low_s = keep_both("w1_low", EXPERTS, HIDDEN)
        w2_high, w2_high_s = keep_both("w2_high", EXPERTS, HID_CHUNKS, P)
        w2_low, w2_low_s = keep_both("w2_low", EXPERTS, HID_CHUNKS, P)
        x_high, x_high_s = keep_both("x_high", AHEAD, 512)
        x_low, x_low_s = keep_both("x_low", AHEAD, 512)
        hid_high, hid_high_s = keep_both("hid_high", HID_CHUNKS, 512)
        hid_low, hid_low_s = keep_both("hid_low", HID_CHUNKS, 512)
        y_acc = keep(512)
        y_part = [keep(512) for _ in range(2)]
        weightT = keep(N_TOK, parts=ROUTERS * EXPERTS)
        pw_sb = keep(ADDR)
        u_sb = keep(ROUTERS * EXPERTS, parts=ADDR)
        b2_sb = keep(P, parts=EXPERTS)
        at_shares = top[0]
        share1 = keep(EXPERTS, 512)
        share2 = keep(EXPERTS, 512)
        top[0] = at_shares
        moe_norm = keep(TILES, P)
        addr = keep(N_TOK, parts=ADDR)
        logit = keep(TILES, ROUTERS * EXPERTS)
        weight = keep(TILES, ROUTERS * EXPERTS)
        above = keep(TILES, ROUTERS * EXPERTS)
        equal = keep(TILES, ROUTERS * EXPERTS)
        ranks = keep(TILES, ROUTERS * EXPERTS)
        fresh = keep(TILES, ROUTERS * EXPERTS)
        top8 = keep(TILES * ROUTERS, 8)
        room = keep(TILES * ROUTERS)
        total = keep(TILES * ROUTERS)

        top[0] = phase_base
        sT = keep(N_TOK)
        nT = sT
        wqkv_sb = keep(3 * HEADS * HEAD_DIM)
        wo_sb = keep(4, P)
        wf1_sb = keep(2 * FF)
        wf2_sb = keep(3, P)
        cols = keep(9)
        qk_rows = keep(4, HEAD_DIM)
        mask_sb = keep(KEYS)
        norms = keep(TILES, 2, HEADS)
        inv_norm = keep(TILES, 2, HEADS)
        row_max = keep(2, HEADS)
        row_scale = keep(2, HEADS)
        row_bias = keep(2, HEADS)
        row_sum = keep(2, HEADS)
        row_inv = keep(2, HEADS)
        after_weights = at_heads = top[0]
        qhT = keep(4, N_TOK)
        khT = keep(4, N_TOK)
        ff_norm = carve(at_heads, TILES, P)
        v_tok = keep(TILES, 512)
        v_low = keep(TILES, 256, parts=HEAD_DIM)
        at_work = top[0]
        scaled = keep(4, TILES, HEAD_DIM)
        q_rot = keep(2, 512)
        k_rot = keep(2, 512)
        rot_tmp = keep(4, 512)
        squares = keep(4, 512)
        top[0] = at_work
        scores = keep(2 * HEADS, KEYS)
        probs_own = keep(2 * HEADS, P)
        probs_before = keep(2 * HEADS * WINDOW)
        probsT = keep(3 * 4, P)
        oT = keep(4, 512)
        top[0] = at_work + 4 * TILES * HEAD_DIM
        ff_g = keep(3, 512)
        ff_h = keep(6, 512)
        top[0] = after_weights
        gla_norm = keep(TILES, P)
        wqf_sb = keep(2 * P)
        wi_sb = keep(LIN_DIM, P)
        wo8_sb = keep(LIN_DIM, P)
        soft = keep(TILES, 2, P)
        neg_max = keep(TILES, 2)
        soft_sum = keep(TILES, 2)
        qT = keep(N_TOK)
        keepT = keep(N_TOK)
        kT = keep(N_TOK)
        kv = [keep(N_TOK) for _ in range(2)]
        state = [keep(N_TOK) for _ in range(2)]
        read = [keep(N_TOK) for _ in range(2)]
        assert top[0] <= at_work
        share_d = nc.dram_tensor("share_d", [ROUTERS * EXPERTS, N_TOK], F32, kind="Internal").ap()
        k_pad = nc.dram_tensor("k_pad", [P, 2 * CHUNK], F32, kind="Internal").ap()

        block = ctx.enter_context(nc.Block())

        LN_A, LN_B, LN_C, LN_D = 0, 1 + S4_LAYERS, 2 + S4_LAYERS, 3 + S4_LAYERS
        LN_S4, LN_FF = 1, 4 + S4_LAYERS

        def going_back(n):
            return n if isinstance(n, int) and n == LN_A else n - S4_LAYERS

        def ln_pe_tokens(pe, src, written=None):
            for b in range(BLOCKS):
                if written is not None:
                    written(b)
                for t in range(4):
                    c = 4 * b + t
                    last = nc.tensor.transpose(bank[b][:, t * P:(t + 1) * P], src[:, c * P:(c + 1) * P], ident)
                last.then_inc(sem("ln_tokens"), 1)

        def ln_pe_back(pe, n, normed):
            for b in range(BLOCKS):
                pe.wait_ge(sem("ln_normed" if b < 2 else "ln_normed_act"), going_back(n) * 2 + b % 2 + 1)
                for t in range(4):
                    c = 4 * b + t
                    last = nc.tensor.transpose(bank[4 + b][:, t * P:(t + 1) * P], normed[:, c, :], ident)
                last.then_inc(sem("ln_back"), 1)

        def ln_dve_stats(dve, n):
            for half in range(2):
                for b in (2 * half, 2 * half + 1):
                    dve.wait_ge(sem("ln_tokens"), n * BLOCKS + b + 1)
                    for t in range(4):
                        c = 4 * b + t
                        nc.vector.bn_stats(stats[:, c, :], bank[b][:, t * P:(t + 1) * P]).then_inc(sem("ln_stats"), 1)
                dve.wait_ge(sem("ln_stats"), n * TILES + 8 * (half + 1))
                nc.vector.memset(turn_mark[:, half:half + 1], 0.0)
                for c in range(8 * half, 8 * half + 8):
                    nc.vector.bn_aggr(mean_var[:, c, :], stats[:, c, :]).then_inc(sem("ln_aggr"), 1)

        def ln_dve(dve, n, normed, dst, scale, bias):
            ln_dve_stats(dve, n)
            dve.wait_ge(sem("ln_rstd"), n * 2 + 1)
            for b in range(2):
                for t in range(4):
                    c = 4 * b + t
                    last = nc.vector.tensor_scalar(normed[:, c, :], bank[b][:, t * P:(t + 1) * P],
                                                   mean_var[:, c, 0:1], rstd[:, c:c + 1],
                                                   ALU.subtract, ALU.mult)
                last.then_inc(sem("ln_normed"), 1)
            for b in range(2):
                dve.wait_ge(sem("ln_back"), going_back(n) * BLOCKS + b + 1)
                nc.vector.tensor_scalar(dst[:, 512 * b:512 * b + 512], bank[4 + b][:, :], scale, bias,
                                        ALU.mult, ALU.add).then_inc(sem("ln_out_dve"), 1)

        def ln_pool(pool, n, shared):
            G_ = nc.gpsimd
            for half in range(2):
                tiles = slice(8 * half, 8 * half + 8)
                pool.wait_ge(sem("ln_aggr"), n * TILES + 8 * (half + 1))
                G_.tensor_tensor(var_eps[:, tiles], mean_var[:, tiles, 1], eps_col[:, tiles], ALU.add).then_inc(sem("ln_eps"), 1)
                if half and shared:
                    G_.tensor_tensor(neg_mean, mean_var[:, tiles, 0], neg_one, ALU.mult)
                pool.wait_ge(sem("ln_eps"), n * 2 + half + 1)
                G_.tensor_tensor(rstd[:, tiles], var_eps[:, tiles], neg_half[:, tiles], ALU.pow).then_inc(sem("ln_rstd"), 1)
            if shared:
                pool.wait_ge(sem("ln_rstd"), n * 2 + 2)
                G_.tensor_tensor(shift, neg_mean, rstd[:, tiles], ALU.mult).then_inc(sem("ln_shift"), 1)

        def ln_act(act, n, normed, dst, scale, bias):
            act.wait_ge(sem("ln_shift"), going_back(n) + 1)
            for b in (2, 3):
                for t in range(4):
                    c = 4 * b + t
                    last = nc.scalar.activation(normed[:, c, :], bank[b][:, t * P:(t + 1) * P], ACT.Identity,
                                                bias=shift[:, c - 8:c - 7], scale=rstd[:, c:c + 1])
                last.then_inc(sem("ln_normed_act"), 1)
            for b in (2, 3):
                act.wait_ge(sem("ln_back"), going_back(n) * BLOCKS + b + 1)
                nc.scalar.activation(dst[:, 512 * b:512 * b + 512], bank[4 + b][:, :], ACT.Identity,
                                     bias=bias, scale=scale).then_inc(sem("ln_out_act"), 1)

        def ln_out(engine, n, blocks):
            for b in blocks:
                engine.wait_ge(sem("ln_out_dve" if b < 2 else "ln_out_act"), going_back(n) * 2 + b % 2 + 1)

        CLOSE, FAR = slice(0, NEAR), slice(NEAR, N_EXP)

        def s4_dve_angles(dve, G):
            V = nc.vector
            dve.wait_ge(sem("s4_exps"), G + 1)
            V.scalar_tensor_tensor(dta[:, 0, :], exps[:, 1, :], -1.0, exps[:, 0, :], ALU.mult, ALU.mult)
            V.tensor_tensor(dta[:, 1, :], prm[:, 2, :], exps[:, 0, :], ALU.mult).then_inc(sem("s4_dta"), 1)
            dve.wait_ge(sem("s4_dta"), G + 1)
            V.tensor_tensor(mag, dta[:, 0, :].unsqueeze(2).to_broadcast([P, HG, NEAR]),
                            expo[:, 0:NEAR].unsqueeze(1).to_broadcast([P, HG, NEAR]), ALU.mult).then_inc(sem("s4_marg"), 1)

        def s4_dve_reduce(dve, chain, G):
            V = nc.vector
            link = chain.link
            dve.wait_ge(sem("s4_turns"), G + 1)
            for part in (TWO_PI_1, TWO_PI_2, TWO_PI_3):
                link(V.scalar_tensor_tensor(theta, turns, -part, theta, ALU.mult, ALU.add))
            V.tensor_scalar(theta, theta, 3.1415925, -3.1415925, ALU.min, ALU.max).then_inc(sem("s4_theta"), 1)

        def s4_dve_powers(dve, chain, G):
            V = nc.vector
            link = chain.link
            a_im, c_re, c_im = (prm[:, i, :] for i in (2, 3, 4))
            e_are = exps[:, 1, :]
            dve.wait_ge(sem("s4_sin"), G * 3 + 3)
            dve.wait_ge(sem("s4_mag"), G * 2 + 2)
            s0, s1, s2, s3, s4_, s5, s6, s7, cd_re, c2_im, c2_re, cd_im = small
            V.tensor_copy(s0, theta[:, :, ONE])
            V.tensor_tensor(anc_re, mag, cosn[:, :, 0:NEAR], ALU.mult)
            V.tensor_tensor(anc_im, mag, sn[:, :, 0:NEAR], ALU.mult).then_inc(sem("s4_anchors"), 1)
            dve.wait_ge(sem("s4_anchors"), G + 1)
            link(V.scalar_tensor_tensor(s1, mag[:, :, ONE], 1.0, tanh, ALU.add, ALU.mult))
            link(V.tensor_tensor(s1, s1, cosn[:, :, ONE], ALU.mult))
            link(V.scalar_tensor_tensor(s1, s0, -2.0, s1, ALU.mult, ALU.add))
            e_re, e_im = s1, anc_im[:, :, ONE]
            V.tensor_tensor(s2, e_are, e_are, ALU.mult)
            link(V.tensor_tensor(s3, a_im, a_im, ALU.mult))
            link(V.tensor_tensor(s2, s2, s3, ALU.add))
            link(V.reciprocal(s2, s2))
            V.tensor_tensor(s3, e_im, a_im, ALU.mult)
            V.tensor_tensor(s4_, e_re, e_are, ALU.mult)
            V.tensor_tensor(s5, e_im, e_are, ALU.mult)
            link(V.tensor_tensor(s6, e_re, a_im, ALU.mult))
            V.tensor_tensor(s3, s3, s4_, ALU.subtract)
            link(V.scalar_tensor_tensor(s5, s5, -1.0, s6, ALU.mult, ALU.subtract))
            V.scalar_tensor_tensor(s3, s3, 2.0, s2, ALU.mult, ALU.mult)
            link(V.scalar_tensor_tensor(s5, s5, 2.0, s2, ALU.mult, ALU.mult))
            V.tensor_tensor(s4_, c_re, s3, ALU.mult)
            V.tensor_tensor(s6, c_im, s5, ALU.mult)
            V.tensor_tensor(s7, c_re, s5, ALU.mult)
            link(V.tensor_tensor(s0, c_im, s3, ALU.mult))
            V.tensor_tensor(cd_re, s4_, s6, ALU.subtract).then_inc(sem("s4_cd"), 1)
            link(V.tensor_tensor(cd_im, s7, s0, ALU.add))
            dve.wait_ge(sem("s4_cd"), G + 1)
            w_re, w_im = anc_re[:, :, ONE], anc_im[:, :, ONE]
            V.tensor_tensor(s3, cd_re, w_re, ALU.mult)
            V.tensor_tensor(s4_, cd_im, w_im, ALU.mult)
            V.tensor_tensor(s5, cd_re, w_im, ALU.mult)
            link(V.tensor_tensor(s6, cd_im, w_re, ALU.mult))
            V.tensor_tensor(c2_re, s3, s4_, ALU.subtract)
            V.tensor_tensor(c2_im, s5, s6, ALU.add).then_inc(sem("s4_coef"), 1)
            dve.wait_ge(sem("s4_coef"), G + 1)
            V.tensor_tensor(four(pow_re), hi(anc_re), lo(anc_re), ALU.mult)
            link(V.tensor_tensor(four(k_re), hi(anc_im), lo(anc_im), ALU.mult))
            V.tensor_tensor(pow_re, pow_re, k_re, ALU.subtract).then_inc(sem("s4_pow_re"), 1)
            dve.wait_ge(sem("s4_pow_re"), G + 1)
            V.tensor_tensor(k_re, pow_re, c2_re.unsqueeze(2).to_broadcast([P, HG, CHUNK]), ALU.mult).then_inc(sem("s4_k_re"), 1)

        def s4_dve_layer(dve, chain, L, more):
            V = nc.vector
            link = chain.link
            if more:
                s4_dve_angles(dve, L + 1)
            ln_dve_stats(dve, LN_S4 + L)
            dve.wait_ge(sem("s4_layer_in"), L * 64 + 64)
            V.memset(turn_mark[:, 2:3], 0.0)
            dve.wait_ge(sem("ln_aggr"), (LN_S4 + L + 1) * TILES)
            for c in range(TILES):
                last = V.scalar_tensor_tensor(z_tok[:, c, :], bank[c // 4][:, (c % 4) * P:(c % 4 + 1) * P], mean_var[:, c, 0:1],
                                              ln_wb[:, 0, :], ALU.subtract, ALU.mult)
            link(last)
            dve.wait_ge(sem("ln_rstd"), (LN_S4 + L) * 2 + 2)
            for b in range(BLOCKS):
                tiles = slice(4 * b, 4 * b + 4)
                V.tensor_tensor(z_tok[:, tiles, :], z_tok[:, tiles, :],
                                rstd[:, tiles].unsqueeze(2).to_broadcast([P, 4, P]), ALU.mult).then_inc(sem("s4_scaled"), 1)
            tokens = zu[0:CHUNK].rearrange("p h (t half) -> p half t h", half=2)
            for b in range(BLOCKS):
                dve.wait_ge(sem("s4_scaled"), L * BLOCKS + b + 1)
                tiles = slice(4 * b, 4 * b + 4)
                for half in range(2):
                    r = slice(CHUNK * half, CHUNK * half + CHUNK)
                    last = V.tensor_tensor(tokens[:, half, tiles, :], z_tok[r, tiles, :],
                                           ln_wb[r, 1, :].unsqueeze(1).to_broadcast([CHUNK, 4, P]), ALU.add)
            last.then_inc(sem("s4_z"), 1)
            if more:
                s4_dve_reduce(dve, chain, L + 1)
            for k in range(PIECES):
                dve.wait_ge(sem("s4_in_ps"), L * PIECES + k + 1)
                last = V.transpose(glu_sig[:, 512 * k:512 * k + 512], bank[k][:, :])
            link(last)
            dve.wait_ge(sem("s4_phases"), L + 1)
            phi_c, phi_s = cosn[:, :, NEAR:N_EXP], sn[:, :, NEAR:N_EXP]
            in_re, in_im = states[:, :, 0, :], states[:, :, 1, :]
            V.tensor_tensor(b_re, in_re, phi_c, ALU.mult)
            V.tensor_tensor(s_a, in_im, phi_s, ALU.mult)
            V.tensor_tensor(b_im, in_im, phi_c, ALU.mult)
            link(V.tensor_tensor(s_b, in_re, phi_s, ALU.mult))
            V.tensor_tensor(b_re, b_re, s_a, ALU.add)
            link(V.tensor_tensor(b_im, b_im, s_b, ALU.subtract))
            flat = lambda t: t.rearrange("p h c -> p (h c)")
            V.tensor_tensor_scan(flat(s_a), flat(decay), flat(b_re), 0.0, ALU.mult, ALU.add)
            link(V.tensor_tensor_scan(flat(s_b), flat(decay), flat(b_im), 0.0, ALU.mult, ALU.add))
            c1 = CHUNKS - 1
            sa_, sb_, gr, gi = (t[:, :, 0:c1] for t in (s_a, s_b, g_re, g_im))
            V.memset(u_re[:, :, 0], 0.0)
            V.memset(u_im[:, :, 0], 0.0)
            V.tensor_tensor(b_re[:, :, 0:c1], sa_, gr, ALU.mult)
            link(V.tensor_tensor(b_im[:, :, 0:c1], sb_, gi, ALU.mult))
            V.tensor_tensor(u_re[:, :, 1:CHUNKS], b_re[:, :, 0:c1], b_im[:, :, 0:c1], ALU.subtract).then_inc(sem("s4_u_re"), 1)
            V.tensor_tensor(sa_, sa_, gi, ALU.mult)
            link(V.tensor_tensor(sb_, sb_, gr, ALU.mult))
            V.scalar_tensor_tensor(u_im[:, :, 1:CHUNKS], sa_, -1.0, sb_, ALU.mult, ALU.subtract).then_inc(sem("s4_u"), 1)
            if more:
                dve.wait_ge(sem("s4_pow_moved"), L * 128 + 128)
                s4_dve_powers(dve, chain, L + 1)
            dve.wait_ge(sem("s4_y"), L * PIECES + PIECES)
            V.transpose(yT.rearrange("p (c i) -> p i c", i=CHUNK), y_act).then_inc(sem("s4_yT"), 1)
            for b in range(BLOCKS):
                dve.wait_ge(sem("s4_sig"), L * BLOCKS + b + 1)
                sl = slice(512 * b, 512 * b + 512)
                link(V.scalar_tensor_tensor(glu_sig[:, sl], bank[4 + 2 * (b % 2)][:, :], b_out[:, 0:1],
                                            glu_sig[:, sl], ALU.add, ALU.mult))
                V.tensor_tensor(hT[:, sl], hT[:, sl], glu_sig[:, sl], ALU.add).then_inc(sem("s4_h"), 1)

        def s4_pe_layer(pe, L, first):
            T = nc.tensor
            ln_pe_tokens(pe, hT, (lambda b: ln_out(pe, LN_A, (b,))) if first else
                         (lambda b: pe.wait_ge(sem("s4_h"), (L - 1) * BLOCKS + b + 1)))
            pe.wait_ge(sem("s4_k_re"), L + 1)
            pe.wait_ge(sem("s4_k_im"), L + 1)
            for k in range(PIECES):
                T.matmul(bank[4 + k][0:GROUPS, :], sel[:, 0, :], k_re[:, PIECE * k:PIECE * (k + 1), :], start=True, stop=False)
                T.matmul(bank[4 + k][0:GROUPS, :], sel[:, 1, :], k_im[:, PIECE * k:PIECE * (k + 1), :], start=False, stop=True).then_inc(sem("s4_k_ps"), 1)
            pe.wait_ge(sem("s4_k_rows"), L * (PIECES + 1) + 1)
            pe.wait_ge(sem("s4_layer_in"), L * 64 + 64)
            T.matmul(bank[4][0:GROUPS, 0:HG], sel[:, 0, :], small[8], start=True, stop=False)
            T.matmul(bank[4][0:GROUPS, 0:HG], ident[0:GROUPS, 0:GROUPS], skip, start=False, stop=True).then_inc(sem("s4_k_ps"), 1)
            pe.wait_ge(sem("s4_pow_re"), L + 1)
            pe.wait_ge(sem("s4_pow_im"), L + 1)
            pe.sem_inc(sem("turn"), 1)
            for q in range(HG // 2):
                if q >= 4:
                    pe.wait_ge(sem("s4_back"), L * (HG // 2) + q - 3)
                else:
                    pe.wait_ge(sem("s4_k_rows"), L * (PIECES + 1) + (q + 1 if q else PIECES + 1))
                pe.sem_inc(sem("turn"), 1)
                for i in range(4):
                    last = T.transpose(bank[4 + q % 4][0:CHUNK, i * P:(i + 1) * P], (pow_re, pow_im)[i % 2][:, 2 * q + i // 2, :], ident)
                last.then_inc(sem("s4_back_ps"), 1)
            pe.wait_ge(sem("s4_back"), (L + 1) * (HG // 2))
            pe.sem_inc(sem("turn"), 1)
            pe.wait_ge(sem("s4_z"), L + 1)
            pe.sem_inc(sem("turn"), 1)
            for k in range(PIECES):
                for hh in range(PIECE * k, PIECE * (k + 1)):
                    for g in range(GROUPS):
                        last = T.matmul(bank[k][32 * g:32 * g + 32, 2 * MODES * (hh % PIECE):2 * MODES * (hh % PIECE + 1)],
                                        zu[0:CHUNK, HG * g + hh, :], back[:, hh, :, 32 * g:32 * g + 32], start=True, stop=True)
                last.then_inc(sem("s4_in_ps"), 1)
            pe.wait_ge(sem("s4_toep_in"), L * 16 * PIECES + 16 * PIECES)
            pe.wait_ge(sem("s4_pow_moved"), L * 128 + 128)
            pe.wait_ge(sem("s4_u_moved"), L * 128 + 128)
            for k in range(PIECES):
                for hh in range(PIECE * k, PIECE * (k + 1)):
                    for g in range(GROUPS):
                        last = T.matmul(bank[4 + k][32 * g:32 * g + 32, CHUNK * (hh % PIECE):CHUNK * (hh % PIECE + 1)],
                                        zu[:, HG * g + hh, :], tp[:, HG * g + hh, :], start=True, stop=True)
                last.then_inc(sem("s4_y_ps"), 1)
            pe.wait_ge(sem("s4_y_ps"), (L + 1) * PIECES)
            pe.sem_inc(sem("s4_tp_free"), 1)
            pe.wait_ge(sem("s4_yT"), L + 1)
            for b in range(BLOCKS):
                if b >= 2:
                    pe.wait_ge(sem("s4_h"), L * BLOCKS + b - 1)
                rhs = yT[:, 512 * b:512 * b + 512]
                for k in range(2):
                    last = T.matmul(bank[4 + 2 * (b % 2) + k][:, :], w_out[:, k * P:(k + 1) * P], rhs, start=True, stop=True)
                last.then_inc(sem("s4_glu_ps"), 1)

        def s4_act_magnitudes(act, G):
            A = nc.scalar
            act.wait_ge(sem("s4_prm_in"), G * 16 + 16)
            A.activation(exps, prm[:, 0:2, :], ACT.Exp).then_inc(sem("s4_exps"), 1)
            act.wait_ge(sem("s4_dta"), G + 1)
            A.activation(tanh, dta[:, 0, :], ACT.Tanh, scale=0.5)
            act.wait_ge(sem("s4_marg"), G + 1)
            A.activation(mag, mag, ACT.Exp).then_inc(sem("s4_mag"), 1)

        def s4_act_decay(act, G):
            nc.scalar.activation(r_chunk, dta[:, 0, :], ACT.Exp, scale=float(CHUNK)).then_inc(sem("s4_mag"), 1)

        def s4_act_sines(act, G, which, done):
            A = nc.scalar
            act.wait_ge(sem("s4_theta"), G + 1)
            A.activation(sn[:, :, which], theta[:, :, which], ACT.Sin)
            A.activation(turns[:, :, which], theta[:, :, which], ACT.Sin, scale=0.5).then_inc(sem(done), 1)
            act.wait_ge(sem(done), G * 3 + 1)
            A.activation(theta[:, :, which], turns[:, :, which], ACT.Square).then_inc(sem(done), 1)
            act.wait_ge(sem(done), G * 3 + 2)
            A.activation(cosn[:, :, which], theta[:, :, which], ACT.Copy, scale=-2.0, bias=1.0).then_inc(sem(done), 1)

        def s4_act_layer(act, L, more):
            A = nc.scalar
            if more:
                s4_act_magnitudes(act, L + 1)
            for k in range(PIECES):
                act.wait_ge(sem("s4_k_ps"), L * (PIECES + 1) + k + 1)
                src = bank[4 + k][0:GROUPS, :].rearrange("p (a b) -> p a b", a=PIECE)
                A.activation(k_rows[:, PIECE * k:PIECE * (k + 1), 0:CHUNK - 1], src[:, :, 1:CHUNK], ACT.Copy).then_inc(sem("s4_k_rows"), 1)
            act.wait_ge(sem("s4_k_ps"), (L + 1) * (PIECES + 1))
            A.activation(k_rows[:, :, CHUNK - 1], bank[4][0:GROUPS, 0:HG], ACT.Copy).then_inc(sem("s4_k_rows"), 1)
            for q in range(HG // 2):
                act.wait_ge(sem("s4_back_ps"), L * (HG // 2) + q + 1)
                A.activation(back[:, 2 * q:2 * q + 2], bank[4 + q % 4][0:CHUNK, :].rearrange("p (a b c) -> p a b c", a=2, b=2), ACT.Copy).then_inc(sem("s4_back"), 1)
            if more:
                act.wait_ge(sem("s4_phases"), L + 1)
                s4_act_decay(act, L + 1)
            if more:
                s4_act_sines(act, L + 1, CLOSE, "s4_sin")
            act.wait_ge(sem("s4_u"), L + 1)
            if more:
                s4_act_sines(act, L + 1, FAR, "s4_sin_far")
            for k in range(PIECES):
                act.wait_ge(sem("s4_y_ps"), L * PIECES + k + 1)
                A.activation(y_act.rearrange("p i h -> p h i")[:, PIECE * k:PIECE * (k + 1), :],
                             bank[4 + k][:, :].rearrange("p (h i) -> p h i", i=CHUNK)[:, :, ::-1],
                             ACT.Gelu_apprx_tanh).then_inc(sem("s4_y"), 1)
            act.wait_ge(sem("s4_yT"), L + 1)
            for b in range(BLOCKS):
                act.wait_ge(sem("s4_glu_ps"), L * BLOCKS + b + 1)
                A.activation(glu_sig[:, 512 * b:512 * b + 512], bank[5 + 2 * (b % 2)][:, :],
                             ACT.Sigmoid, bias=b_out[:, 1:2]).then_inc(sem("s4_sig"), 1)

        def s4_pool_powers(pool, chain, G):
            G_ = nc.gpsimd
            pool.wait_ge(sem("s4_anchors"), G + 1)
            G_.tensor_tensor(four(pow_im), hi(anc_re), lo(anc_im), ALU.mult)
            chain.link(G_.tensor_tensor(four(k_im), hi(anc_im), lo(anc_re), ALU.mult))
            G_.tensor_tensor(pow_im, pow_im, k_im, ALU.add).then_inc(sem("s4_pow_im"), 1)
            pool.wait_ge(sem("s4_coef"), G + 1)
            pool.wait_ge(sem("s4_pow_im"), G + 1)
            G_.tensor_tensor(k_im, pow_im, small[9].unsqueeze(2).to_broadcast([P, HG, CHUNK]), ALU.mult).then_inc(sem("s4_k_im"), 1)
            pool.wait_ge(sem("s4_sin_far"), G * 3 + 3)
            cc = [P, HG, CHUNKS]
            phi_c, phi_s = cosn[:, :, NEAR:N_EXP], sn[:, :, NEAR:N_EXP]
            c2r, c2i = small[10].unsqueeze(2).to_broadcast(cc), small[9].unsqueeze(2).to_broadcast(cc)
            G_.tensor_tensor(decay[:, :, 1:CHUNKS], r_chunk.unsqueeze(2).to_broadcast([P, HG, CHUNKS - 1]),
                             ones.unsqueeze(1).to_broadcast([P, HG, CHUNKS - 1]), ALU.mult)
            G_.tensor_tensor(g_re, phi_c, c2r, ALU.mult)
            G_.tensor_tensor(g_im, phi_c, c2i, ALU.mult)
            G_.tensor_tensor(g_x, phi_s, c2i, ALU.mult)
            chain.link(G_.tensor_tensor(g_y, phi_s, c2r, ALU.mult))
            G_.tensor_tensor(g_re, g_re, g_x, ALU.subtract)
            G_.tensor_tensor(g_im, g_im, g_y, ALU.add).then_inc(sem("s4_phases"), 1)

        def s4_pool_angles(pool, chain, G):
            G_ = nc.gpsimd
            wide = [P, HG, N_EXP]

            def link(instruction):
                chain.link(instruction)
                pool.sem_inc(sem("turn"), 1)

            pool.wait_ge(sem("s4_dta"), G + 1)
            link(G_.tensor_tensor(theta, dta[:, 1, :].unsqueeze(2).to_broadcast(wide),
                                  expo.unsqueeze(1).to_broadcast(wide), ALU.mult))
            link(G_.tensor_scalar(turns, theta, 1.0 / (2 * math.pi), MAGIC, ALU.mult, ALU.add))
            G_.tensor_scalar(turns, turns, MAGIC, None, ALU.subtract).then_inc(sem("s4_turns"), 1)

        lo = lambda t: t[:, :, 0:LOW].unsqueeze(2).to_broadcast([P, HG, HIGH, LOW])
        hi = lambda t: t[:, :, LOW:NEAR].unsqueeze(3).to_broadcast([P, HG, HIGH, LOW])
        four = lambda t: t.rearrange("p h (a b) -> p h a b", a=HIGH)
        g_x, g_y = (y.rearrange("p a b -> p (a b)")[:, 0:HG * CHUNKS].rearrange("p (h c) -> p h c", c=CHUNKS) for y in (theta, turns))

        def s4_sp_layer(sp, L, first, more):
            whole = (lambda x: x) if isinstance(L, int) else sp.snap
            one, rows, k_out = whole(L + 1), whole((L + 1) * (PIECES + 1)), whole(L * 16 + 16)
            toep_in, h = whole(L * 16 * PIECES), L if first else whole(L * BLOCKS)

            def turn():
                sp.sem_inc(sem("turn"), 1)

            if more:
                sp.wait_ge(sem("s4_coef"), one)
                turn()
                sp.dma_start(prm, dram["prm"][L + 1]).then_inc(sem("s4_prm_in"), 16)
            if not first:
                sp.wait_ge(sem("s4_h"), h)
                turn()
            for dst, name in ((skip, "skip"), (ln_wb, "ln_wb"), (w_out, "w_out"), (b_out, "b_out")):
                sp.dma_start(dst, dram[name][L]).then_inc(sem("s4_layer_in"), 16)
            for name in ("s4_tp_free", "s4_pow_re", "s4_pow_im"):
                sp.wait_ge(sem(name), one)
                turn()
            for ri, src in ((0, pow_re), (1, pow_im)):
                for g in range(GROUPS):
                    at = CHUNK + MODES * ri
                    sp.dma_start(tp[at:at + MODES, HG * g:HG * (g + 1), :], src[32 * g:32 * g + 32]).then_inc(sem("s4_pow_moved"), 16)
            sp.wait_ge(sem("s4_k_rows"), rows)
            turn()
            sp.dma_start(k_pad[:, 0:CHUNK].rearrange("(g h) m -> g h m", g=GROUPS), k_rows).then_inc(sem("s4_k_out"), 16)
            sp.wait_ge(sem("s4_k_out"), k_out)
            turn()
            for g in range(GROUPS):
                src = bass.AP(tensor=k_pad.tensor, offset=g * HG * 2 * CHUNK, ap=[[1, CHUNK], [2 * CHUNK, HG], [1, CHUNK]])
                sp.dma_start(tp[0:CHUNK, HG * g:HG * (g + 1), :], src).then_inc(sem("s4_toep_in"), 16)
            for ri, src, ready in ((0, u_re, "s4_u_re"), (1, u_im, "s4_u")):
                sp.wait_ge(sem(ready), one)
                turn()
                for g in range(GROUPS):
                    at = CHUNK + MODES * ri
                    sp.dma_start(zu[at:at + MODES, HG * g:HG * (g + 1), :], src[32 * g:32 * g + 32]).then_inc(sem("s4_u_moved"), 16)

        def moe_act(act):
            A = nc.scalar
            ln_act(act, LN_B, moe_norm, hT, one_plus[:, 4:5], mod[:, 3:4])
            act.wait_ge(sem("moe_w1_in"), 16)
            for e in range(EXPERTS):
                A.activation(w1_high_s[:, e, :], w1_low[:, e, :], ACT.Copy).then_inc(sem("moe_w1_high"), 1)
            act.wait_ge(sem("moe_shifted"), 1)
            A.activation(weight, logit, ACT.Exp).then_inc(sem("moe_exp"), 1)
            act.wait_ge(sem("moe_w2_in"), 16)
            for e in range(EXPERTS):
                A.activation(w2_high_s[:, e], w2_low[:, e], ACT.Copy).then_inc(sem("moe_w2_high"), 1)

            def high(b, e):
                act.wait_ge(sem("moe_raw"), b * EXPERTS + e + 1)
                A.activation(x_high_s[:, e % AHEAD, :], x_low[:, e % AHEAD, :], ACT.Copy).then_inc(sem("moe_x_high"), 1)

            def block_of_tokens(b, more):
                for e in range(AHEAD, EXPERTS):
                    high(b, e)
                for m in range(HID_CHUNKS):
                    act.wait_ge(sem("moe_h"), b * HID_CHUNKS + m + 1)
                    A.activation(hid_low[:, m, :], bank[m][:, :], ACT.Gelu)
                    A.activation(hid_high_s[:, m, :], bank[m][:, :], ACT.Gelu).then_inc(sem("moe_hid_high"), 1)
                if more:
                    for e in range(AHEAD):
                        high(b + 1, e)

            for e in range(AHEAD):
                high(0, e)
            with act.Fori(0, BLOCKS - 1) as b:
                block_of_tokens(b, more=True)
            block_of_tokens(BLOCKS - 1, more=False)

        def moe_dve(dve, link):
            V = nc.vector
            ln_dve(dve, LN_B, moe_norm, hT, one_plus[:, 4:5], mod[:, 3:4])
            link(V.memset(fresh, 1.0))
            g3 = lambda t: t.rearrange("p c (r e) -> p (c r) e", r=ROUTERS)
            flat = lambda t: t.rearrange("p c e -> p (c e)")
            groups = TILES * ROUTERS
            wide = [P, groups, EXPERTS]
            V.memset(g3(fresh)[:, :, 0:1], 0.0)
            for b in range(BLOCKS):
                dve.wait_ge(sem("moe_addr_ps"), b + 1)
                V.tensor_copy(addr[:, 512 * b:512 * b + 512], bank[b][0:ADDR, :]).then_inc(sem("moe_addr"), 1)
            half = TILES // 2
            for i in range(2):
                dve.wait_ge(sem("moe_logit_ps"), i + 1)
                link(V.tensor_copy(logit[:, half * i:half * (i + 1), :],
                                   bank[4 + i][:, 0:half * 36].rearrange("p (c e) -> p c e", e=36)))
            for k in range(groups):
                last = V.max(top8[:, k, :], g3(logit)[:, k, :])
            link(last)
            third = top8[:, :, 2:3].to_broadcast(wide)
            V.tensor_tensor(g3(above), g3(logit), third, ALU.is_gt)
            link(V.tensor_tensor(g3(equal), g3(logit), third, ALU.is_equal))
            V.tensor_tensor_scan(flat(ranks), flat(fresh), flat(equal), 0.0, ALU.mult, ALU.add)
            V.tensor_tensor(g3(logit), g3(logit), top8[:, :, 0:1].to_broadcast(wide), ALU.subtract).then_inc(sem("moe_shifted"), 1)
            link(V.tensor_reduce(room, g3(above), AX.X, ALU.add))
            link(V.tensor_scalar(room, room, -1.0, float(TOP), ALU.mult, ALU.add))
            link(V.tensor_tensor(g3(ranks), g3(ranks), room.unsqueeze(2).to_broadcast(wide), ALU.is_le))
            link(V.tensor_tensor(equal, equal, ranks, ALU.mult))
            link(V.tensor_tensor(above, above, equal, ALU.add))
            dve.wait_ge(sem("moe_exp"), 1)
            link(V.tensor_tensor(weight, weight, above, ALU.mult))
            link(V.tensor_reduce(total, g3(weight), AX.X, ALU.add))
            link(V.reciprocal(total, total))
            V.tensor_tensor(g3(weight), g3(weight), total.unsqueeze(2).to_broadcast(wide), ALU.mult).then_inc(sem("moe_weight"), 1)
            for b in range(BLOCKS):
                dve.wait_ge(sem("moe_wT_ps"), b + 1)
                V.tensor_copy(weightT[:, 512 * b:512 * b + 512], bank[b][0:36, :]).then_inc(sem("moe_wT"), 1)
            ln_out(dve, LN_B, range(BLOCKS))

        def moe_dve_blocks(dve, chain):
            V = nc.vector
            for name, n in (("moe_share_free1", 1), ("moe_share_free2", 1), ("moe_y_read", 2), ("moe_x", 1)):
                dve.sem_inc(sem(name), n)

            def raw(b, e):
                n = b * EXPERTS + e
                if e in (0, AHEAD):
                    dve.wait_ge(sem("moe_share_in1" if e else "moe_share_in0"), b * 16 + 16)
                if not isinstance(n, int) or n >= AHEAD:
                    dve.wait_ge(sem("moe_x_used"), n - AHEAD + 1)
                cols = slice(512 * b, 512 * b + 512) if isinstance(b, int) else bass.ts(b, 512)
                V.tensor_tensor(x_low[:, e % AHEAD, :], hT[:, cols], share1[:, e, :], ALU.mult).then_inc(sem("moe_raw"), 1)

            def low(b, e):
                dve.wait_ge(sem("moe_x_high"), b * EXPERTS + e + 1)
                V.tensor_tensor(x_low_s[:, e % AHEAD, :], x_low[:, e % AHEAD, :], x_high_s[:, e % AHEAD, :],
                                ALU.subtract).then_inc(sem("moe_x_low"), 1)

            def block_of_tokens(b, more):
                for e in range(AHEAD, EXPERTS):
                    raw(b, e)
                    low(b, e - 1)
                low(b, EXPERTS - 1)
                dve.wait_ge(sem("moe_x_low"), (b + 1) * EXPERTS)
                dve.sem_inc(sem("moe_share_free1"), 1)
                for m in range(HID_CHUNKS):
                    dve.wait_ge(sem("moe_hid_high"), b * HID_CHUNKS + m + 1)
                    V.tensor_tensor(hid_low_s[:, m, :], hid_low[:, m, :], hid_high_s[:, m, :],
                                    ALU.subtract).then_inc(sem("moe_hid_low"), 1)
                dve.wait_ge(sem("moe_share_in2"), b * 16 + 16)
                for e in range(EXPERTS):
                    dve.wait_ge(sem("moe_y_ps"), b * EXPERTS + e + 1)
                    part = y_acc if e == 0 else y_part[e % 2]
                    V.tensor_tensor(part, bank[4 + e % 2][:, :], share2[:, e, :], ALU.mult).then_inc(sem("moe_y_read"), 1)
                    if e:
                        dve.wait_ge(sem("moe_y_read"), b * EXPERTS + e + 3)
                        if e > 1:
                            chain.wait()
                        chain.mark(V.tensor_tensor(y_acc, y_acc, part, ALU.add))
                    if more and e >= EXPERTS - AHEAD - 1 and e < EXPERTS - 1:
                        k = e - (EXPERTS - AHEAD - 1)
                        raw(b + 1, k)
                        if k:
                            low(b + 1, k - 1)
                dve.sem_inc(sem("moe_share_free2"), 1)
                chain.wait()
                dve.wait_ge(sem("moe_b2_ps"), b + 1)
                chain.link(V.tensor_tensor(y_acc, y_acc, bank[6][:, :], ALU.add))
                cols = slice(512 * b, 512 * b + 512) if isinstance(b, int) else bass.ts(b, 512)
                V.scalar_tensor_tensor(xT[:, cols], y_acc, gate[:, 5:6], xT[:, cols],
                                       ALU.mult, ALU.add).then_inc(sem("moe_x"), 1)
                dve.wait_ge(sem("moe_x"), b + 2)

            raw(0, 0)
            for e in range(1, AHEAD):
                raw(0, e)
                low(0, e - 1)
            with dve.Fori(0, BLOCKS - 1) as b:
                chain.body(b, EXPERTS)
                block_of_tokens(b, more=True)
            chain.leave(BLOCKS - 1)
            block_of_tokens(BLOCKS - 1, more=False)

        def moe_pe(pe):
            T = nc.tensor
            pe.wait_ge(sem("x_s4"), BLOCKS)
            ln_pe_tokens(pe, xT)
            ln_pe_back(pe, LN_B, moe_norm)
            pe.wait_ge(sem("moe_consts_in"), 48)
            for b in range(BLOCKS):
                ln_out(pe, LN_B, (b,))
                T.matmul(bank[b][0:ADDR, :], pw_sb, hT[:, 512 * b:512 * b + 512], start=True, stop=True).then_inc(sem("moe_addr_ps"), 1)
            half = TILES // 2
            for c in range(TILES):
                pe.wait_ge(sem("moe_addr"), c // 4 + 1)
                last = T.matmul(bank[4 + c // half][:, 36 * (c % half):36 * (c % half) + 36],
                                addr[:, c * P:(c + 1) * P], u_sb, start=True, stop=True)
                if c % half == half - 1:
                    last.then_inc(sem("moe_logit_ps"), 1)
            pe.wait_ge(sem("moe_weight"), 1)
            for c in range(TILES):
                last = T.transpose(bank[c // 4][0:36, (c % 4) * P:(c % 4 + 1) * P], weight[:, c, :], ident)
                if c % 4 == 3:
                    last.then_inc(sem("moe_wT_ps"), 1)
            pe.wait_ge(sem("moe_wT"), BLOCKS)
            def thrice(dst, w_large, w_small, x_large, x_small, first, last):
                T.matmul(dst, w_small, x_large, start=first, stop=False)
                T.matmul(dst, w_large, x_small, start=False, stop=False)
                return T.matmul(dst, w_large, x_large, start=False, stop=last)

            pe.wait_ge(sem("moe_w1_low"), EXPERTS)
            with pe.Fori(0, BLOCKS) as b:
                for e in range(EXPERTS):
                    pe.wait_ge(sem("moe_x_low"), b * EXPERTS + e + 1)
                    for m in range(HID_CHUNKS):
                        cols = slice(m * P, (m + 1) * P)
                        last = thrice(bank[m][:, :], w1_high_s[:, e, cols], w1_low_s[:, e, cols],
                                      x_high_s[:, e % AHEAD, :], x_low_s[:, e % AHEAD, :], e == 0, e == EXPERTS - 1)
                        if e == EXPERTS - 1:
                            last.then_inc(sem("moe_h"), 1)
                    if e == EXPERTS - 1:
                        pe.wait_ge(sem("moe_h"), b * HID_CHUNKS + HID_CHUNKS)
                        pe.sem_inc(sem("moe_x_used"), 1)
                    else:
                        last.then_inc(sem("moe_x_used"), 1)
                pe.wait_ge(sem("moe_x"), b + 1)
                T.matmul(bank[6][:, :], b2_sb, weightT[0:EXPERTS, bass.ts(b, 512)], start=True, stop=True).then_inc(sem("moe_b2_ps"), 1)
                pe.wait_ge(sem("moe_w2_low"), EXPERTS)

                def output(e, m):
                    return thrice(bank[4 + e % 2][:, :], w2_high_s[:, e, m, :], w2_low_s[:, e, m, :],
                                  hid_high_s[:, m, :], hid_low_s[:, m, :], m == 0, m == HID_CHUNKS - 1)

                pe.wait_ge(sem("moe_y_read"), b * EXPERTS + 2)
                for m in range(HID_CHUNKS):
                    pe.wait_ge(sem("moe_hid_low"), b * HID_CHUNKS + m + 1)
                    for e in range(2):
                        last = output(e, m)
                        if m == HID_CHUNKS - 1:
                            last.then_inc(sem("moe_y_ps"), 1)
                for e in range(2, EXPERTS):
                    pe.wait_ge(sem("moe_y_read"), b * EXPERTS + e + 1)
                    for m in range(HID_CHUNKS):
                        last = output(e, m)
                    last.then_inc(sem("moe_y_ps"), 1)

        def gla_act(act):
            A = nc.scalar
            ln_act(act, LN_C, gla_norm, hT, one_plus[:, 7:8], mod[:, 6:7])
            for k in range(8):
                act.wait_ge(sem("gla_max"), k + 1)
                for i in range(4):
                    c, j = 2 * k + i // 2, i % 2
                    last = A.activation(soft[:, c, j, :], bank[k][:, i * P:(i + 1) * P], ACT.Exp,
                                        bias=neg_max[:, c, j:j + 1], accum_out=soft_sum[:, c, j:j + 1])
                last.then_inc(sem("gla_exp"), 1)
            for b in range(BLOCKS):
                act.wait_ge(sem("gla_T_ps"), 2 * b + 2)
                sl = slice(512 * b, 512 * b + 512)
                A.activation(keepT[:, sl], bank[2 * b % 8 + 1][:, :], ACT.Copy)
                A.activation(kT[:, sl], bank[2 * b % 8 + 1][:, :], ACT.Copy, scale=-1.0, bias=1.0).then_inc(sem("gla_k"), 1)

        def gla_dve(dve, link):
            V = nc.vector
            for name in ("ff_wqkv_free", "ff_w_free", "ff_tables_free"):
                dve.sem_inc(sem(name), 1)
            ln_dve(dve, LN_C, gla_norm, hT, one_plus[:, 7:8], mod[:, 6:7])
            for k in range(8):
                dve.wait_ge(sem("gla_logit_ps"), k + 1)
                V.tensor_reduce(neg_max[:, 2 * k:2 * k + 2, :].rearrange("p c j -> p (c j)"),
                                bank[k][:, :].rearrange("p (i d) -> p i d", i=4), AX.X, ALU.max,
                                negate=True).then_inc(sem("gla_max"), 1)
            for k in range(8):
                dve.wait_ge(sem("gla_exp"), k + 1)
                two = slice(2 * k, 2 * k + 2)
                link(V.reciprocal(soft_sum[:, two, :], soft_sum[:, two, :]))
                link(V.tensor_scalar(soft_sum[:, two, 0:1], soft_sum[:, two, 0:1], LIN_DIM ** -0.5, None, ALU.mult))
                V.tensor_tensor(soft[:, two].rearrange("p c j d -> p (c j) d"), soft[:, two].rearrange("p c j d -> p (c j) d"),
                                soft_sum[:, two, :].rearrange("p c j -> p (c j)").unsqueeze(2).to_broadcast([P, 4, P]),
                                ALU.mult).then_inc(sem("gla_soft"), 1)
            for b in range(BLOCKS):
                dve.wait_ge(sem("gla_T_ps"), 2 * b + 1)
                V.tensor_copy(qT[:, 512 * b:512 * b + 512], bank[2 * b % 8][:, :]).then_inc(sem("gla_q"), 1)
            dve.wait_ge(sem("gla_k"), BLOCKS)
            for v in range(LIN_DIM):
                i = v % 2
                for b in range(BLOCKS):
                    dve.wait_ge(sem("gla_v_ps"), BLOCKS * v + b + 1)
                    sl = slice(512 * b, 512 * b + 512)
                    V.tensor_tensor(kv[i][:, sl], bank[b][:, :], kT[:, sl], ALU.mult).then_inc(sem("gla_kv"), 1)
                dve.wait_ge(sem("gla_kv"), BLOCKS * (v + 1))
                if v >= 2:
                    dve.wait_ge(sem("gla_read"), v - 1)
                V.tensor_tensor_scan(state[i], keepT, kv[i], 0.0, ALU.mult, ALU.add).then_inc(sem("gla_state"), 1)
            for b in range(BLOCKS):
                dve.wait_ge(sem("gla_o_ps"), b + 1)
                sl = slice(512 * b, 512 * b + 512)
                V.scalar_tensor_tensor(xT[:, sl], bank[4 + b][:, :], gate[:, 8:9], xT[:, sl], ALU.mult, ALU.add).then_inc(sem("gla_x"), 1)

        def gla_pe(pe):
            T = nc.tensor
            pe.wait_ge(sem("moe_x"), BLOCKS + 1)
            ln_pe_tokens(pe, xT)
            ln_pe_back(pe, LN_C, gla_norm)
            pe.wait_ge(sem("gla_w_in"), 48)
            ln_out(pe, LN_C, range(BLOCKS))
            for c in range(TILES):
                last = T.matmul(bank[c // 2][:, 256 * (c % 2):256 * (c % 2) + 256], hT[:, c * P:(c + 1) * P], wqf_sb, start=True, stop=True)
                if c % 2:
                    last.then_inc(sem("gla_logit_ps"), 1)
            pe.wait_ge(sem("gla_exp"), 8)
            for b in range(BLOCKS):
                pe.wait_ge(sem("gla_soft"), 2 * b + 2)
                for j in range(2):
                    for t in range(4):
                        last = T.transpose(bank[2 * b + j][:, t * P:(t + 1) * P], soft[:, 4 * b + t, j, :], ident)
                    last.then_inc(sem("gla_T_ps"), 1)

            def values(v):
                for b in range(BLOCKS):
                    if v:
                        pe.wait_ge(sem("gla_kv"), BLOCKS * (v - 1) + b + 1)
                    T.matmul(bank[b][:, :], wi_sb[:, v, :], hT[:, 512 * b:512 * b + 512], start=True, stop=True).then_inc(sem("gla_v_ps"), 1)

            pe.wait_ge(sem("gla_q"), BLOCKS)
            pe.wait_ge(sem("gla_k"), BLOCKS)
            values(0)
            for v in range(LIN_DIM):
                if v + 1 < LIN_DIM:
                    values(v + 1)
                pe.wait_ge(sem("gla_read"), v + 1)
                for b in range(BLOCKS):
                    last = T.matmul(bank[4 + b][:, :], wo8_sb[:, v, :], read[v % 2][:, 512 * b:512 * b + 512],
                                    start=(v == 0), stop=(v == LIN_DIM - 1))
                    if v == LIN_DIM - 1:
                        last.then_inc(sem("gla_o_ps"), 1)
                if v < LIN_DIM - 1:
                    last.then_inc(sem("gla_read_used"), 1)

        PROJECTED = ((0, 1, 2), (3, 6, 7))
        FF_BANKS = ((0, 1), (2, 3), (6, 7))

        def ff_act(act):
            A = nc.scalar
            ln_act(act, LN_D, ff_norm, hT, one_plus[:, 10:11], mod[:, 9:10])
            with act.Fori(0, DEPTH) as L:
                for c in range(TILES + 1):
                    if c < TILES:
                        q, k, v = PROJECTED[c % 2]
                        act.wait_ge(sem("ff_qk_ps"), L * TILES + c + 1)
                        if c >= 2:
                            act.wait_ge(sem("ff_norm2"), L * TILES + c - 1)
                        A.activation(squares[:, 2 * (c % 2)], bank[q][:, :], ACT.Square).then_inc(sem("ff_sq"), 1)
                        A.activation(squares[:, 2 * (c % 2) + 1], bank[k][:, :], ACT.Square).then_inc(sem("ff_sq"), 1)
                    if c:
                        act.wait_ge(sem("ff_norm2"), L * TILES + c)
                        A.activation(norms[:, c - 1], norms[:, c - 1], ACT.Sqrt).then_inc(sem("ff_norm"), 1)
                    if c < TILES:
                        act.wait_ge(sem("ff_v_ps"), L * TILES + c + 1)
                        A.activation(v_low[:, c, :].rearrange("p (a b) -> p a b", a=4),
                                     bank[v][HEAD_DIM:P, :].rearrange("p (a b) -> p a b", a=4)[:, :, 0:HEAD_DIM], ACT.Copy)
                        A.activation(v_tok[:, c, :], bank[v][:, :], ACT.Copy).then_inc(sem("ff_v"), 1)
                    if c:
                        for name, dst, bk in (("q", qhT, 4), ("k", khT, 5)):
                            act.wait_ge(sem(f"ff_{name}T_ps"), L * TILES + c)
                            A.activation(dst[:, :, (c - 1) * P:c * P], bank[bk][:, :].rearrange("p (j t) -> p j t", j=4),
                                         ACT.Copy).then_inc(sem(f"ff_{name}T"), 1)

                def exponentials(c):
                    act.wait_ge(sem("at_bias"), L * TILES + c + 1)
                    first = WINDOW if c == 0 else 0
                    for h in range(HEADS):
                        i = HEADS * (c % 2) + h
                        A.activation(scores[:, i, first:KEYS], scores[:, i, first:KEYS], ACT.Exp,
                                     scale=row_scale[:, c % 2, h:h + 1], bias=row_bias[:, c % 2, h:h + 1],
                                     accum_out=row_sum[:, c % 2, h:h + 1]).then_inc(sem("at_exp"), 1)

                exponentials(0)
                for c in range(TILES):
                    if c + 1 < TILES:
                        exponentials(c + 1)
                    act.wait_ge(sem("at_PT_ps"), L * 3 * TILES + 3 * c + 3)
                    A.activation(probsT[:, 4:8, :], bank[4][:, :].rearrange("p (a b) -> p a b", a=4), ACT.Copy).then_inc(sem("at_PT_act"), 1)
                    act.wait_ge(sem("at_o_ps"), L * TILES + c + 1)
                    if c % 4 == 0 and c:
                        act.wait_ge(sem("at_wo_ps"), L * BLOCKS + c // 4)
                    A.activation(oT[0:HEAD_DIM, :, (c % 4) * P:(c % 4 + 1) * P], bank[6][0:HEAD_DIM, :].rearrange("p (j t) -> p j t", j=4),
                                 ACT.Copy).then_inc(sem("at_o_even"), 1)
                ln_act(act, LN_FF + L, ff_norm, nT, cols[:, 7:8], cols[:, 8:9])
                n = len(FF_CHUNKS)
                for b in range(BLOCKS):
                    for i, (at, size) in enumerate(FF_CHUNKS):
                        k = n * b + i
                        act.wait_ge(sem("ff_ag_ps"), L * n * BLOCKS + k + 1)
                        if b:
                            act.wait_ge(sem("ff_act"), L * n * BLOCKS + k - n + 1)
                        A.activation(ff_g[0:size, i, :], bank[FF_BANKS[i][1]][0:size, :], ACT.Gelu,
                                     bias=cols[0:size, 3 + i:4 + i]).then_inc(sem("ff_gelu"), 1)

        def ff_pool_tables(pool, L):
            pool.wait_ge(sem("ff_wqkv_in"), L * 48 + 48)
            for i in range(4):
                row = qk_rows[:, i, :].unsqueeze(1).to_broadcast([P, TILES, HEAD_DIM])
                last = nc.gpsimd.tensor_tensor(scaled[:, i], scaled[:, i], row, ALU.mult)
            last.then_inc(sem("ff_tables"), 1)

        def ff_pool_layer(pool, chain, L):
            for c in range(TILES + 1):
                if c:
                    pool.wait_ge(sem("ff_inv"), L * TILES + c)
                    chain.wait()
                    k8 = k_rot[:, (c - 1) % 2].rearrange("p (h d) -> p h d", h=HEADS)
                    nc.gpsimd.tensor_tensor(k8, k8, inv_norm[:, c - 1, 1, :].unsqueeze(2).to_broadcast([P, HEADS, HEAD_DIM]),
                                            ALU.mult).then_inc(sem("ff_k"), 1)
                if c < TILES:
                    i = c % 2
                    pool.wait_ge(sem("ff_rot"), L * 2 * TILES + 2 * c + 1)
                    nc.gpsimd.tensor_tensor(q_rot[:, i], q_rot[:, i], rot_tmp[:, 2 * i], ALU.add).then_inc(sem("ff_q"), 1)
                    pool.wait_ge(sem("ff_rot"), L * 2 * TILES + 2 * c + 2)
                    chain.mark(nc.gpsimd.tensor_tensor(k_rot[:, i], k_rot[:, i], rot_tmp[:, 2 * i + 1], ALU.add))
            for c in range(TILES):
                pool.wait_ge(sem("at_inv"), L * TILES + c + 1)
                if c >= 2:
                    pool.wait_ge(sem("at_PT_ps"), L * 3 * TILES + 3 * (c - 1))
                two = slice(HEADS * (c % 2), HEADS * (c % 2 + 1))
                inv = lambda n: row_inv[:, c % 2].unsqueeze(2).to_broadcast([P, HEADS, n])
                if c:
                    nc.gpsimd.tensor_tensor(probs_before.rearrange("p (h j) -> p h j", j=WINDOW)[:, two],
                                            scores[:, two, 0:WINDOW], inv(WINDOW), ALU.mult)
                nc.gpsimd.tensor_tensor(probs_own[:, two], scores[:, two, WINDOW:KEYS], inv(P),
                                        ALU.mult).then_inc(sem("at_P"), 1)
            ln_pool(pool, LN_FF + L, shared=True)

        def ff_dve(dve, chain):
            V = nc.vector
            link = chain.link
            ln_dve(dve, LN_D, ff_norm, hT, one_plus[:, 10:11], mod[:, 9:10])
            dve.wait_ge(sem("ff_consts_in"), 16)
            ln_out(dve, LN_D, range(BLOCKS))

            def shift(name):
                V.memset(sT[HEAD_DIM:P, 0:1], 0.0)
                V.tensor_copy(sT[0:HEAD_DIM, :], hT[0:HEAD_DIM, :])
                V.tensor_copy(sT[HEAD_DIM:P, 1:N_TOK], hT[HEAD_DIM:P, 0:N_TOK - 1]).then_inc(sem(name), 1)

            with dve.Fori(0, DEPTH) as L:
                chain.body(L, FF_DVE_LINKS)
                shift("ff_s")
                dve.wait_ge(sem("ff_tables"), L + 1)
                for c in range(TILES + 1):
                    i = c % 2
                    for j, dst in ((0, q_rot), (1, k_rot)):
                        if c < TILES:
                            dve.wait_ge(sem("ff_sq"), L * 2 * TILES + 2 * c + j + 1)
                            if c >= 2:
                                dve.wait_ge(sem("ff_qT_ps" if j == 0 else "ff_kT_ps"), L * TILES + c - 1)
                            src = bank[PROJECTED[i][j]]
                            row = scaled[:, 2 * j, c, :].unsqueeze(1).to_broadcast([P, HEADS, HEAD_DIM])
                            V.tensor_tensor(dst[:, i].rearrange("p (h d) -> p h d", h=HEADS),
                                            src[:, :].rearrange("p (h d) -> p h d", h=HEADS), row, ALU.mult)
                            row = scaled[:, 2 * j + 1, c, :].rearrange("p (s d) -> p s d", s=2).unsqueeze(1).to_broadcast([P, HEADS, 2, HEAD_DIM // 2])
                            V.tensor_tensor(rot_tmp[:, 2 * i + j].rearrange("p (h s d) -> p h s d", h=HEADS, s=2),
                                            src[:, :].rearrange("p (h s d) -> p h s d", h=HEADS, s=2)[:, :, ::-1, :],
                                            row, ALU.mult).then_inc(sem("ff_rot"), 1)
                        if j == 1 and c:
                            dve.wait_ge(sem("ff_norm"), L * TILES + c)
                            V.reciprocal(inv_norm[:, c - 1], norms[:, c - 1]).then_inc(sem("ff_inv"), 1)
                    if c < TILES:
                        link(V.tensor_reduce(norms[:, c].rearrange("p j h -> p (j h)"),
                                             squares[:, 2 * i:2 * i + 2].rearrange("p j (h d) -> p (j h) d", h=HEADS), AX.X, ALU.add))
                        V.tensor_scalar(norms[:, c], norms[:, c], 1e-24, None, ALU.max).then_inc(sem("ff_norm2"), 1)
                dve.wait_ge(sem("ff_v"), L * TILES + TILES)
                dve.wait_ge(sem("ff_inv"), L * TILES + TILES)
                dve.sem_inc(sem("ff_wqkv_free"), 1)

                def masked(c, ks):
                    i = c % 2
                    first = WINDOW if c == 0 else 0
                    if c >= 2:
                        dve.wait_ge(sem("at_P"), L * TILES + c - 1)
                    for k in ks:
                        dve.wait_ge(sem("at_s_ps"), L * 4 * TILES + 4 * c + k + 1)
                        s2 = bank[k][:, 0:2 * KEYS].rearrange("p (h j) -> p h j", h=2)
                        h0 = HEADS * i + 4 * (k // 2) + k % 2
                        V.tensor_tensor(scores[:, h0:h0 + 3:2, first:KEYS], s2[:, :, first:KEYS],
                                        mask_sb[:, first:KEYS].unsqueeze(1).to_broadcast([P, 2, KEYS - first]),
                                        ALU.add).then_inc(sem("at_s"), 1)

                def maxima(c):
                    i = c % 2
                    first = WINDOW if c == 0 else 0
                    V.tensor_scalar(row_scale[:, i], inv_norm[:, c, 0, :], QK_SCALE, None, ALU.mult)
                    dve.wait_ge(sem("at_s"), L * 4 * TILES + 4 * c + 4)
                    link(V.tensor_reduce(row_max[:, i], scores[:, HEADS * i:HEADS * (i + 1), first:KEYS], AX.X, ALU.max))
                    V.scalar_tensor_tensor(row_bias[:, i], row_max[:, i], -1.0, row_scale[:, i], ALU.mult, ALU.mult).then_inc(sem("at_bias"), 1)

                def inverse_sums(c):
                    dve.wait_ge(sem("at_exp"), L * HEADS * TILES + HEADS * (c + 1))
                    if c >= 2:
                        dve.wait_ge(sem("at_P"), L * TILES + c - 1)
                    V.reciprocal(row_inv[:, c % 2], row_sum[:, c % 2]).then_inc(sem("at_inv"), 1)

                def attended(b):
                    dve.wait_ge(sem("at_wo_ps"), L * BLOCKS + b + 1)
                    sl = slice(512 * b, 512 * b + 512)
                    V.tensor_tensor(hT[:, sl], hT[:, sl], bank[5][:, :], ALU.add).then_inc(sem("at_h"), 1)

                masked(0, range(4))
                maxima(0)
                masked(1, range(4))
                maxima(1)
                inverse_sums(0)
                for c in range(TILES):
                    if c + 2 < TILES:
                        masked(c + 2, (0, 1))
                    for k, bk, to in ((0, 4, 0), (1, 5, 8)):
                        dve.wait_ge(sem("at_PT_ps"), L * 3 * TILES + 3 * c + k + 1)
                        V.tensor_copy(probsT[:, to:to + 4, :], bank[bk][:, :].rearrange("p (a b) -> p a b", a=4)).then_inc(sem("at_PT_dve"), 1)
                    if c + 2 < TILES:
                        masked(c + 2, (2, 3))
                    if c + 1 < TILES:
                        inverse_sums(c + 1)
                    if c + 2 < TILES:
                        maxima(c + 2)
                    dve.wait_ge(sem("at_o_ps"), L * TILES + c + 1)
                    if c % 4 == 0 and c:
                        dve.wait_ge(sem("at_wo_ps"), L * BLOCKS + c // 4)
                    V.tensor_copy(oT[HEAD_DIM:P, :, (c % 4) * P:(c % 4 + 1) * P],
                                  bank[7][HEAD_DIM:P, :].rearrange("p (j t) -> p j t", j=4)).then_inc(sem("at_o_odd"), 1)
                    if c % 4 == 0 and c:
                        attended(c // 4 - 1)
                attended(BLOCKS - 1)
                dve.wait_ge(sem("at_h"), L * BLOCKS + BLOCKS)
                dve.wait_ge(sem("at_o_even"), L * TILES + TILES)
                dve.sem_inc(sem("ff_tables_free"), 1)
                shift("ff_s2")
                ln_dve(dve, LN_FF + L, ff_norm, nT, cols[:, 7:8], cols[:, 8:9])
                n = len(FF_CHUNKS)

                def fed(b):
                    dve.wait_ge(sem("ff_y_ps"), L * BLOCKS + b + 1)
                    sl = slice(512 * b, 512 * b + 512)
                    V.scalar_tensor_tensor(hT[:, sl], bank[4 + b % 2][:, :], cols[:, 6:7], hT[:, sl], ALU.add, ALU.add).then_inc(sem("ff_x"), 1)

                for b in range(BLOCKS):
                    for i, (at, size) in enumerate(FF_CHUNKS):
                        k = n * b + i
                        dve.wait_ge(sem("ff_gelu"), L * n * BLOCKS + k + 1)
                        V.scalar_tensor_tensor(ff_h[0:size, n * (b % 2) + i, :], bank[FF_BANKS[i][0]][0:size, :], cols[0:size, i:i + 1],
                                               ff_g[0:size, i, :], ALU.add, ALU.mult).then_inc(sem("ff_act"), 1)
                        if i == 0 and b:
                            fed(b - 1)
                fed(BLOCKS - 1)
                dve.wait_ge(sem("ff_x"), L * BLOCKS + BLOCKS)
                dve.sem_inc(sem("ff_w_free"), 1)
            chain.leave(DEPTH)
            for b in range(BLOCKS):
                sl = slice(512 * b, 512 * b + 512)
                V.scalar_tensor_tensor(xT[:, sl], hT[:, sl], gate[:, 11:12], xT[:, sl], ALU.mult, ALU.add).then_inc(sem("x_ff"), 1)

        def ff_pe(pe):
            T = nc.tensor
            pe.wait_ge(sem("gla_x"), BLOCKS)
            ln_pe_tokens(pe, xT)
            ln_pe_back(pe, LN_D, ff_norm)
            ln_out(pe, LN_D, range(BLOCKS))
            with pe.Fori(0, DEPTH) as L:
                pe.wait_ge(sem("ff_s"), L + 1)
                pe.wait_ge(sem("ff_wqkv_in"), L * 48 + 48)

                def project(c):
                    q, k, v = PROJECTED[c % 2]
                    if c >= 2:
                        pe.wait_ge(sem("ff_rot"), L * 2 * TILES + 2 * (c - 1))
                        pe.wait_ge(sem("ff_sq"), L * 2 * TILES + 2 * (c - 1))
                    x = sT[:, c * P:(c + 1) * P]
                    T.matmul(bank[q][:, :], x, wqkv_sb[:, 0:512], start=True, stop=True)
                    T.matmul(bank[k][:, :], x, wqkv_sb[:, 512:1024], start=True, stop=True).then_inc(sem("ff_qk_ps"), 1)
                    if c >= 2:
                        pe.wait_ge(sem("ff_v"), L * TILES + c - 1)
                    T.matmul(bank[v][:, :], x, wqkv_sb[:, 1024:1536], start=True, stop=True).then_inc(sem("ff_v_ps"), 1)

                project(0)
                for c in range(TILES + 1):
                    if c + 1 < TILES:
                        project(c + 1)
                    if c:
                        for name, src, bk in (("q", q_rot, 4), ("k", k_rot, 5)):
                            pe.wait_ge(sem("ff_" + name), L * TILES + c)
                            if c >= 2:
                                pe.wait_ge(sem(f"ff_{name}T"), L * TILES + c - 1)
                            for j in range(4):
                                last = T.transpose(bank[bk][:, j * P:(j + 1) * P], src[:, (c - 1) % 2, j * P:(j + 1) * P], ident)
                            last.then_inc(sem(f"ff_{name}T_ps"), 1)

                def score(c, ks):
                    first = WINDOW if c == 0 else 0
                    for k in ks:
                        for i in range(2):
                            bk, slot = 2 * (k // 2) + i, k % 2
                            if c and slot == 0:
                                pe.wait_ge(sem("at_s"), L * 4 * TILES + 4 * (c - 1) + bk + 1)
                            r = slice(64 * i, 64 * i + 64)
                            last = T.matmul(bank[bk][:, KEYS * slot + first:KEYS * (slot + 1)], qhT[r, k, c * P:(c + 1) * P],
                                            khT[r, k, c * P - WINDOW + first:(c + 1) * P], start=True, stop=True)
                            if slot == 1:
                                last.then_inc(sem("at_s_ps"), 1)

                def output():
                    for j in range(4):
                        last = T.matmul(bank[5][:, :], wo_sb[:, j, :], oT[:, j, :], start=(j == 0), stop=(j == 3))
                    last.then_inc(sem("at_wo_ps"), 1)

                def turn_probs(c, bk, pieces):
                    for j, piece in enumerate(pieces):
                        last = T.transpose(bank[bk][:, j * P:(j + 1) * P], piece, ident)
                    last.then_inc(sem("at_PT_ps"), 1)

                pe.wait_ge(sem("ff_qT"), L * TILES + TILES)
                pe.wait_ge(sem("ff_kT"), L * TILES + TILES)
                pe.wait_ge(sem("ff_w_in"), L * 64 + 64)
                score(0, range(4))
                score(1, range(4))
                for c in range(TILES):
                    at = HEADS * (c % 2)
                    own = [probs_own[:, at + h, :] for h in range(HEADS)]
                    before = [probs_before[:, (at + 2 * m) * WINDOW:(at + 2 * m + 2) * WINDOW] for m in range(HEADS // 2)]
                    if c + 2 < TILES:
                        score(c + 2, (0, 1))
                    pe.wait_ge(sem("at_P"), L * TILES + c + 1)
                    turn_probs(c, 4, own[0:4])
                    if c % 4 == 1 and c > 1:
                        pe.wait_ge(sem("at_h"), L * BLOCKS + c // 4)
                    turn_probs(c, 5, before)
                    if c + 2 < TILES:
                        score(c + 2, (2, 3))
                    pe.wait_ge(sem("at_PT_dve"), L * 2 * TILES + 2 * c + 1)
                    turn_probs(c, 4, own[4:8])
                    pe.wait_ge(sem("at_PT_dve"), L * 2 * TILES + 2 * c + 2)
                    if c:
                        pe.wait_ge(sem("at_o_even"), L * TILES + c)
                        pe.wait_ge(sem("at_o_odd"), L * TILES + c)
                    if c % 4 == 0 and c:
                        output()
                    for m in range(HEADS // 2):
                        if m == 2:
                            pe.wait_ge(sem("at_PT_act"), L * TILES + c + 1)
                        cols_ = slice(m * P, (m + 1) * P)
                        even, odd = bank[6][0:HEAD_DIM, cols_], bank[7][HEAD_DIM:P, cols_]
                        T.matmul(even, v_tok[:, c, P * m:P * m + HEAD_DIM], probsT[:, 2 * m, :], start=True, stop=(c == 0))
                        last = T.matmul(odd, v_tok[:, c, P * m + HEAD_DIM:P * (m + 1)], probsT[:, 2 * m + 1, :], start=True, stop=(c == 0))
                        if c:
                            T.matmul(even, v_low[:, c - 1, HEAD_DIM * m:HEAD_DIM * (m + 1)], probsT[0:WINDOW, 8 + m, :], start=False, stop=True)
                            last = T.matmul(odd, v_tok[HEAD_DIM:P, c - 1, P * m + HEAD_DIM:P * (m + 1)], probsT[WINDOW:P, 8 + m, :], start=False, stop=True)
                    last.then_inc(sem("at_o_ps"), 1)
                pe.wait_ge(sem("at_o_even"), L * TILES + TILES)
                pe.wait_ge(sem("at_o_odd"), L * TILES + TILES)
                output()
                pe.wait_ge(sem("ff_s2"), L + 1)
                ln_pe_tokens(pe, sT)
                ln_pe_back(pe, LN_FF + L, ff_norm)
                n = len(FF_CHUNKS)

                def feed(b):
                    pe.wait_ge(sem("ff_act"), L * n * BLOCKS + n * (b + 1))
                    if b >= 2:
                        pe.wait_ge(sem("ff_x"), L * BLOCKS + b - 1)
                    for i, (at, size) in enumerate(FF_CHUNKS):
                        last = T.matmul(bank[4 + b % 2][:, :], wf2_sb[0:size, i, :], ff_h[0:size, n * (b % 2) + i, :],
                                        start=(i == 0), stop=(i == n - 1))
                    last.then_inc(sem("ff_y_ps"), 1)

                for b in range(BLOCKS):
                    ln_out(pe, LN_FF + L, (b,))
                    rhs = nT[:, 512 * b:512 * b + 512]
                    for i, (at, size) in enumerate(FF_CHUNKS):
                        a_bank, g_bank = FF_BANKS[i]
                        if b:
                            pe.wait_ge(sem("ff_act"), L * n * BLOCKS + n * (b - 1) + i + 1)
                        elif i == 2:
                            ln_out(pe, LN_FF + L, (2, 3))
                        T.matmul(bank[g_bank][0:size, :], wf1_sb[:, FF + at:FF + at + size], rhs, start=True, stop=True)
                        T.matmul(bank[a_bank][0:size, :], wf1_sb[:, at:at + size], rhs,
                                 start=True, stop=True).then_inc(sem("ff_ag_ps"), 1)
                        if b and i == 1:
                            feed(b - 1)
                feed(BLOCKS - 1)
                pe.wait_ge(sem("ff_x"), L * BLOCKS + BLOCKS)

        @block.sync
        def _(sp):
            sp.dma_start(prm, dram["prm"][0]).then_inc(sem("s4_prm_in"), 16)
            sp.dma_start(expo, dram["expo"].to_broadcast([P, N_EXP])).then_inc(sem("expo_in"), 16)
            sp.dma_start(ident, dram["ident"]).then_inc(sem("consts_in"), 16)
            sp.dma_start(cond, dram["cond"]).then_inc(sem("consts_in"), 16)
            sp.dma_start(wmod_sb, dram["wmod"]).then_inc(sem("consts_in"), 16)
            sp.dma_start(sel, dram["sel"]).then_inc(sem("consts_in"), 16)
            sp.dma_start(xT, dram["xT"]).then_inc(sem("x_in"), 16)
            sp.wait_ge(sem("zero_set"), 1)
            sp.dma_start(k_pad[:, CHUNK:2 * CHUNK], k_im[:, 0, :]).then_inc(sem("s4_zero_out"), 16)
            s4_sp_layer(sp, 0, first=True, more=True)
            with sp.Fori(1, S4_LAYERS - 1) as L:
                s4_sp_layer(sp, L, first=False, more=True)
            s4_sp_layer(sp, S4_LAYERS - 1, first=False, more=False)
            sp.wait_ge(sem("x_s4"), BLOCKS)
            for dst, name in ((pw_sb, "pw"), (u_sb, "u"), (b2_sb, "b2")):
                sp.dma_start(dst, dram[name]).then_inc(sem("moe_consts_in"), 16)
            sp.dma_start(w1_low, dram["w1"]).then_inc(sem("moe_w1_in"), 16)
            sp.dma_start(w2_low, dram["w2"]).then_inc(sem("moe_w2_in"), 16)
            sp.wait_ge(sem("moe_wT"), BLOCKS)
            sp.dma_start(share_d, weightT).then_inc(sem("moe_wT_out"), 16)
            sp.wait_ge(sem("moe_wT_out"), 16)
            with sp.Fori(0, BLOCKS) as b:
                free = sp.snap(b + 1)
                for r, (dst, name) in enumerate(((share1, "1"), (share2, "2"))):
                    sp.wait_ge(sem("moe_share_free" + name), free)
                    sp.sem_inc(sem("turn"), 1)
                    rows = share_d[(r + 1) * EXPERTS:(r + 2) * EXPERTS, bass.ts(b, 512)]
                    if r == 0:
                        sp.dma_start(dst[:, 0:AHEAD], rows[0:AHEAD].partition_broadcast(P)).then_inc(sem("moe_share_in0"), 16)
                        sp.dma_start(dst[:, AHEAD:], rows[AHEAD:].partition_broadcast(P)).then_inc(sem("moe_share_in1"), 16)
                    else:
                        sp.dma_start(dst, rows.partition_broadcast(P)).then_inc(sem("moe_share_in2"), 16)
            sp.wait_ge(sem("moe_x"), BLOCKS + 1)
            for dst, name in ((wqf_sb, "wqf"), (wi_sb, "wi"), (wo8_sb, "wo8")):
                sp.dma_start(dst, dram[name]).then_inc(sem("gla_w_in"), 16)
            sp.dma_start(mask_sb, dram["mask"]).then_inc(sem("ff_consts_in"), 16)
            with sp.Fori(0, DEPTH) as L:
                one = sp.snap(L + 1)
                sp.wait_ge(sem("ff_wqkv_free"), one)
                sp.sem_inc(sem("turn"), 1)
                sp.dma_start(wqkv_sb, dram["wqkv"][L]).then_inc(sem("ff_wqkv_in"), 16)
                sp.dma_start(qk_rows, dram["qk_rows"][L]).then_inc(sem("ff_wqkv_in"), 16)
                sp.wait_ge(sem("ff_tables_free"), one)
                sp.sem_inc(sem("turn"), 1)
                sp.dma_start(scaled, dram["tables"]).then_inc(sem("ff_wqkv_in"), 16)
                sp.wait_ge(sem("ff_w_free"), one)
                sp.sem_inc(sem("turn"), 1)
                for dst, name in ((wo_sb, "wo"), (wf1_sb, "wf1"), (wf2_sb, "wf2"), (cols, "cols")):
                    sp.dma_start(dst, dram[name][L]).then_inc(sem("ff_w_in"), 16)
            sp.wait_ge(sem("result"), BLOCKS)
            sp.dma_start(out.rearrange("o (c i) d -> i (o c) d", i=P), ff_norm).then_inc(sem("stored"), 16)
            sp.wait_ge(sem("stored"), 16)

        @block.gpsimd
        def _(pool):
            nc.gpsimd.memset(eps_col, EPS_LN)
            nc.gpsimd.memset(neg_one, -1.0)
            nc.gpsimd.memset(ones, 1.0)
            nc.gpsimd.memset(neg_half, -0.5).then_inc(sem("p_set"), 1)
            pool.wait_ge(sem("p_set"), 1)
            chain = Chain(pool, sem("p_chain"))
            pool.wait_ge(sem("expo_in"), 16)
            s4_pool_angles(pool, chain, 0)
            ln_pool(pool, LN_A, shared=True)
            s4_pool_powers(pool, chain, 0)
            with pool.Fori(0, S4_LAYERS - 1) as L:
                chain.body(L, 4)
                ln_pool(pool, LN_S4 + L, shared=False)
                s4_pool_angles(pool, chain, L + 1)
                pool.wait_ge(sem("s4_pow_moved"), L * 128 + 128)
                pool.wait_ge(sem("s4_u"), L + 1)
                s4_pool_powers(pool, chain, L + 1)
            chain.leave(S4_LAYERS - 1)
            ln_pool(pool, LN_S4 + S4_LAYERS - 1, shared=False)
            ln_pool(pool, LN_B, shared=True)
            for w_high_s, w_low, w_low_s, n in ((w1_high_s, w1_low, w1_low_s, "1"), (w2_high_s, w2_low, w2_low_s, "2")):
                for e in range(EXPERTS):
                    pool.wait_ge(sem(f"moe_w{n}_high"), e + 1)
                    nc.gpsimd.tensor_tensor(w_low_s[:, e], w_low[:, e], w_high_s[:, e], ALU.subtract).then_inc(sem(f"moe_w{n}_low"), 1)
            ln_pool(pool, LN_C, shared=True)
            ff_pool_tables(pool, 0)
            for v in range(LIN_DIM):
                i = v % 2
                pool.wait_ge(sem("gla_state"), v + 1)
                if v >= 2:
                    pool.wait_ge(sem("gla_read_used"), v - 1)
                nc.gpsimd.tensor_tensor(read[i], state[i], qT, ALU.mult).then_inc(sem("gla_read"), 1)
            ln_pool(pool, LN_D, shared=True)
            with pool.Fori(0, DEPTH - 1) as L:
                chain.body(L, TILES)
                ff_pool_layer(pool, chain, L)
                ff_pool_tables(pool, L + 1)
            chain.leave(DEPTH - 1)
            ff_pool_layer(pool, chain, DEPTH - 1)

        @block.scalar
        def _(act):
            s4_act_magnitudes(act, 0)
            s4_act_decay(act, 0)
            act.wait_ge(sem("consts_in"), 64)
            nc.scalar.activation(cond_sig, cond, ACT.Sigmoid).then_inc(sem("cond_sig"), 1)
            act.wait_ge(sem("mod_ready"), 1)
            ln_act(act, LN_A, z_tok, hT, one_plus[:, 1:2], mod[:, 0:1])
            s4_act_sines(act, 0, CLOSE, "s4_sin")
            s4_act_sines(act, 0, FAR, "s4_sin_far")
            with act.Fori(0, S4_LAYERS - 1) as L:
                s4_act_layer(act, L, more=True)
            s4_act_layer(act, S4_LAYERS - 1, more=False)
            moe_act(act)
            gla_act(act)
            ff_act(act)
            for b in range(BLOCKS):
                act.wait_ge(sem("result_ps"), b + 1)
                nc.scalar.activation(ff_norm[:, 4 * b:4 * b + 4, :], bank[b][:, :].rearrange("p (a b) -> p a b", a=4), ACT.Copy).then_inc(sem("result"), 1)

        @block.vector
        def _(dve):
            chain = Chain(dve, sem("v_chain"))
            link = chain.link
            V = nc.vector
            V.memset(k_im[:, 0, :], 0.0).then_inc(sem("zero_set"), 1)
            V.memset(decay, 0.0)
            dve.wait_ge(sem("expo_in"), 16)
            s4_dve_angles(dve, 0)
            dve.wait_ge(sem("cond_sig"), 1)
            V.tensor_tensor(cond_silu, cond, cond_sig, ALU.mult).then_inc(sem("cond_silu"), 1)
            dve.wait_ge(sem("mod_ps"), 1)
            link(V.tensor_copy(mod, bank[7][:, 0:12]))
            V.tensor_scalar(mod_sign, mod, 0.0, 2.0, ALU.is_ge, ALU.mult)
            V.tensor_scalar(one_plus, mod, 1.0, None, ALU.add)
            link(V.scalar_tensor_tensor(mod_abs, mod, -1.0, mod, ALU.mult, ALU.max))
            link(V.tensor_scalar(mod_abs, mod_abs, 0.25, None, ALU.max))
            V.scalar_tensor_tensor(gate, mod_sign, -1.0, mod_abs, ALU.add, ALU.mult).then_inc(sem("mod_ready"), 1)
            dve.wait_ge(sem("mod_ready"), 1)
            ln_dve(dve, LN_A, z_tok, hT, one_plus[:, 1:2], mod[:, 0:1])
            s4_dve_reduce(dve, chain, 0)
            dve.wait_ge(sem("s4_zero_out"), 16)
            s4_dve_powers(dve, chain, 0)
            with dve.Fori(0, S4_LAYERS - 1) as L:
                chain.body(L, S4_DVE_LINKS)
                s4_dve_layer(dve, chain, L, more=True)
            chain.leave(S4_LAYERS - 1)
            s4_dve_layer(dve, chain, S4_LAYERS - 1, more=False)
            dve.wait_ge(sem("s4_h"), S4_LAYERS * BLOCKS)
            for b in range(BLOCKS):
                sl = slice(512 * b, 512 * b + 512)
                V.scalar_tensor_tensor(xT[:, sl], hT[:, sl], gate[:, 2:3], xT[:, sl], ALU.mult, ALU.add).then_inc(sem("x_s4"), 1)
            moe_dve(dve, link)
            moe_dve_blocks(dve, chain)
            gla_dve(dve, link)
            ff_dve(dve, chain)

        @block.tensor
        def _(pe):
            T = nc.tensor
            pe.wait_ge(sem("cond_silu"), 1)
            for i in range(12):
                last = T.matmul(bank[7][:, i:i + 1], wmod_sb[:, i // 6, (i % 6) * P:(i % 6 + 1) * P],
                                cond_silu[:, i // 6:i // 6 + 1], start=True, stop=True)
            last.then_inc(sem("mod_ps"), 1)
            pe.wait_ge(sem("mod_ps"), 1)
            pe.sem_inc(sem("s4_tp_free"), 1)
            pe.wait_ge(sem("x_in"), 16)
            ln_pe_tokens(pe, xT)
            pe.wait_ge(sem("mod_ready"), 1)
            ln_pe_back(pe, LN_A, z_tok)
            pe.wait_ge(sem("consts_in"), 64)
            s4_pe_layer(pe, 0, first=True)
            with pe.Fori(1, S4_LAYERS) as L:
                s4_pe_layer(pe, L, first=False)
            moe_pe(pe)
            gla_pe(pe)
            ff_pe(pe)
            for b in range(BLOCKS):
                pe.wait_ge(sem("x_ff"), b + 1)
                for t in range(4):
                    last = T.transpose(bank[b][:, t * P:(t + 1) * P], xT[:, (4 * b + t) * P:(4 * b + t + 1) * P], ident)
                last.then_inc(sem("result_ps"), 1)


S4_DVE_LINKS = 27
FF_DVE_LINKS = 32


def kernel(**inputs):
    import concourse.bacc as bacc
    from concourse.bass_utils import run_bass_kernel_spmd

    def arr(name):
        return np.ascontiguousarray(inputs[name])

    def modes(a):
        return a.reshape(S4_LAYERS, GROUPS, HG, MODES).transpose(0, 1, 3, 2).reshape(S4_LAYERS, P, HG)

    log_dt = np.repeat(arr("L0_attn_log_dt").reshape(S4_LAYERS, GROUPS, 1, HG), MODES, axis=2)
    prm = np.stack([log_dt.reshape(S4_LAYERS, P, HG)] + [modes(arr("L0_attn_" + n)) for n in ("A_re_log", "A_im", "C_re", "C_im")], axis=2)
    ln_wb = np.stack([arr("L0_attn_ln_w"), arr("L0_attn_ln_b")], axis=1)
    laid = {
        "ident": np.eye(P, dtype=np.float32),
        "cond": np.stack([arr("L0_c").reshape(P), arr("L1_c").reshape(P)], axis=1),
        "wmod": np.stack([arr("L0_wmod"), arr("L1_wmod")], axis=1),
        "xT": arr("L0_attn_x").reshape(N_TOK, P).T,
        "sel": np.stack([np.repeat(s * np.eye(GROUPS, dtype=np.float32), MODES, axis=0) for s in (1, -1)], axis=1),
        "expo": exponents().reshape(1, N_EXP),
        "prm": prm,
        "skip": arr("L0_attn_D_skip").reshape(S4_LAYERS, GROUPS, HG),
        "ln_wb": np.repeat(ln_wb.reshape(S4_LAYERS, 1, 2, P), P, axis=1),
        "w_out": arr("L0_attn_W_out").transpose(0, 2, 1),
        "b_out": arr("L0_attn_b_out").reshape(S4_LAYERS, 2, P).transpose(0, 2, 1),
    }
    order = [2, 0, 1]
    u = np.stack([arr("L0_ffn_U1"), arr("L0_ffn_U2"), arr("L0_ffn_U3")])[order]
    qs, ks = arr("L1_ffn_q_scale"), arr("L1_ffn_k_scale")
    swap = lambda a: np.concatenate([a[:, HEAD_DIM // 2:], a[:, :HEAD_DIM // 2]], axis=1)
    qk_rows = np.stack([qs, swap(qs), ks, swap(ks)], axis=1)
    b1 = arr("L1_ffn_b1")
    cols = np.zeros((DEPTH, P, 9), np.float32)
    for i, (at, size) in enumerate(FF_CHUNKS):
        cols[:, :size, i] = b1[:, at:at + size]
        cols[:, :size, 3 + i] = b1[:, FF + at:FF + at + size]
    cols[:, :, 6], cols[:, :, 7], cols[:, :, 8] = arr("L1_ffn_b2"), arr("L1_ffn_ln_g"), arr("L1_ffn_ln_b")
    wf2 = np.zeros((DEPTH, P, 3, P), np.float32)
    for i, (at, size) in enumerate(FF_CHUNKS):
        wf2[:, :size, i] = arr("L1_ffn_w2")[:, at:at + size]
    wi = arr("L1_attn_Wi").reshape(P, LIN_HEADS, 1, LIN_DIM)
    wo8 = arr("L1_attn_Wo").reshape(LIN_HEADS, LIN_DIM, 1, P)
    laid.update({
        "pw": arr("L0_ffn_P_w").T,
        "u": u.reshape(ROUTERS * EXPERTS, ADDR).T,
        "b2": arr("L0_ffn_b2"),
        "w1": arr("L0_ffn_W1").transpose(2, 0, 1),
        "w2": arr("L0_ffn_W2").reshape(EXPERTS, P, HID_CHUNKS, P).transpose(3, 0, 2, 1),
        "wqf": np.concatenate([arr("L1_attn_Wq"), arr("L1_attn_Wf")], axis=1),
        "wi": np.repeat(wi, LIN_DIM, axis=2).transpose(0, 3, 1, 2).reshape(P, LIN_DIM, P),
        "wo8": np.repeat(wo8, LIN_DIM, axis=2).transpose(0, 2, 1, 3).reshape(P, LIN_DIM, P),
        "mask": window_mask(),
        "tables": rotary_tables().reshape(4, TILES, P, HEAD_DIM).transpose(2, 0, 1, 3),
        "wqkv": arr("L1_ffn_wqkv"),
        "qk_rows": np.repeat(qk_rows.reshape(DEPTH, 1, 4, HEAD_DIM), P, axis=1),
        "wo": arr("L1_ffn_wo").reshape(DEPTH, 4, P, P).transpose(0, 2, 1, 3),
        "wf1": arr("L1_ffn_w1"),
        "wf2": wf2,
        "cols": cols,
    })
    nc = bacc.Bacc("TRN2", target_bir_lowering=False, num_devices=1)
    arrays, dram = {}, {}
    for name, a in laid.items():
        a = np.ascontiguousarray(a)
        arrays[name + "_dram"] = a
        dram[name] = nc.dram_tensor(name + "_dram", a.shape, F32, kind="ExternalInput").ap()
    out = nc.dram_tensor("out_0_dram", (1, N_TOK, P), F32, kind="ExternalOutput").ap()
    program(nc, dram, out)
    r = run_bass_kernel_spmd(nc, [arrays], core_ids=[0])
    return r.results[0]["out_0_dram"]
```
